# Optimizing a Trainium2 kernel written in Bass

```python
import numpy as np
import jax
import jax.numpy as jnp

def _softmax(x, axis=-1):
    return jax.nn.softmax(x, axis=axis)

def _gelu(x):
    return jax.nn.gelu(x, approximate=True)

def _silu(x):
    return jax.nn.silu(x)

def _sigmoid(x):
    return jax.nn.sigmoid(x)

def _layernorm(x, axis=-1, eps=1e-05):
    m = jnp.mean(x, axis=axis, keepdims=True)
    v = jnp.var(x, axis=axis, keepdims=True)
    return (x - m) / jnp.sqrt(v + eps)

def _scatter_add(tgt, idx, src, axis=0):
    return tgt.at[idx].add(src)

def _segment_sum(src, seg, n):
    return jax.ops.segment_sum(src, seg, n)
kernel_name = 'mk_gnn_resnorm_d2_gnn_r8_fc3208'

def setup_inputs(seed: int=0):
    np.random.seed(seed)
    _w = jnp.asarray

    def _rec_inputs():
        import jax
        import jax.numpy as jnp
        _gk = jax.random.key(seed)
        x = -0.000202 + 1 * jax.random.normal(jax.random.fold_in(_gk, 1), (12500, 64), jnp.float32)
        src = jax.random.randint(jax.random.fold_in(_gk, 2), (400000,), 0, 12500, jnp.int32)
        dst = jnp.minimum((12500 * jax.random.uniform(jax.random.fold_in(_gk, 3), (400000,)) ** 2.0).astype(jnp.int32), 99999)
        _o = jnp.argsort(dst, stable=True)
        src = src[_o]
        dst = dst[_o]
        edge_weight = jax.random.uniform(jax.random.fold_in(_gk, 12), (400000,), jnp.float32, 0.0, 0.999999)
        edge_weight1 = 0.000452788 + 0.999756 * jax.random.normal(jax.random.fold_in(_gk, 13), (400000, 1), jnp.float32)
        return (x, src, dst, edge_weight, edge_weight1)
    x, src, dst, edge_weight, edge_weight1 = _rec_inputs()

    def _L0_gnn_setup():
        import jax, jax.numpy as jnp
        import numpy as np
        N_NODES = 12500
        N_EDGES = 200000
        D_IN = 64
        D_OUT = 64
        key = jax.random.key(seed)
        k1, k2, k3, k4 = jax.random.split(key, 4)
        x = jax.random.normal(k1, (N_NODES, D_IN), dtype=jnp.float32)
        edge_index = jax.random.randint(k2, (2, N_EDGES), 0, N_NODES, dtype=jnp.int64)
        edge_weight = jax.random.uniform(k3, (N_EDGES,), dtype=jnp.float32)
        W = jax.random.normal(k4, (D_OUT, D_IN), dtype=jnp.float32) * (1.0 / np.sqrt(D_IN))
        b = jnp.zeros((D_OUT,), dtype=jnp.float32)
        return {'x': x, 'edge_index': edge_index, 'edge_weight': edge_weight, 'W': W, 'b': b}
    _L0_gnn_all = _L0_gnn_setup()
    _L0_gnn_in = {k: v for k, v in _L0_gnn_all.items() if k in ('W', 'b')}
    del _L0_gnn_all

    def _L1_gnn_setup():
        import jax, jax.numpy as jnp
        import numpy as np
        N = 12500
        E = 200000
        ND = 64
        ED = 1
        HD = 128
        key = jax.random.key(seed)
        ks = jax.random.split(key, 12)
        x = jax.random.normal(ks[0], (N, ND), dtype=jnp.float32)
        edge_index = jax.random.randint(ks[1], (2, E), 0, N, dtype=jnp.int32)
        edge_attr = jax.random.normal(ks[2], (E, ED), dtype=jnp.float32)
        s1 = 1.0 / np.sqrt(2 * ND + ED)
        W1 = jax.random.uniform(ks[3], (HD, 2 * ND + ED), minval=-s1, maxval=s1, dtype=jnp.float32)
        b1 = jax.random.uniform(ks[4], (HD,), minval=-s1, maxval=s1, dtype=jnp.float32)
        s2 = 1.0 / np.sqrt(HD)
        W2 = jax.random.uniform(ks[5], (ND, HD), minval=-s2, maxval=s2, dtype=jnp.float32)
        b2 = jax.random.uniform(ks[6], (ND,), minval=-s2, maxval=s2, dtype=jnp.float32)
        sg = 1.0 / np.sqrt(ND)
        W_ih = jax.random.uniform(ks[7], (3 * ND, ND), minval=-sg, maxval=sg, dtype=jnp.float32)
        b_ih = jax.random.uniform(ks[8], (3 * ND,), minval=-sg, maxval=sg, dtype=jnp.float32)
        W_hh = jax.random.uniform(ks[9], (3 * ND, ND), minval=-sg, maxval=sg, dtype=jnp.float32)
        b_hh = jax.random.uniform(ks[10], (3 * ND,), minval=-sg, maxval=sg, dtype=jnp.float32)
        return {'x': x, 'edge_index': edge_index, 'edge_attr': edge_attr, 'W1': W1, 'b1': b1, 'W2': W2, 'b2': b2, 'W_ih': W_ih, 'b_ih': b_ih, 'W_hh': W_hh, 'b_hh': b_hh}
    _L1_gnn_all = _L1_gnn_setup()
    _L1_gnn_in = {k: v for k, v in _L1_gnn_all.items() if k in ('W1', 'b1', 'W2', 'b2', 'W_ih', 'b_ih', 'W_hh', 'b_hh')}
    del _L1_gnn_all
    return {'x': x, 'src': src, 'dst': dst, 'edge_weight': edge_weight, 'edge_weight1': edge_weight1, 'L0_gnn_W': _L0_gnn_in['W'], 'L0_gnn_b': _L0_gnn_in['b'], 'L1_gnn_W1': _L1_gnn_in['W1'], 'L1_gnn_b1': _L1_gnn_in['b1'], 'L1_gnn_W2': _L1_gnn_in['W2'], 'L1_gnn_b2': _L1_gnn_in['b2'], 'L1_gnn_W_ih': _L1_gnn_in['W_ih'], 'L1_gnn_b_ih': _L1_gnn_in['b_ih'], 'L1_gnn_W_hh': _L1_gnn_in['W_hh'], 'L1_gnn_b_hh': _L1_gnn_in['b_hh']}

def reference(x, src, dst, edge_weight, edge_weight1, L0_gnn_W, L0_gnn_b, L1_gnn_W1, L1_gnn_b1, L1_gnn_W2, L1_gnn_b2, L1_gnn_W_ih, L1_gnn_b_ih, L1_gnn_W_hh, L1_gnn_b_hh):
    import jax
    import jax.numpy as jnp

    def _L0_gnn_ref(x, edge_index, edge_weight, W, b):
        import jax, jax.numpy as jnp
        import numpy as np
        N_NODES = 12500
        N_EDGES = 200000
        D_IN = 64
        D_OUT = 64
        N = x.shape[0]
        loop = jnp.arange(N, dtype=edge_index.dtype)
        row = jnp.concatenate([edge_index[0], loop])
        col = jnp.concatenate([edge_index[1], loop])
        w = jnp.concatenate([edge_weight, jnp.ones((N,), dtype=x.dtype)])
        deg = jax.ops.segment_sum(w, row, num_segments=N)
        safe = jnp.where(deg > 0, deg, 1.0)
        dinv = jnp.where(deg > 0, safe ** (-0.5), 0.0)
        norm_w = dinv[row] * w * dinv[col]
        agg = jax.ops.segment_sum(norm_w[:, None] * x[col], row, num_segments=N)
        return agg @ W.T + b

    def _L1_gnn_ref(x, edge_index, edge_attr, W1, b1, W2, b2, W_ih, b_ih, W_hh, b_hh):
        import jax, jax.numpy as jnp
        import numpy as np
        N = 12500
        E = 200000
        ND = 64
        ED = 1
        HD = 128
        src, dst = (edge_index[0], edge_index[1])
        m = jnp.concatenate([x[src], x[dst], edge_attr], axis=-1)
        m = jax.nn.relu(m @ W1.T + b1) @ W2.T + b2
        aggr = jnp.zeros_like(x).at[dst].add(m)
        gi = aggr @ W_ih.T + b_ih
        gh = x @ W_hh.T + b_hh
        i_r, i_z, i_n = jnp.split(gi, 3, axis=-1)
        h_r, h_z, h_n = jnp.split(gh, 3, axis=-1)
        r = jax.nn.sigmoid(i_r + h_r)
        z = jax.nn.sigmoid(i_z + h_z)
        n = jnp.tanh(i_n + r * h_n)
        return (1.0 - z) * n + z * x
    edge_index = jnp.stack([src, dst])
    x = _layernorm(x + _L0_gnn_ref(x, edge_index, edge_weight, L0_gnn_W, L0_gnn_b), axis=-1)
    x = _layernorm(x + _L1_gnn_ref(x, edge_index, edge_weight1, L1_gnn_W1, L1_gnn_b1, L1_gnn_W2, L1_gnn_b2, L1_gnn_W_ih, L1_gnn_b_ih, L1_gnn_W_hh, L1_gnn_b_hh), axis=-1)
    return x

_drawn_inputs = setup_inputs


def setup_inputs(seed=0):
    import zlib

    import numpy as np

    out = dict(_drawn_inputs(seed))
    spreads = {'L0_gnn_b': (0.0, 0.1)}
    factors = {'edge_weight1': 4.724, 'L1_gnn_b_ih': 3.505, 'L1_gnn_b_hh': 4.923}
    for name, (base, spread) in spreads.items():
        noise = np.random.default_rng([zlib.crc32(name.encode()), seed]).standard_normal(out[name].shape)
        drawn = base * np.exp(spread * noise) if base else spread * noise
        out[name] = jnp.asarray(drawn.astype(out[name].dtype))
    for name, factor in factors.items():
        out[name] = (out[name] * factor).astype(out[name].dtype)
    return out
```

```python
from contextlib import ExitStack

import concourse.bass as bass
from concourse import mybir

F32, BF16, I32 = mybir.dt.float32, mybir.dt.bfloat16, mybir.dt.int32
ALU, ACT = mybir.AluOpType, mybir.ActivationFunctionType
AX_X = mybir.AxisListType.X

P = 128
N, E, D, HD = 12500, 400000, 64, 128
NW = (N + P - 1) // P
LAST = N - (NW - 1) * P
TILES = E // P
G = 5
GE = G * P
NG = TILES // G
NB = 25
BT = TILES // NB
ROW = D + 1
NQ = (E + NW * (GE - 1)) // GE + 1
NQ += NQ % 2
QP = 6
EPS = 1e-05
UB = 7
NU = NW // UB
MAXSTEP = NG * NW
NCOL = 4
assert TILES == NG * G == NB * BT and NG == 5 * (NB * BT // 25) and NW % UB == 0 and NQ <= P * QP


def wait(eng, sem, value):
    if not isinstance(value, int) or value > 0:
        eng.wait_ge(sem, value)


def wait_alone(eng, sem, value, passed):
    eng.wait_ge(sem, value)
    eng.sem_inc(passed, 1)


def over_pairs(eng, n, body, first=0):
    body(0, 0, 0)
    body(1, 1, 0)
    with eng.Fori(1, n // 2) as i:
        body(i * 2, 0, i)
        body(i * 2 + 1, 1, i)
    if n % 2:
        body(n - 1, 0, n // 2)


def cols(t, start, size):
    return t[:, bass.ds(start, size)]


def split3(ap, n):
    return ap.rearrange("p (a b) -> p a b", a=n)


def program(nc, x, src, dst, w, attr, W, b, W1, b1, W2, b2, W_ih, b_ih, W_hh, b_hh, out, places, table, moved, a_dram, x1_dram):
    with ExitStack() as ctx:
        def sb(name, shape, dt):
            return ctx.enter_context(nc.sbuf_tensor(name, shape, dt))

        lane_row = sb("lane_row", [P, P], BF16)
        node_id = sb("node_id", [P, NW], F32)
        window_base = sb("window_base", [P, NW], F32)
        ident = sb("ident", [P, P], F32)
        before = sb("before", [P, P], F32)
        before_bf = sb("before_bf", [P, P], BF16)
        upto_bf = sb("upto_bf", [P, P], BF16)
        ones_bf = sb("ones_bf", [P, P], BF16)
        ones = sb("ones", [P, P], F32)
        eps = sb("eps", [P, 1], F32)
        zero_bf = sb("zero_bf", [P, 512], BF16)
        src_cols = sb("src_cols", [P, 2, TILES], BF16)
        edge_cols = sb("edge_cols", [P, 2, TILES], F32)
        src_hi, src_lo = src_cols[:, 0, :], src_cols[:, 1, :]
        weight, dst_f = edge_cols[:, 0, :], edge_cols[:, 1, :]
        step_tab = sb("step_tab", [1, 3 * NG], I32)
        q_tab = sb("q_tab", [1, P * QP], I32)
        dinv = sb("dinv", [P, NW], F32)
        start_row = sb("start_row", [P, NW], F32)
        tables = sb("tables", [P, NW * 3 * HD], BF16)
        sums = sb("sums", [P, NW, HD + 1], F32)
        W_T = sb("W_T", [D, D], F32)
        W1_T = sb("W1_T", [D, 2 * HD], F32)
        c_row = sb("c_row", [1, HD], F32)
        W2_T = sb("W2_T", [HD, D], F32)
        Wih_T = sb("Wih_T", [D, 3 * D], F32)
        Whh_T = sb("Whh_T", [D, 3 * D], F32)
        b_b = sb("b_b", [P, D], F32)
        b1_b = sb("b1_b", [P, HD], F32)
        b2_b = sb("b2_b", [P, D], F32)
        bih_b = sb("bih_b", [P, 3 * D], F32)
        bhh_b = sb("bhh_b", [P, 3 * D], F32)

        flat = sums[:, :, :].rearrange("p a b -> p (a b)")
        acc = flat[:, 0:NW * D]
        xs = flat[:, NW * D:2 * NW * D].rearrange("p (a b) -> p a b", b=D)

        constants(nc, lane_row, node_id, window_base, ident, before, before_bf, upto_bf, ones_bf, ones, eps, zero_bf)
        weights(nc, ident, W, W1, W2, W_ih, W_hh, b, b1, b2, b_ih, b_hh, W_T, W1_T, c_row, W2_T, Wih_T, Whh_T,
                b_b, b1_b, b2_b, bih_b, bhh_b)
        edge_columns(nc, src, dst, w, ident, src_cols, edge_cols)
        steps_table(nc, dst, before, table, sums, step_tab)
        counts(nc, lane_row, ones, ones_bf, before, src_hi, src_lo, weight, moved, places, sums, dinv, start_row, q_tab)
        scaled_nodes(nc, x, xs, dinv, tables, acc)
        move_rows(nc, dst, lane_row, node_id, before_bf, upto_bf, ones_bf, ones, zero_bf, src_hi, src_lo, weight,
                  step_tab, start_row, tables, moved)
        sum_moved(nc, lane_row, q_tab, moved, acc)
        nodes(nc, ident, eps, xs, dinv, acc, W_T, b_b, W1_T, b1_b, tables, a_dram, x1_dram)
        messages(nc, dst, attr, lane_row, node_id, window_base, ones_bf, src_hi, src_lo, dst_f, c_row, step_tab, tables, sums, a_dram)
        update(nc, ident, eps, x1_dram, sums, W2_T, b2_b, Wih_T, bih_b, Whh_T, bhh_b, out)


def constants(nc, lane_row, node_id, window_base, ident, before, before_bf, upto_bf, ones_bf, ones, eps, zero_bf):
    with ExitStack() as ctx:
        row_i = ctx.enter_context(nc.sbuf_tensor("row_i", [P, P], I32))
        node_i = ctx.enter_context(nc.sbuf_tensor("node_i", [P, NW], I32))
        base_i = ctx.enter_context(nc.sbuf_tensor("base_i", [P, NW], I32))
        made = ctx.enter_context(nc.semaphore("iotas_made"))
        lanes = ctx.enter_context(nc.semaphore("lanes_made"))
        block = ctx.enter_context(nc.Block())

        @block.gpsimd
        def _(pool):
            pool.iota(row_i[:, :], [[1, P]], base=0, channel_multiplier=0)
            pool.iota(node_i[:, :], [[P, NW]], base=0, channel_multiplier=1)
            pool.iota(base_i[:, :], [[P, NW]], base=0, channel_multiplier=0).then_inc(made, 1)

        @block.vector
        def _(dve):
            dve.memset(ones[:, :], 1.0)
            dve.memset(ones_bf[:, :], 1.0)
            dve.memset(eps[:, :], EPS)
            dve.memset(zero_bf[:, :], 0.0)
            dve.wait_ge(made, 1)
            dve.tensor_copy(lane_row[:, :], row_i[:, :]).then_inc(lanes, 1)
            dve.tensor_copy(window_base[:, :], base_i[:, :]).then_inc(lanes, 1)
            dve.tensor_copy(node_id[:, :], node_i[:, :]).then_inc(lanes, 1)
            dve.wait_ge(lanes, 3)
            lane = node_id[:, 0:1]
            dve.tensor_scalar(ident[:, :], lane_row[:, :], lane, None, ALU.is_equal)
            dve.tensor_scalar(before[:, :], lane_row[:, :], lane, None, ALU.is_gt)
            dve.tensor_scalar(before_bf[:, :], lane_row[:, :], lane, None, ALU.is_gt)
            dve.tensor_scalar(upto_bf[:, :], lane_row[:, :], lane, None, ALU.is_le)


def weights(nc, ident, W, W1, W2, W_ih, W_hh, b, b1, b2, b_ih, b_hh, W_T, W1_T, c_row, W2_T, Wih_T, Whh_T,
            b_b, b1_b, b2_b, bih_b, bhh_b):
    with ExitStack() as ctx:
        def sb(name, shape):
            return ctx.enter_context(nc.sbuf_tensor(name, shape, F32))

        W_s, W1_s, W2_s = sb("W_s", [D, D]), sb("W1_s", [HD, 2 * D + 1]), sb("W2_s", [D, HD])
        ih_s, hh_s = sb("ih_s", [D, 3, D]), sb("hh_s", [D, 3, D])
        ps = ctx.enter_context(nc.psum_tensor("ps_weights", [P, 4, 512], F32))
        loaded = ctx.enter_context(nc.semaphore("weights_loaded"))
        turned = ctx.enter_context(nc.semaphore("weights_turned"))
        block = ctx.enter_context(nc.Block())
        loads = [(W_s[:, :], W), (W1_s[:, :], W1), (W2_s[:, :], W2),
                 (ih_s[:, :, :], W_ih.rearrange("(a r) c -> r a c", a=3)),
                 (hh_s[:, :, :], W_hh.rearrange("(a r) c -> r a c", a=3))]
        loads += [(t[:, :], v.unsqueeze(0).to_broadcast([P, v.shape[0]]))
                  for t, v in ((b_b, b), (b1_b, b1), (b2_b, b2), (bih_b, b_ih), (bhh_b, b_hh))]

        @block.sync
        def _(sp):
            for dest, source in loads:
                sp.dma_start(dest, source).then_inc(loaded, 16)
            sp.wait_ge(loaded, 16 * len(loads))

        @block.tensor
        def _(pe):
            pe.wait_ge(loaded, 16 * len(loads))
            pe.transpose(ps[0:D, 0, 0:D], W_s[:, :], ident[0:D, 0:D])
            pe.transpose(ps[0:D, 1, 0:HD], W1_s[:, 0:D], ident[:, :])
            pe.transpose(ps[0:D, 1, HD:2 * HD], W1_s[:, D:2 * D], ident[:, :])
            pe.transpose(ps[:, 0, 256:256 + D], W2_s[:, :], ident[0:D, 0:D])
            pe.matmul(ps[0:1, 0, 384:512], W1_s[:, 2 * D:2 * D + 1], ident[:, :], start=True, stop=True)
            for i in range(3):
                pe.transpose(ps[0:D, 2, i * D:(i + 1) * D], ih_s[:, i, :], ident[0:D, 0:D])
                last = pe.transpose(ps[0:D, 3, i * D:(i + 1) * D], hh_s[:, i, :], ident[0:D, 0:D])
            last.then_inc(turned, 1)

        @block.vector
        def _(dve):
            dve.wait_ge(turned, 1)
            dve.tensor_copy(W_T[:, :], ps[0:D, 0, 0:D])
            dve.tensor_copy(W1_T[:, :], ps[0:D, 1, 0:2 * HD])
            dve.tensor_copy(W2_T[:, :], ps[:, 0, 256:256 + D])
            dve.tensor_copy(c_row[:, :], ps[0:1, 0, 384:512])
            dve.tensor_copy(Wih_T[:, :], ps[0:D, 2, 0:3 * D])
            dve.tensor_copy(Whh_T[:, :], ps[0:D, 3, 0:3 * D])


def edge_columns(nc, src, dst, w, ident, src_cols, edge_cols):
    with ExitStack() as ctx:
        raw = ctx.enter_context(nc.sbuf_tensor("edge_raw", [BT, 2, 3, P], I32))
        part = ctx.enter_context(nc.sbuf_tensor("edge_part", [BT, 2, 2, P], I32))
        rows = ctx.enter_context(nc.sbuf_tensor("edge_rows", [BT, 2, NCOL, P], F32))
        ps = ctx.enter_context(nc.psum_tensor("ps_cols", [P, 2, 512], F32))
        raw_in = [ctx.enter_context(nc.semaphore(f"raw_in{s}")) for s in range(2)]
        parted = ctx.enter_context(nc.semaphore("parts_made"))
        rows_made = ctx.enter_context(nc.semaphore("rows_made"))
        turned = ctx.enter_context(nc.semaphore("cols_turned"))
        copied = ctx.enter_context(nc.semaphore("cols_copied"))
        block = ctx.enter_context(nc.Block())
        views = [v.rearrange("(t p) -> t p", p=P) for v in (src, dst, w)]

        @block.sync
        def _(sp):
            def load(i, s, use):
                wait(sp, rows_made, i - 1)
                for a, v in enumerate(views):
                    d = raw[:, s, a, :] if a < 2 else raw[:, s, a, :].bitcast(F32)
                    sp.dma_start(d, v[bass.ds(i * BT, BT), :]).then_inc(raw_in[s], 16)
            over_pairs(sp, NB, load)

        @block.vector
        def _(dve):
            def make(i, s, use):
                dve.wait_ge(raw_in[s], use * 48 + 48)
                wait(dve, turned, i - 1)
                dve.tensor_scalar(part[:, s, 0, :], raw[:, s, 0, :], 7, None, ALU.logical_shift_right).then_inc(parted, 1)
                dve.tensor_scalar(part[:, s, 1, :], raw[:, s, 0, :], P - 1, None, ALU.bitwise_and).then_inc(parted, 1)
                dve.tensor_copy(rows[:, s, 2, :], raw[:, s, 2, :].bitcast(F32))
                dve.tensor_copy(rows[:, s, 3, :], raw[:, s, 1, :])
                dve.wait_ge(parted, i * 2 + 2)
                dve.tensor_copy(rows[:, s, 0:2, :], part[:, s, :, :]).then_inc(rows_made, 1)
            over_pairs(dve, NB, make)

        @block.tensor
        def _(pe):
            def turn(i, s, use):
                pe.wait_ge(rows_made, i + 1)
                wait(pe, copied, i - 1)
                for a in range(NCOL):
                    last = pe.transpose(ps[:, s, a * BT:(a + 1) * BT], rows[:, s, a, :], ident[0:BT, 0:BT])
                last.then_inc(turned, 1)
            over_pairs(pe, NB, turn)

        @block.scalar
        def _(act):
            def copy(i, s, use):
                act.wait_ge(turned, i + 1)
                act.activation(src_cols[:, :, bass.ds(i * BT, BT)], split3(ps[:, s, 0:2 * BT], 2), ACT.Copy)
                act.activation(edge_cols[:, :, bass.ds(i * BT, BT)], split3(ps[:, s, 2 * BT:4 * BT], 2), ACT.Copy).then_inc(copied, 1)
            over_pairs(act, NB, copy)


def steps_table(nc, dst, before, table, sums, step_tab):
    R = NG // G
    with ExitStack() as ctx:
        def sb(name, shape, dt):
            return ctx.enter_context(nc.sbuf_tensor(name, shape, dt))

        ids = sums[:, :, :].rearrange("p a b -> p (a b)")[0:R, 0:G * GE].bitcast(I32)
        ends = sb("ends", [R, 2, G], I32)
        wins = sb("wins", [R, 2, G], I32)
        win_f = sb("win_f", [R, 2, G], F32)
        width = sb("width", [R, G + 1], F32)
        first = sb("first", [R, G + 1], F32)
        tab_f = sb("tab_f", [R, G, 3], F32)
        tab_i = sb("tab_i", [R, G, 3], I32)
        ps = ctx.enter_context(nc.psum_tensor("ps_steps", [P, 512], F32))
        ids_in = ctx.enter_context(nc.semaphore("ids_in"))
        chain = ctx.enter_context(nc.semaphore("steps_chain"))
        widths = ctx.enter_context(nc.semaphore("widths_made"))
        summed = ctx.enter_context(nc.semaphore("widths_summed"))
        made = ctx.enter_context(nc.semaphore("steps_made"))
        kept = ctx.enter_context(nc.semaphore("steps_kept"))
        back = ctx.enter_context(nc.semaphore("steps_back"))
        block = ctx.enter_context(nc.Block())

        @block.sync
        def _(sp):
            sp.dma_start(ids, dst.rearrange("(p e) -> p e", p=R)).then_inc(ids_in, 16)
            sp.wait_ge(made, 1)
            sp.dma_start(table.rearrange("(p e) -> p e", p=R), tab_i[:, :, :].rearrange("p a b -> p (a b)")).then_inc(kept, 16)
            sp.wait_ge(kept, 16)
            sp.dma_start(step_tab[:, :], table.unsqueeze(0)).then_inc(back, 16)
            sp.wait_ge(back, 16)

        @block.tensor
        def _(pe):
            pe.wait_ge(widths, 1)
            pe.matmul(ps[0:R, 0:1], before[0:R, 0:R], width[:, G:G + 1], start=True, stop=True).then_inc(summed, 1)

        @block.vector
        def _(dve):
            n = 0

            def then(instruction):
                nonlocal n
                n += 1
                instruction.then_inc(chain, 1)
                dve.wait_ge(chain, n)

            dve.wait_ge(ids_in, 16)
            dve.tensor_reduce(ends[:, 0, :], split3(ids, G), AX_X, ALU.min)
            then(dve.tensor_reduce(ends[:, 1, :], split3(ids, G), AX_X, ALU.max))
            then(dve.tensor_scalar(wins[:, :, :], ends[:, :, :], 7, None, ALU.logical_shift_right))
            then(dve.tensor_copy(win_f[:, :, :], wins[:, :, :]))
            then(dve.scalar_tensor_tensor(width[:, 0:G], win_f[:, 1, :], 1.0, win_f[:, 0, :], ALU.add, ALU.subtract))
            dve.tensor_reduce(width[:, G:G + 1], width[:, 0:G], AX_X, ALU.add).then_inc(widths, 1)
            dve.wait_ge(summed, 1)
            then(dve.tensor_copy(first[:, 0:1], ps[0:R, 0:1]))
            for j in range(G):
                then(dve.tensor_tensor(first[:, j + 1:j + 2], first[:, j:j + 1], width[:, j:j + 1], ALU.add))
            dve.tensor_copy(tab_f[:, :, 0], first[:, 0:G])
            dve.tensor_copy(tab_f[:, :, 1], first[:, 1:G + 1])
            then(dve.tensor_tensor(tab_f[:, :, 2], win_f[:, 0, :], first[:, 0:G], ALU.subtract))
            dve.tensor_copy(tab_i[:, :, :], tab_f[:, :, :]).then_inc(made, 1)


def counts(nc, lane_row, ones, ones_bf, before, src_hi, src_lo, weight, moved, places, sums, dinv, start_row, q_tab):
    ZG = 4
    with ExitStack() as ctx:
        def sb(name, shape, dt):
            return ctx.enter_context(nc.sbuf_tensor(name, shape, dt))

        def sem(name):
            return ctx.enter_context(nc.semaphore(name))

        lo_hot = sb("lo_hot", [P, 2, G, P], F32)
        hi_hot = sb("hi_hot", [P, 2, G, 2, NW], F32)
        ps = ctx.enter_context(nc.psum_tensor("ps_counts", [P, 2, NW], F32))
        ps_sum = ctx.enter_context(nc.psum_tensor("ps_sum", [P, 512], F32))
        zeros = sums[:, :, :].rearrange("p a b -> p (a b)")[:, 0:ZG * G * ROW]
        deg, live, safe, root = (sb(n, [P, NW], F32) for n in ("deg", "live", "safe", "root"))
        per_lane = sb("per_lane", [P, NW], F32)
        total = sb("total", [NW, 1], F32)
        groups = sb("groups", [NW, 1], F32)
        steps_i = sb("steps_i", [NW, NG + 1], I32)
        full = sb("full", [NW, NG + 1], F32)
        padded = sb("padded", [NW, 1], F32)
        padded_b = sb("padded_b", [NW, P], F32)
        q_i = sb("q_i", [P, QP], I32)
        q_f = sb("q_f", [P, QP], F32)
        q_le = sb("q_le", [P, QP, NW], F32)
        q_win = sb("q_win", [P, QP], F32)
        q_out = sb("q_out", [P, QP], I32)
        zeroed, zero_done = sem("zeros_made"), sem("zero_done")
        hot_made, weighted, used = sem("hot_made"), sem("hot_weighted"), sem("hot_used")
        chain, lane_counts, win_counts = sem("count_chain"), sem("lane_counts"), sem("window_counts")
        pads_made, starts_made = sem("pads_made"), sem("starts_made")
        guarded, rooted = sem("degree_guarded"), sem("degree_rooted")
        q_ready, q_made, q_kept, q_back = sem("q_ready"), sem("q_made"), sem("q_kept"), sem("q_back")
        block = ctx.enter_context(nc.Block())

        @block.sync
        def _(sp):
            sp.wait_ge(zeroed, 1)
            with sp.Fori(0, NQ // ZG) as i:
                sp.dma_start(moved[bass.ds(i * (ZG * GE), ZG * GE), :].rearrange("(p r) c -> p (r c)", p=P),
                             zeros).then_inc(zero_done, 16)
            for i in range(NQ // ZG * ZG, NQ):
                sp.dma_start(moved[i * GE:(i + 1) * GE, :].rearrange("(p r) c -> p (r c)", p=P),
                             zeros[:, 0:G * ROW]).then_inc(zero_done, 16)
            sp.wait_ge(q_made, 1)
            sp.dma_start(places.rearrange("(p e) -> p e", p=P), q_out[:, :]).then_inc(q_kept, 16)
            sp.wait_ge(q_kept, 16)
            sp.dma_start(q_tab[:, :], places.unsqueeze(0)).then_inc(q_back, 16)
            sp.wait_ge(q_back, 16)
            sp.wait_ge(zero_done, 16 * (NQ // ZG + NQ % ZG))

        @block.gpsimd
        def _(pool):
            pool.memset(zeros, 0.0).then_inc(zeroed, 1)
            pool.iota(q_i[:, :], [[GE, QP]], base=0, channel_multiplier=GE * QP).then_inc(q_ready, 1)
            pool.iota(steps_i[:, :], [[GE, NG + 1]], base=GE, channel_multiplier=0).then_inc(q_ready, 1)

            def body(g, s, use):
                pool.wait_ge(hot_made, g + 1)
                pool.tensor_tensor(hi_hot[:, s, :, 0, :], hi_hot[:, s, :, 1, :],
                                   cols(weight, g * G, G).unsqueeze(2).to_broadcast([P, G, NW]), ALU.mult).then_inc(weighted, 1)
            over_pairs(pool, NG, body)

        @block.vector
        def _(dve):
            def body(g, s, use):
                wait(dve, used, g - 1)
                dve.tensor_tensor(hi_hot[:, s, :, 1, :], lane_row[:, 0:NW].unsqueeze(1).to_broadcast([P, G, NW]),
                                  cols(src_hi, g * G, G).unsqueeze(2).to_broadcast([P, G, NW]), ALU.is_equal).then_inc(hot_made, 1)
                dve.tensor_tensor(lo_hot[:, s, :, :], lane_row[:, :].unsqueeze(1).to_broadcast([P, G, P]),
                                  cols(src_lo, g * G, G).unsqueeze(2).to_broadcast([P, G, P]), ALU.is_equal).then_inc(chain, 1)
            over_pairs(dve, NG, body)
            n = NG

            def then(instruction):
                nonlocal n
                n += 1
                instruction.then_inc(chain, 1)
                dve.wait_ge(chain, n)

            dve.wait_ge(used, NG)
            dve.tensor_copy(per_lane[:, :], ps[:, 1, :]).then_inc(lane_counts, 1)
            then(dve.tensor_scalar(deg[:, :], ps[:, 0, :], 1.0, None, ALU.add))
            then(dve.tensor_scalar(live[:, :], deg[:, :], 0.0, None, ALU.is_gt))
            then(dve.tensor_tensor(safe[:, :], deg[:, :], live[:, :], ALU.mult))
            then(dve.scalar_tensor_tensor(root[:, :], live[:, :], -1.0, safe[:, :], ALU.mult, ALU.add))
            then(dve.tensor_scalar(safe[:, :], root[:, :], 1.0, None, ALU.add))
            dve.engine_nop().then_inc(guarded, 1)
            dve.wait_ge(rooted, 1)
            then(dve.reciprocal(safe[:, :], root[:, :]))
            then(dve.tensor_tensor(dinv[:, :], safe[:, :], live[:, :], ALU.mult))
            dve.wait_ge(win_counts, 1)
            dve.wait_ge(q_ready, 2)
            then(dve.tensor_scalar(total[:, :], ps_sum[0:NW, 0:1], float(GE - 1), None, ALU.add))
            then(dve.tensor_scalar(full[:, :], steps_i[:, :], total[:, 0:1], None, ALU.is_le))
            then(dve.tensor_reduce(groups[:, :], full[:, :], AX_X, ALU.add))
            then(dve.tensor_scalar(padded[:, :], groups[:, :], float(GE), None, ALU.mult))
            dve.tensor_copy(padded_b[:, :], padded[:, 0:1].to_broadcast([NW, P])).then_inc(pads_made, 1)
            dve.wait_ge(starts_made, 1)
            dve.tensor_copy(q_f[:, :], q_i[:, :])
            then(dve.tensor_copy(start_row[:, :], ps_sum[:, 128:128 + NW]))
            then(dve.tensor_tensor(q_le[:, :, :], start_row[:, :].unsqueeze(1).to_broadcast([P, QP, NW]),
                                   q_f[:, :].unsqueeze(2).to_broadcast([P, QP, NW]), ALU.is_le))
            then(dve.tensor_reduce(q_win[:, :], q_le[:, :, :], AX_X, ALU.add))
            dve.tensor_scalar(q_out[:, :], q_win[:, :], -1.0, None, ALU.add).then_inc(q_made, 1)

        @block.scalar
        def _(act):
            act.wait_ge(guarded, 1)
            act.activation(root[:, :], safe[:, :], ACT.Sqrt).then_inc(rooted, 1)

        @block.tensor
        def _(pe):
            def body(g, s, use):
                pe.wait_ge(weighted, g + 1)
                pe.wait_ge(chain, g + 1)
                for j in range(G):
                    last = pe.matmul(ps[:, :, :].rearrange("p a b -> p (a b)"), lo_hot[:, s, j, :],
                                     hi_hot[:, s, j, :, :].rearrange("p a b -> p (a b)"),
                                     start=isinstance(g, int) and g == 0 and j == 0,
                                     stop=isinstance(g, int) and g == NG - 1 and j == G - 1, skip_group_check=True)
                last.then_inc(used, 1)
            over_pairs(pe, NG, body)
            pe.wait_ge(lane_counts, 1)
            pe.matmul(ps_sum[0:NW, 0:1], per_lane[:, :], ones[:, 0:1], start=True, stop=True).then_inc(win_counts, 1)
            pe.wait_ge(pads_made, 1)
            pe.matmul(ps_sum[:, 128:128 + NW], padded_b[:, :], before[0:NW, 0:NW], start=True, stop=True).then_inc(starts_made, 1)


def split_bf16(dve, then, value, rest, parts, last_sem):
    then(dve.tensor_copy(parts[0], value))
    then(dve.tensor_tensor(rest, value, parts[0], ALU.subtract))
    then(dve.tensor_copy(parts[1], rest))
    dve.tensor_tensor(parts[2], rest, parts[1], ALU.subtract).then_inc(last_sem, 1)


def scaled_nodes(nc, x, xs, dinv, tables, acc):
    with ExitStack() as ctx:
        y = acc.rearrange("p (a b) -> p a b", b=D)
        rest = tables[:, NW * 3 * D:NW * 5 * D].bitcast(F32).rearrange("p (a b) -> p a b", b=D)
        parts = tables[:, 0:NW * 3 * D].rearrange("p (a k b) -> p a k b", k=3, b=D)
        cleared = ctx.enter_context(nc.semaphore("x_cleared"))
        x_in = ctx.enter_context(nc.semaphore("x_in"))
        chain = ctx.enter_context(nc.semaphore("y_chain"))
        done = ctx.enter_context(nc.semaphore("y_done"))
        block = ctx.enter_context(nc.Block())

        @block.sync
        def _(sp):
            sp.wait_ge(cleared, 1)
            sp.dma_start(xs[:, 0:NW - 1, :], x[0:(NW - 1) * P, :].rearrange("(a p) c -> p a c", p=P)).then_inc(x_in, 16)
            sp.dma_start(xs[0:LAST, NW - 1, :], x[(NW - 1) * P:N, :]).then_inc(x_in, 16)

        @block.vector
        def _(dve):
            n = 0

            def then(instruction):
                nonlocal n
                n += 1
                instruction.then_inc(chain, 1)
                dve.wait_ge(chain, n)

            dve.memset(xs[:, NW - 1, :], 0.0).then_inc(cleared, 1)
            dve.wait_ge(x_in, 32)
            then(dve.tensor_tensor(y, xs[:, :, :], dinv[:, :].unsqueeze(2).to_broadcast([P, NW, D]), ALU.mult))
            split_bf16(dve, then, y, rest, [parts[:, :, k, :] for k in range(3)], done)


def move_rows(nc, dst, lane_row, node_id, before_bf, upto_bf, ones_bf, ones, zero_bf, src_hi, src_lo, weight,
              step_tab, start_row, tables, moved):
    with ExitStack() as ctx:
        def sb(name, shape, dt):
            return ctx.enter_context(nc.sbuf_tensor(name, shape, dt))

        def sem(name):
            return ctx.enter_context(nc.semaphore(name))

        dst_rows = sb("dst_rows", [P, 2, GE], I32)
        dst_hot = sb("dst_hot", [P, 2 * GE], BF16)
        hi_hot = sb("place_hot", [P, 2, G, NW], BF16)
        junk = sb("junk", [P, 2, G, NW], F32)
        place_f = sb("place_f", [P, 2, G], F32)
        place = sb("place", [P, 2, G], I32)
        rows = sb("rows", [P, 2, G, ROW], F32)
        ps_rows = ctx.enter_context(nc.psum_tensor("ps_rows", [P, 2, 512], F32))
        ps_place = ctx.enter_context(nc.psum_tensor("ps_place", [P, G, NW], F32))
        rows_in = [sem(f"dst_rows_in{s}") for s in range(2)]
        scattered = [sem(f"scattered{s}") for s in range(2)]
        hot_made, steps_done = sem("dst_hot_made"), sem("gather_steps_done")
        hi_made, placed, read = sem("place_hot_made"), sem("placed"), sem("places_read")
        cast, rows_ready = sem("places_cast"), sem("rows_ready")
        parts = tables[:, 0:NW * 3 * D]
        passed = sem("move_rows_passed")
        block = ctx.enter_context(nc.Block())

        @block.sync
        def _(sp):
            def body(g, s, use):
                wait(sp, placed, g - 1)
                sp.dma_start(dst_rows[:, s, :], dst[bass.ds(g * GE, GE)].unsqueeze(0).to_broadcast([P, GE])).then_inc(rows_in[s], 16)
            over_pairs(sp, NG, body)

        @block.vector
        def _(dve):
            def read_places(g, s, use):
                dve.wait_ge(placed, g + 1)
                for j in range(G):
                    last = dve.tensor_tensor_reduce(junk[:, s, j, :], ps_place[:, j, :], hi_hot[:, s, j, :], 1.0, 0.0,
                                                    ALU.mult, ALU.add, place_f[:, s, j:j + 1])
                last.then_inc(read, 1)
                dve.wait_ge(read, g + 1)
                wait(dve, scattered[s], use * (16 * G))
                dve.tensor_copy(place[:, s, :], place_f[:, s, :]).then_inc(cast, 1)

            def body(g, s, use):
                wait(dve, placed, g)
                dve.tensor_tensor(hi_hot[:, s, :, :], lane_row[:, 0:NW].unsqueeze(1).to_broadcast([P, G, NW]),
                                  cols(src_hi, g * G, G).unsqueeze(2).to_broadcast([P, G, NW]), ALU.is_equal).then_inc(hi_made, 1)
                k0, k1, to_window = load_steps(dve, step_tab, g)
                wait_alone(dve, rows_in[s], use * 16 + 16, passed)
                with dve.Fori(k0, k1) as k:
                    dve.wait_ge(steps_done, k + 1)
                    dve.tensor_scalar(cols(dst_hot, (k % 2) * GE, GE), dst_rows[:, s, :], cols(node_id, window(dve, k + to_window), 1), None,
                                      ALU.is_equal).then_inc(hot_made, 1)
                if isinstance(g, int) and g == 0:
                    return
                read_places(g - 1, 1 - s, use if s else use - 1)
            over_pairs(dve, NG, body)
            read_places(NG - 1, (NG - 1) % 2, (NG - 1) // 2)

        @block.tensor
        def _(pe):
            pe.sem_inc(steps_done, 2)
            pe.matmul(ps_place[:, :, :], ones[0:1, :], start_row[0:1, :].unsqueeze(1).to_broadcast([1, G, NW]),
                      start=True, stop=False, skip_group_check=True)

            def body(g, s, use):
                wait(pe, rows_ready, g - 1)
                pe.matmul(ps_rows[:, s, 0:G * D], zero_bf[:, 0:P], zero_bf[:, 0:G * D], start=True, stop=False, skip_group_check=True)
                k0, k1, to_window = load_steps(pe, step_tab, g)
                with pe.Fori(k0, k1) as k:
                    pe.wait_ge(hot_made, k + 1)
                    at = window(pe, k + to_window) * (3 * D)
                    for j in range(G):
                        for i in range(3):
                            last = pe.matmul(ps_rows[:, s, j * D:(j + 1) * D], cols(dst_hot, (k % 2) * GE + j * P, P),
                                             cols(parts, at + i * D, D), start=False, stop=False, skip_group_check=True)
                    last.then_inc(steps_done, 1)

                def advance(j0, j1, stationary, hot):
                    last = pe.matmul(ps_place[:, j0:j1, :], stationary[:, :], hot, start=False, stop=False, skip_group_check=True)
                    return last

                if not (isinstance(g, int) and g == 0):
                    pe.wait_ge(read, g)
                    advance(0, G, upto_bf, hi_hot[:, 1 - s, :, :])
                    for j in range(1, G):
                        advance(0, j, ones_bf, hi_hot[:, 1 - s, j:j + 1, :].to_broadcast([P, j, NW]))
                pe.wait_ge(hi_made, g + 1)
                for j in range(G - 1):
                    advance(j + 1, G, ones_bf, hi_hot[:, s, j:j + 1, :].to_broadcast([P, G - 1 - j, NW]))
                advance(0, G, before_bf, hi_hot[:, s, :, :]).then_inc(placed, 1)
            over_pairs(pe, NG, body)

        @block.scalar
        def _(act):
            def body(g, s, use):
                act.wait_ge(placed, g + 1)
                wait(act, scattered[s], use * (16 * G))
                for j in range(G):
                    act.activation(rows[:, s, j, 0:D], ps_rows[:, s, j * D:(j + 1) * D], ACT.Copy, scale=cols(weight, g * G + j, 1))
                act.activation(rows[:, s, :, D], cols(src_lo, g * G, G), ACT.Copy).then_inc(rows_ready, 1)
            over_pairs(act, NG, body)

        @block.gpsimd
        def _(pool):
            def body(g, s, use):
                pool.wait_ge(cast, g + 1)
                wait_alone(pool, rows_ready, g + 1, passed)
                for j in range(G):
                    pool.indirect_dma_start(out=moved[:, :], out_offset=bass.IndirectOffsetOnAxis(ap=place[:, s, j:j + 1], axis=0),
                                            in_=rows[:, s, j, :], in_offset=None).then_inc(scattered[s], 16)
            over_pairs(pool, NG, body)
            pool.wait_ge(scattered[0], 16 * G * ((NG + 1) // 2))
            pool.wait_ge(scattered[1], 16 * G * (NG // 2))


def load_steps(eng, step_tab, g):
    k0 = eng.value_load(step_tab[0:1, bass.ds(g * 3, 1)], min_val=0, max_val=MAXSTEP)
    k1 = eng.value_load(step_tab[0:1, bass.ds(g * 3 + 1, 1)], min_val=0, max_val=MAXSTEP)
    to_window = eng.value_load(step_tab[0:1, bass.ds(g * 3 + 2, 1)], min_val=-MAXSTEP, max_val=NW - 1)
    return k0, k1, to_window


def window(eng, value):
    return eng.snap(value).with_bounds(min_val=0, max_val=NW - 1)


def sum_moved(nc, lane_row, q_tab, moved, acc):
    with ExitStack() as ctx:
        def sb(name, shape, dt):
            return ctx.enter_context(nc.sbuf_tensor(name, shape, dt))

        def sem(name):
            return ctx.enter_context(nc.semaphore(name))

        rows = sb("moved_rows", [P, 2, G, ROW], F32)
        hot = sb("lane_hot", [P, 2, G, P], F32)
        ps = ctx.enter_context(nc.psum_tensor("ps_moved", [P, 2, 512], F32))
        rows_in = [sem(f"moved_in{s}") for s in range(2)]
        hot_made, summed, added, cleared = sem("lane_hot_made"), sem("rows_summed"), sem("sums_added"), sem("sums_cleared")
        block = ctx.enter_context(nc.Block())

        @block.sync
        def _(sp):
            def body(q, s, use):
                wait(sp, summed, q - 1)
                sp.dma_start(rows[:, s, :, :].rearrange("p a b -> p (a b)"),
                             moved[bass.ds(q * GE, GE), :].rearrange("(p r) c -> p (r c)", p=P)).then_inc(rows_in[s], 16)
            over_pairs(sp, NQ, body)

        @block.vector
        def _(dve):
            def add(q, s):
                dve.wait_ge(summed, q + 1)
                wait(dve, added, q)
                at = dve.value_load(q_tab[0:1, bass.ds(q, 1)], min_val=0, max_val=NW - 1)
                here = cols(acc, at * D, D)
                dve.tensor_tensor(here, here, ps[:, s, 0:D], ALU.add).then_inc(added, 1)

            dve.memset(acc, 0.0).then_inc(cleared, 1)
            dve.wait_ge(cleared, 1)

            def body(q, s, use):
                dve.wait_ge(rows_in[s], use * 16 + 16)
                wait(dve, summed, q - 1)
                dve.tensor_tensor(hot[:, s, :, :], lane_row[:, :].unsqueeze(1).to_broadcast([P, G, P]),
                                  rows[:, s, :, D:D + 1].to_broadcast([P, G, P]), ALU.is_equal).then_inc(hot_made, 1)
                if not (isinstance(q, int) and q == 0):
                    add(q - 1, 1 - s)
            over_pairs(dve, NQ, body)
            add(NQ - 1, (NQ - 1) % 2)

        @block.tensor
        def _(pe):
            def body(q, s, use):
                pe.wait_ge(hot_made, q + 1)
                wait(pe, added, q - 1)
                for j in range(G):
                    last = pe.matmul(ps[:, s, 0:D], hot[:, s, j, :], rows[:, s, j, 0:D], start=(j == 0), stop=(j == G - 1))
                last.then_inc(summed, 1)
            over_pairs(pe, NQ, body)


def nodes(nc, ident, eps, xs, dinv, acc, W_T, b_b, W1_T, b1_b, tables, a_dram, x1_dram):
    with ExitStack() as ctx:
        def sb(name, shape, dt=F32):
            return ctx.enter_context(nc.sbuf_tensor(name, shape, dt))

        def sem(name):
            return ctx.enter_context(nc.semaphore(name))

        agg = sb("agg", [P, UB, D])
        aggT = sb("aggT", [D, UB * P])
        z = sb("z", [P, UB, D])
        stats = sb("stats", [P, UB, 6])
        mv = sb("mv", [P, UB, 2])
        std = sb("std", [P, UB])
        rstd = sb("rstd", [P, UB])
        x_new = sb("x_new", [P, UB, D])
        xT = sb("xT", [D, UB * P])
        a_out = sb("a_out", [P, UB, HD])
        b_f = sb("b_f", [P, UB, HD])
        b_rest = sb("b_rest", [P, UB, HD])
        ps_T = ctx.enter_context(nc.psum_tensor("ps_T", [P, 1024], F32))
        ps_z = ctx.enter_context(nc.psum_tensor("ps_z", [P, UB, D], F32))
        ps_ab = ctx.enter_context(nc.psum_tensor("ps_ab", [P, 8, 2 * HD], F32))
        chain, made, turned, copied = sem("node_chain"), sem("agg_made"), sem("agg_turned"), sem("agg_copied")
        projected, varied, rooted, normed = sem("projected"), sem("variance_made"), sem("variance_rooted"), sem("normed")
        x_turned, x_copied, halves, b_read, b_split = sem("x_turned"), sem("x_copied"), sem("halves_made"), sem("b_read"), sem("b_split")
        a_copied, stored = sem("a_copied"), sem("a_stored")
        passed = sem("nodes_passed")
        block = ctx.enter_context(nc.Block())

        @block.vector
        def _(dve):
            def batch(m, steps):
                n = 0

                def then(instruction):
                    nonlocal n
                    n += 1
                    instruction.then_inc(chain, 1)
                    wait_alone(dve, chain, m * steps + n, passed)

                x_b = xs[:, bass.ds(m * UB, UB), :]
                d_b = cols(dinv, m * UB, UB).unsqueeze(2).to_broadcast([P, UB, D])
                a_b = split3(cols(acc, m * (UB * D), UB * D), UB)
                then(dve.tensor_tensor(z[:, :, :], x_b, d_b, ALU.mult))
                then(dve.tensor_tensor(z[:, :, :], z[:, :, :], a_b, ALU.add))
                dve.tensor_tensor(agg[:, :, :], z[:, :, :], d_b, ALU.mult).then_inc(made, 1)
                dve.wait_ge(projected, m + 1)
                then(dve.tensor_tensor(z[:, :, :], ps_z[:, :, :], b_b[:, :].unsqueeze(1).to_broadcast([P, UB, D]), ALU.add))
                then(dve.tensor_tensor(z[:, :, :], z[:, :, :], x_b, ALU.add))
                for j in range(UB):
                    last = dve.bn_stats(stats[:, j, :], z[:, j, :])
                then(last)
                for j in range(UB):
                    last = dve.bn_aggr(mv[:, j, :], stats[:, j, :])
                last.then_inc(varied, 1)
                dve.wait_ge(rooted, m + 1)
                then(dve.reciprocal(rstd[:, :], std[:, :]))
                then(dve.tensor_tensor(z[:, :, :], z[:, :, :], mv[:, :, 0:1].to_broadcast([P, UB, D]), ALU.subtract))
                dve.tensor_tensor(x_new[:, :, :], z[:, :, :], rstd[:, :].unsqueeze(2).to_broadcast([P, UB, D]), ALU.mult).then_inc(normed, 1)
                dve.wait_ge(halves, m + 1)
                dve.tensor_tensor(b_f[:, :, :], ps_ab[:, 0:UB, HD:], b1_b[:, :].unsqueeze(1).to_broadcast([P, UB, HD]), ALU.add).then_inc(b_read, 1)
                dve.wait_ge(b_read, m + 1)
                b_parts = cols(tables, m * (UB * 3 * HD), UB * 3 * HD).rearrange("p (a k b) -> p a k b", k=3, b=HD)
                split_bf16(dve, then, b_f[:, :, :], b_rest[:, :, :], [b_parts[:, :, i, :] for i in range(3)], b_split)
                dve.wait_ge(b_split, m + 1)
                dve.wait_ge(stored, m * 32 + 32)
                assert n == steps, n

            with dve.Fori(0, NU) as m:
                batch(m, 10)

        @block.scalar
        def _(act):
            with act.Fori(0, NU) as m:
                act.wait_ge(turned, m + 1)
                act.activation(aggT[:, :], ps_T[0:D, 0:UB * P], ACT.Copy).then_inc(copied, 1)
                act.wait_ge(varied, m + 1)
                act.activation(std[:, :], mv[:, :, 1], ACT.Sqrt, bias=eps[:, 0:1]).then_inc(rooted, 1)
                act.wait_ge(x_turned, m + 1)
                act.activation(xT[:, :], ps_T[0:D, 0:UB * P], ACT.Copy).then_inc(x_copied, 1)
                act.wait_ge(b_read, m + 1)
                act.activation(a_out[:, :, :], ps_ab[:, 0:UB, 0:HD], ACT.Copy).then_inc(a_copied, 1)
                act.wait_ge(normed, m + 1)
                act.dma_start(x1_dram[bass.ds(m * (UB * P), UB * P), :].rearrange("(a p) c -> p a c", p=P),
                              x_new[:, :, :]).then_inc(stored, 16)
                act.wait_ge(a_copied, m + 1)
                act.dma_start(a_dram[bass.ds(m * (UB * P), UB * P), :].rearrange("(a p) c -> p a c", p=P),
                              a_out[:, :, :]).then_inc(stored, 16)
                act.wait_ge(stored, m * 32 + 32)

        @block.tensor
        def _(pe):
            with pe.Fori(0, NU) as m:
                wait_alone(pe, made, m + 1, passed)
                for j in range(UB):
                    last = pe.transpose(ps_T[0:D, j * P:(j + 1) * P], agg[:, j, :], ident[:, :])
                last.then_inc(turned, 1)
                pe.wait_ge(copied, m + 1)
                for j in range(UB):
                    last = pe.matmul(ps_z[:, j, :], aggT[:, j * P:(j + 1) * P], W_T[:, :], start=True, stop=True)
                last.then_inc(projected, 1)
                wait_alone(pe, normed, m + 1, passed)
                for j in range(UB):
                    last = pe.transpose(ps_T[0:D, j * P:(j + 1) * P], x_new[:, j, :], ident[:, :])
                last.then_inc(x_turned, 1)
                pe.wait_ge(x_copied, m + 1)
                for j in range(UB):
                    last = pe.matmul(ps_ab[:, j, :], xT[:, j * P:(j + 1) * P], W1_T[:, :], start=True, stop=True)
                last.then_inc(halves, 1)


def messages(nc, dst, attr, lane_row, node_id, window_base, ones_bf, src_hi, src_lo, dst_f, c_row, step_tab, tables, sums, a_dram):
    with ExitStack() as ctx:
        def sb(name, shape, dt):
            return ctx.enter_context(nc.sbuf_tensor(name, shape, dt))

        def sem(name):
            return ctx.enter_context(nc.semaphore(name))

        dst_rows = sb("m_dst_rows", [P, 2, GE], I32)
        attr_row = sb("attr_row", [1, 2, GE], F32)
        dst_hot = sb("m_dst_hot", [P, 2 * GE], BF16)
        node_hot = sb("node_hot", [P, G, P], F32)
        src_f = sb("src_f", [P, 2, G], F32)
        src_i = sb("src_i", [P, 2, G], I32)
        a_rows = sb("a_rows", [P, 2, G, HD], F32)
        hidden = sb("hidden", [P, 2, G, HD + 1], F32)
        ps_pre = ctx.enter_context(nc.psum_tensor("ps_pre", [P, 2, 1024], F32))
        ps_sum = ctx.enter_context(nc.psum_tensor("ps_msum", [P, 512], F32))
        ps_mark = ctx.enter_context(nc.psum_tensor("ps_mark", [P, 512], F32))
        rows_in = [sem(f"edge_rows_in{s}") for s in range(2)]
        a_in = [sem(f"a_rows_in{s}") for s in range(2)]
        cleared, indexed, index_f = sem("m_cleared"), sem("indexed"), sem("index_f")
        hot_made, steps_done, gathered = sem("m_dst_hot_made"), sem("m_steps_done"), sem("m_gathered")
        added, relued = sem("pre_added"), sem("relued")
        node_hot_made, summed, kept = sem("node_hot_made"), sem("window_summed"), sem("window_kept")
        passed = sem("messages_passed")
        block = ctx.enter_context(nc.Block())

        @block.sync
        def _(sp):
            def body(g, s, use):
                wait(sp, gathered, g - 1)
                sp.dma_start(dst_rows[:, s, :], dst[bass.ds(g * GE, GE)].unsqueeze(0).to_broadcast([P, GE])).then_inc(rows_in[s], 16)
                sp.dma_start(attr_row[:, s, :], attr[bass.ds(g * GE, GE), :].rearrange("e c -> c e")).then_inc(rows_in[s], 16)
            over_pairs(sp, NG, body)

        @block.gpsimd
        def _(pool):
            def body(g, s, use):
                wait(pool, added, g - 1)
                wait_alone(pool, indexed, g + 1, passed)
                for j in range(G):
                    pool.indirect_dma_start(out=a_rows[:, s, j, :], out_offset=None, in_=a_dram[:, :],
                                            in_offset=bass.IndirectOffsetOnAxis(ap=src_i[:, s, j:j + 1], axis=0)).then_inc(a_in[s], 16)
            over_pairs(pool, NG, body)

        @block.vector
        def _(dve):
            def add_pre(g, s, use):
                dve.wait_ge(a_in[s], use * (16 * G) + 16 * G)
                dve.wait_ge(gathered, g + 1)
                dve.tensor_tensor(hidden[:, s, :, 0:HD], split3(ps_pre[:, s, 0:G * HD], G), a_rows[:, s, :, :], ALU.add).then_inc(added, 1)

            def sum_windows(g):
                k0, k1, to_window = load_steps(dve, step_tab, g)
                with dve.Fori(k0, k1) as k:
                    at = window(dve, k + to_window)
                    for j in range(G):
                        last = dve.tensor_scalar(node_hot[:, j, :], lane_row[:, :], cols(window_base, at, 1), cols(dst_f, g * G + j, 1),
                                                 ALU.add, ALU.is_equal)
                    last.then_inc(node_hot_made, 1)
                    dve.wait_ge(summed, k + 1)
                    dve.wait_ge(kept, k + 1)
                    here = sums[:, bass.ds(at, 1), :].rearrange("p a b -> p (a b)")
                    dve.tensor_tensor(here, here, ps_sum[:, 0:HD + 1], ALU.add).then_inc(kept, 1)

            dve.memset(sums[:, :, :], 0.0).then_inc(kept, 1)
            dve.memset(hidden[:, :, :, HD], 1.0).then_inc(cleared, 1)

            def body(g, s, use):
                wait(dve, a_in[s], use * (16 * G))
                dve.scalar_tensor_tensor(src_f[:, s, :], cols(src_hi, g * G, G), float(P), cols(src_lo, g * G, G),
                                         ALU.mult, ALU.add).then_inc(index_f, 1)
                dve.wait_ge(index_f, g + 1)
                dve.tensor_copy(src_i[:, s, :], src_f[:, s, :]).then_inc(indexed, 1)
                k0, k1, to_window = load_steps(dve, step_tab, g)
                wait_alone(dve, rows_in[s], use * 32 + 32, passed)
                with dve.Fori(k0, k1) as k:
                    dve.wait_ge(steps_done, k + 1)
                    dve.tensor_scalar(cols(dst_hot, (k % 2) * GE, GE), dst_rows[:, s, :], cols(node_id, window(dve, k + to_window), 1), None,
                                      ALU.is_equal).then_inc(hot_made, 1)
                if isinstance(g, int) and g == 0:
                    return
                add_pre(g - 1, 1 - s, use if s else use - 1)
                sum_windows(g - 1)
            over_pairs(dve, NG, body)
            add_pre(NG - 1, (NG - 1) % 2, (NG - 1) // 2)
            sum_windows(NG - 1)

        @block.scalar
        def _(act):
            def body(g, s, use):
                act.wait_ge(added, g + 1)
                act.activation(hidden[:, s, :, 0:HD], hidden[:, s, :, 0:HD], ACT.Relu).then_inc(relued, 1)
            over_pairs(act, NG, body)

        @block.tensor
        def _(pe):
            def sum_windows(g, s):
                k0, k1, _ = load_steps(pe, step_tab, g)
                wait_alone(pe, relued, g + 1, passed)
                with pe.Fori(k0, k1) as k:
                    pe.wait_ge(node_hot_made, k + 1)
                    for j in range(G):
                        last = pe.matmul(ps_sum[:, 0:HD + 1], node_hot[:, j, :], hidden[:, s, j, :], start=(j == 0), stop=(j == G - 1))
                    last.then_inc(summed, 1)

            pe.sem_inc(steps_done, 2)
            pe.wait_ge(cleared, 1)

            def body(g, s, use):
                wait(pe, added, g - 1)
                pe.wait_ge(rows_in[s], use * 32 + 32)
                for j in range(G):
                    pe.matmul(ps_pre[:, s, j * HD:(j + 1) * HD], attr_row[:, s, j * P:(j + 1) * P], c_row[:, :],
                              start=j in (0, 4), stop=False, skip_group_check=True)
                k0, k1, to_window = load_steps(pe, step_tab, g)
                with pe.Fori(k0, k1) as k:
                    pe.wait_ge(hot_made, k + 1)
                    at = window(pe, k + to_window) * (3 * HD)
                    for j in range(G):
                        for i in range(3):
                            last = pe.matmul(ps_pre[:, s, j * HD:(j + 1) * HD], cols(dst_hot, (k % 2) * GE + j * P, P),
                                             cols(tables, at + i * HD, HD), start=False, stop=False, skip_group_check=True)
                    last.then_inc(steps_done, 1)
                pe.matmul(ps_mark[:, 0:1], ones_bf[:, :], ones_bf[:, 0:1], start=True, stop=True).then_inc(gathered, 1)
                if not (isinstance(g, int) and g == 0):
                    sum_windows(g - 1, 1 - s)
            over_pairs(pe, NG, body)
            sum_windows(NG - 1, (NG - 1) % 2)


def update(nc, ident, eps, x1_dram, sums, W2_T, b2_b, Wih_T, bih_b, Whh_T, bhh_b, out):
    UG = 2
    NS = NW // UG
    with ExitStack() as ctx:
        def sb(name, shape, dt=F32):
            return ctx.enter_context(nc.sbuf_tensor(name, shape, dt))

        def sem(name):
            return ctx.enter_context(nc.semaphore(name))

        hx = sb("hx", [P, UG, HD + 1])
        xws = sb("xw", [P, 2, UG, D])
        hT = sb("hT", [P, UG * P])
        xT = sb("u_xT", [D, UG * P])
        agT = sb("agT", [D, UG * P])
        ag = sb("ag", [P, UG, D])
        cb2 = sb("cb2", [P, UG, D])
        gi, gh = sb("gi", [P, UG, 3 * D]), sb("gh", [P, UG, 3 * D])
        pre_rz, rz = sb("pre_rz", [P, UG, 2 * D]), sb("rz", [P, UG, 2 * D])
        t1, t2, nn = sb("t1", [P, UG, D]), sb("t2", [P, UG, D]), sb("nn", [P, UG, D])
        t3, t4, z1, z2 = (sb(n, [P, UG, D]) for n in ("t3", "t4", "z1", "z2"))
        stats, mv = sb("u_stats", [P, UG, 6]), sb("u_mv", [P, UG, 2])
        rstd, var, power = sb("u_rstd", [P, UG]), sb("u_var", [P, UG]), sb("power", [P, UG])
        res = sb("res", [P, 2, UG, D])
        ps_hT = ctx.enter_context(nc.psum_tensor("ps_hT", [P, 512], F32))
        ps_xT = ctx.enter_context(nc.psum_tensor("ps_xT", [P, 512], F32))
        ps_ag = ctx.enter_context(nc.psum_tensor("ps_ag", [P, UG, D], F32))
        ps_agT = ctx.enter_context(nc.psum_tensor("ps_agT", [P, 512], F32))
        ps_gi = ctx.enter_context(nc.psum_tensor("ps_gi", [P, UG, 256], F32))
        ps_gh = ctx.enter_context(nc.psum_tensor("ps_gh", [P, UG, 256], F32))
        chain, staged, turned, copied = sem("u_chain"), sem("u_staged"), sem("u_turned"), sem("u_copied")
        second, ag_made, ag_turned, ag_copied = sem("second_layer"), sem("ag_made"), sem("ag_turned"), sem("ag_copied")
        gates, rz_ready, rz_done = sem("gates_made"), sem("rz_ready"), sem("rz_done")
        n_ready, n_done, varied, rooted = sem("n_ready"), sem("n_done"), sem("u_varied"), sem("u_rooted")
        eps_added = sem("eps_added")
        x_in = [sem("u_x_in0"), sem("u_x_in1")]
        ready, stored = sem("result_ready"), [sem("stored0"), sem("stored1")]
        passed = sem("update_passed")
        block = ctx.enter_context(nc.Block())

        def per_step(eng, body):
            over_pairs(eng, NS, body)

        @block.vector
        def _(dve):
            def body(m, s, use):
                n, steps = 0, 10

                def then(instruction):
                    nonlocal n
                    n += 1
                    instruction.then_inc(chain, 1)
                    wait_alone(dve, chain, m * steps + n, passed)

                dve.tensor_copy(hx[:, :, :], sums[:, bass.ds(m * UG, UG), :]).then_inc(staged, 1)
                dve.wait_ge(x_in[s], use * 16 + 16)
                dve.wait_ge(staged, m + 1)
                then(dve.tensor_tensor(cb2[:, :, :], hx[:, :, HD:HD + 1].to_broadcast([P, UG, D]),
                                       b2_b[:, :].unsqueeze(1).to_broadcast([P, UG, D]), ALU.mult))
                dve.wait_ge(second, m + 1)
                dve.tensor_tensor(ag[:, :, :], ps_ag[:, :, :], cb2[:, :, :], ALU.add).then_inc(ag_made, 1)
                dve.wait_ge(gates, m + 1)
                dve.tensor_tensor(gi[:, :, :], ps_gi[:, :, 0:3 * D], bih_b[:, :].unsqueeze(1).to_broadcast([P, UG, 3 * D]), ALU.add)
                then(dve.tensor_tensor(gh[:, :, :], ps_gh[:, :, 0:3 * D], bhh_b[:, :].unsqueeze(1).to_broadcast([P, UG, 3 * D]), ALU.add))
                dve.tensor_tensor(pre_rz[:, :, :], gi[:, :, 0:2 * D], gh[:, :, 0:2 * D], ALU.add).then_inc(rz_ready, 1)
                dve.wait_ge(rz_done, m + 1)
                then(dve.tensor_tensor(t1[:, :, :], rz[:, :, 0:D], gh[:, :, 2 * D:], ALU.mult))
                dve.tensor_tensor(t2[:, :, :], gi[:, :, 2 * D:], t1[:, :, :], ALU.add).then_inc(n_ready, 1)
                then(dve.tensor_scalar(t3[:, :, :], rz[:, :, D:], -1.0, 1.0, ALU.mult, ALU.add))
                then(dve.tensor_tensor(t4[:, :, :], rz[:, :, D:], xws[:, s, :, :], ALU.mult))
                dve.wait_ge(n_done, m + 1)
                then(dve.tensor_tensor(t3[:, :, :], t3[:, :, :], nn[:, :, :], ALU.mult))
                then(dve.tensor_tensor(z1[:, :, :], t3[:, :, :], t4[:, :, :], ALU.add))
                then(dve.tensor_tensor(z2[:, :, :], z1[:, :, :], xws[:, s, :, :], ALU.add))
                for j in range(UG):
                    last = dve.bn_stats(stats[:, j, :], z2[:, j, :])
                then(last)
                for j in range(UG):
                    last = dve.bn_aggr(mv[:, j, :], stats[:, j, :])
                last.then_inc(varied, 1)
                dve.wait_ge(rooted, m + 1)
                then(dve.tensor_tensor(z1[:, :, :], z2[:, :, :], mv[:, :, 0:1].to_broadcast([P, UG, D]), ALU.subtract))
                wait(dve, stored[s], use * (16 * UG))
                dve.tensor_tensor(res[:, s, :, :], z1[:, :, :], rstd[:, :].unsqueeze(2).to_broadcast([P, UG, D]), ALU.mult).then_inc(ready, 1)
                assert n == steps, n
            per_step(dve, body)

        @block.gpsimd
        def _(pool):
            pool.memset(power[:, :], -0.5)

            def body(m, s, use):
                pool.wait_ge(varied, m + 1)
                pool.tensor_tensor(var[:, :], mv[:, :, 1], eps[:, 0:1].to_broadcast([P, UG]), ALU.add).then_inc(eps_added, 1)
                pool.wait_ge(eps_added, m + 1)
                pool.tensor_tensor(rstd[:, :], var[:, :], power[:, :], ALU.pow).then_inc(rooted, 1)
            per_step(pool, body)

        @block.scalar
        def _(act):
            def body(m, s, use):
                act.wait_ge(turned, m + 1)
                act.activation(hT[:, :], ps_hT[:, 0:UG * P], ACT.Copy)
                act.activation(xT[:, :], ps_xT[0:D, 0:UG * P], ACT.Copy).then_inc(copied, 1)
                act.wait_ge(ag_turned, m + 1)
                act.activation(agT[:, :], ps_agT[0:D, 0:UG * P], ACT.Copy).then_inc(ag_copied, 1)
                act.wait_ge(rz_ready, m + 1)
                act.activation(rz[:, :, :], pre_rz[:, :, :], ACT.Sigmoid).then_inc(rz_done, 1)
                act.wait_ge(n_ready, m + 1)
                act.activation(nn[:, :, :], t2[:, :, :], ACT.Tanh).then_inc(n_done, 1)
            per_step(act, body)

        @block.tensor
        def _(pe):
            def body(m, s, use):
                pe.wait_ge(staged, m + 1)
                pe.wait_ge(x_in[s], use * 16 + 16)
                for j in range(UG):
                    pe.transpose(ps_hT[:, j * P:(j + 1) * P], hx[:, j, 0:HD], ident[:, :])
                    last = pe.transpose(ps_xT[0:D, j * P:(j + 1) * P], xws[:, s, j, :], ident[:, :])
                last.then_inc(turned, 1)
                pe.wait_ge(copied, m + 1)
                for j in range(UG):
                    last = pe.matmul(ps_ag[:, j, :], hT[:, j * P:(j + 1) * P], W2_T[:, :], start=True, stop=True)
                last.then_inc(second, 1)
                for j in range(UG):
                    pe.matmul(ps_gh[:, j, 0:3 * D], xT[:, j * P:(j + 1) * P], Whh_T[:, :], start=True, stop=True)
                wait_alone(pe, ag_made, m + 1, passed)
                for j in range(UG):
                    last = pe.transpose(ps_agT[0:D, j * P:(j + 1) * P], ag[:, j, :], ident[:, :])
                last.then_inc(ag_turned, 1)
                pe.wait_ge(ag_copied, m + 1)
                for j in range(UG):
                    last = pe.matmul(ps_gi[:, j, 0:3 * D], agT[:, j * P:(j + 1) * P], Wih_T[:, :], start=True, stop=True)
                last.then_inc(gates, 1)
            per_step(pe, body)

        @block.sync
        def _(sp):
            def load(m, s):
                sp.dma_start(xws[:, s, :, :], x1_dram[bass.ds(m * (UG * P), UG * P), :].rearrange("(a p) c -> p a c", p=P)).then_inc(x_in[s], 16)

            load(0, 0)

            def body(m, s, use):
                if not isinstance(m, int) or m + 1 < NS:
                    load(m + 1, 1 - s)
                sp.wait_ge(ready, m + 1)
                for j in range(UG):
                    rows = LAST if isinstance(m, int) and m * UG + j == NW - 1 else P
                    sp.dma_start(out[bass.ds(m * (UG * P) + j * P, rows), :], res[0:rows, s, j, :]).then_inc(stored[s], 16)
            per_step(sp, body)
            sp.wait_ge(stored[0], 16 * UG * ((NS + 1) // 2))
            sp.wait_ge(stored[1], 16 * UG * (NS // 2))


INS = ["x", "src", "dst", "edge_weight", "edge_weight1", "L0_gnn_W", "L0_gnn_b", "L1_gnn_W1", "L1_gnn_b1", "L1_gnn_W2",
       "L1_gnn_b2", "L1_gnn_W_ih", "L1_gnn_b_ih", "L1_gnn_W_hh", "L1_gnn_b_hh"]


def kernel(**inputs):
    import numpy as np
    import concourse.bacc as bacc
    from concourse.bass_utils import run_bass_kernel_spmd

    nc = bacc.Bacc("TRN2", target_bir_lowering=False, num_devices=1)
    arrays, args = {}, []
    for name in INS:
        a = np.ascontiguousarray(inputs[name])
        arrays[f"in_{name}"] = a
        args.append(nc.dram_tensor(f"in_{name}", a.shape, mybir.dt.from_np(a.dtype), kind="ExternalInput").ap())
    x1_dram = nc.dram_tensor("x_after_layer0", (NW * P, D), F32, kind="Internal").ap()
    result = nc.dram_tensor("result", (N, D), F32, kind="ExternalOutput").ap()
    q_windows = nc.dram_tensor("q_windows", (P * QP,), I32, kind="Internal").ap()
    steps = nc.dram_tensor("steps", (3 * NG,), I32, kind="Internal").ap()
    moved = nc.dram_tensor("moved", (NQ * GE, ROW), F32, kind="Internal").ap()
    a_dram = nc.dram_tensor("a_half", (NW * P, HD), F32, kind="Internal").ap()
    program(nc, *args, result, q_windows, steps, moved, a_dram, x1_dram)
    r = run_bass_kernel_spmd(nc, [arrays], core_ids=[0])
    return r.results[0]["result"]
```

```python
from contextlib import ExitStack

import concourse.bass as bass
from concourse import mybir

F32, BF16, I32 = mybir.dt.float32, mybir.dt.bfloat16, mybir.dt.int32
ALU, ACT = mybir.AluOpType, mybir.ActivationFunctionType
AX_X = mybir.AxisListType.X

P = 128
N, E, D, HD = 12500, 400000, 64, 128
NW = (N + P - 1) // P
LAST = N - (NW - 1) * P
TILES = E // P
G = 5
GE = G * P
NG = TILES // G
NB = 25
BT = TILES // NB
ROW = D + 1
NQ = (E + NW * (GE - 1)) // GE + 1
NQ += -NQ % 4
QP = 6
EPS = 1e-05
UB = 7
NU = NW // UB
MAXSTEP = NG * NW
S = 4
NCOL = 4
assert TILES == NG * G == NB * BT and NG == 5 * (NB * BT // 25) and NW % UB == 0 and NQ <= P * QP


def wait(eng, sem, value):
    if not isinstance(value, int) or value > 0:
        eng.wait_ge(sem, value)


def wait_alone(eng, sem, value, passed):
    eng.wait_ge(sem, value)
    eng.sem_inc(passed, 1)


def over_pairs(eng, n, body, first=0):
    body(0, 0, 0)
    body(1, 1, 0)
    with eng.Fori(1, n // 2) as i:
        body(i * 2, 0, i)
        body(i * 2 + 1, 1, i)
    if n % 2:
        body(n - 1, 0, n // 2)


def over_groups(eng, n, body, load=None):
    def turn(i, count):
        loaded = load(i * S, count) if load else None
        for s in range(count):
            body(i * S + s, s, i, loaded)
    turn(0, S)
    with eng.Fori(1, n // S) as i:
        turn(i, S)
    if n % S:
        turn(n // S, n % S)


def last_of(g, s, use):
    return g - 1, (s - 1) % S, use if s else use - 1


def is_first(g):
    return isinstance(g, int) and g == 0


def cols(t, start, size):
    return t[:, bass.ds(start, size)]


def split3(ap, n):
    return ap.rearrange("p (a b) -> p a b", a=n)


def program(nc, x, src, dst, w, attr, W, b, W1, b1, W2, b2, W_ih, b_ih, W_hh, b_hh, out, places, table, moved, a_dram, x1_dram):
    with ExitStack() as ctx:
        def sb(name, shape, dt):
            return ctx.enter_context(nc.sbuf_tensor(name, shape, dt))

        lane_row = sb("lane_row", [P, P], BF16)
        node_id = sb("node_id", [P, NW], F32)
        window_base = sb("window_base", [P, NW], F32)
        ident = sb("ident", [P, P], F32)
        before = sb("before", [P, P], F32)
        before_bf = sb("before_bf", [P, P], BF16)
        upto_bf = sb("upto_bf", [P, P], BF16)
        ones_bf = sb("ones_bf", [P, P], BF16)
        ones = sb("ones", [P, P], F32)
        eps = sb("eps", [P, 1], F32)
        zero_bf = sb("zero_bf", [P, 512], BF16)
        src_cols = sb("src_cols", [P, 2, TILES], BF16)
        edge_cols = sb("edge_cols", [P, 2, TILES], F32)
        src_hi, src_lo = src_cols[:, 0, :], src_cols[:, 1, :]
        weight, dst_f = edge_cols[:, 0, :], edge_cols[:, 1, :]
        step_tab = sb("step_tab", [1, NG + 1], I32)
        q_tab = sb("q_tab", [1, P * QP + 1], I32)
        dinv = sb("dinv", [P, NW], F32)
        start_row = sb("start_row", [P, NW], F32)
        tables = sb("tables", [P, NW * 3 * HD], BF16)
        sums = sb("sums", [P, NW, HD + 1], F32)
        W_T = sb("W_T", [D, D], F32)
        W1_T = sb("W1_T", [D, 2 * HD], F32)
        c_row = sb("c_row", [1, HD], F32)
        W2_T = sb("W2_T", [HD, D], F32)
        Wih_T = sb("Wih_T", [D, 3 * D], F32)
        Whh_T = sb("Whh_T", [D, 3 * D], F32)
        b_b = sb("b_b", [P, D], F32)
        b1_b = sb("b1_b", [P, HD], F32)
        b2_b = sb("b2_b", [P, D], F32)
        bih_b = sb("bih_b", [P, 3 * D], F32)
        bhh_b = sb("bhh_b", [P, 3 * D], F32)

        flat = sums[:, :, :].rearrange("p a b -> p (a b)")
        acc = flat[:, 0:NW * D]
        xs = flat[:, NW * D:2 * NW * D].rearrange("p (a b) -> p a b", b=D)

        constants(nc, lane_row, node_id, window_base, ident, before, before_bf, upto_bf, ones_bf, ones, eps, zero_bf)
        weights(nc, ident, W, W1, W2, W_ih, W_hh, b, b1, b2, b_ih, b_hh, W_T, W1_T, c_row, W2_T, Wih_T, Whh_T,
                b_b, b1_b, b2_b, bih_b, bhh_b)
        edge_columns(nc, src, dst, w, ident, src_cols, edge_cols)
        steps_table(nc, dst, before, table, sums, step_tab, q_tab)
        counts(nc, lane_row, ones, ones_bf, before, src_hi, src_lo, weight, moved, places, sums, dinv, start_row, q_tab)
        scaled_nodes(nc, x, xs, dinv, tables, acc)
        move_rows(nc, dst, lane_row, node_id, before_bf, upto_bf, ones_bf, ones, zero_bf, src_hi, src_lo, weight,
                  step_tab, start_row, tables, moved)
        sum_moved(nc, lane_row, q_tab, moved, acc)
        nodes(nc, ident, eps, xs, dinv, acc, W_T, b_b, W1_T, b1_b, tables, a_dram, x1_dram)
        messages(nc, dst, attr, lane_row, node_id, window_base, ones_bf, src_hi, src_lo, weight, dst_f, c_row, step_tab, tables, sums, a_dram)
        update(nc, ident, eps, x1_dram, sums, W2_T, b2_b, Wih_T, bih_b, Whh_T, bhh_b, out)


def constants(nc, lane_row, node_id, window_base, ident, before, before_bf, upto_bf, ones_bf, ones, eps, zero_bf):
    with ExitStack() as ctx:
        row_i = ctx.enter_context(nc.sbuf_tensor("row_i", [P, P], I32))
        node_i = ctx.enter_context(nc.sbuf_tensor("node_i", [P, NW], I32))
        base_i = ctx.enter_context(nc.sbuf_tensor("base_i", [P, NW], I32))
        made = ctx.enter_context(nc.semaphore("iotas_made"))
        lanes = ctx.enter_context(nc.semaphore("lanes_made"))
        block = ctx.enter_context(nc.Block())

        @block.gpsimd
        def _(pool):
            pool.iota(row_i[:, :], [[1, P]], base=0, channel_multiplier=0)
            pool.iota(node_i[:, :], [[P, NW]], base=0, channel_multiplier=1)
            pool.iota(base_i[:, :], [[P, NW]], base=0, channel_multiplier=0).then_inc(made, 1)

        @block.vector
        def _(dve):
            dve.memset(ones[:, :], 1.0)
            dve.memset(ones_bf[:, :], 1.0)
            dve.memset(eps[:, :], EPS)
            dve.memset(zero_bf[:, :], 0.0)
            dve.wait_ge(made, 1)
            dve.tensor_copy(lane_row[:, :], row_i[:, :]).then_inc(lanes, 1)
            dve.tensor_copy(window_base[:, :], base_i[:, :]).then_inc(lanes, 1)
            dve.tensor_copy(node_id[:, :], node_i[:, :]).then_inc(lanes, 1)
            dve.wait_ge(lanes, 3)
            lane = node_id[:, 0:1]
            dve.tensor_scalar(ident[:, :], lane_row[:, :], lane, None, ALU.is_equal)
            dve.tensor_scalar(before[:, :], lane_row[:, :], lane, None, ALU.is_gt)
            dve.tensor_scalar(before_bf[:, :], lane_row[:, :], lane, None, ALU.is_gt)
            dve.tensor_scalar(upto_bf[:, :], lane_row[:, :], lane, None, ALU.is_le)


def weights(nc, ident, W, W1, W2, W_ih, W_hh, b, b1, b2, b_ih, b_hh, W_T, W1_T, c_row, W2_T, Wih_T, Whh_T,
            b_b, b1_b, b2_b, bih_b, bhh_b):
    with ExitStack() as ctx:
        def sb(name, shape):
            return ctx.enter_context(nc.sbuf_tensor(name, shape, F32))

        W_s, W1_s, W2_s = sb("W_s", [D, D]), sb("W1_s", [HD, 2 * D + 1]), sb("W2_s", [D, HD])
        ih_s, hh_s = sb("ih_s", [D, 3, D]), sb("hh_s", [D, 3, D])
        ps = ctx.enter_context(nc.psum_tensor("ps_weights", [P, 4, 512], F32))
        loaded = ctx.enter_context(nc.semaphore("weights_loaded"))
        turned = ctx.enter_context(nc.semaphore("weights_turned"))
        block = ctx.enter_context(nc.Block())
        loads = [(W_s[:, :], W), (W1_s[:, :], W1), (W2_s[:, :], W2),
                 (ih_s[:, :, :], W_ih.rearrange("(a r) c -> r a c", a=3)),
                 (hh_s[:, :, :], W_hh.rearrange("(a r) c -> r a c", a=3))]
        loads += [(t[:, :], v.unsqueeze(0).to_broadcast([P, v.shape[0]]))
                  for t, v in ((b_b, b), (b1_b, b1), (b2_b, b2), (bih_b, b_ih), (bhh_b, b_hh))]

        @block.sync
        def _(sp):
            for dest, source in loads:
                sp.dma_start(dest, source).then_inc(loaded, 16)
            sp.wait_ge(loaded, 16 * len(loads))

        @block.tensor
        def _(pe):
            pe.wait_ge(loaded, 16 * len(loads))
            pe.transpose(ps[0:D, 0, 0:D], W_s[:, :], ident[0:D, 0:D])
            pe.transpose(ps[0:D, 1, 0:HD], W1_s[:, 0:D], ident[:, :])
            pe.transpose(ps[0:D, 1, HD:2 * HD], W1_s[:, D:2 * D], ident[:, :])
            pe.transpose(ps[:, 0, 256:256 + D], W2_s[:, :], ident[0:D, 0:D])
            pe.matmul(ps[0:1, 0, 384:512], W1_s[:, 2 * D:2 * D + 1], ident[:, :], start=True, stop=True)
            for i in range(3):
                pe.transpose(ps[0:D, 2, i * D:(i + 1) * D], ih_s[:, i, :], ident[0:D, 0:D])
                last = pe.transpose(ps[0:D, 3, i * D:(i + 1) * D], hh_s[:, i, :], ident[0:D, 0:D])
            last.then_inc(turned, 1)

        @block.vector
        def _(dve):
            dve.wait_ge(turned, 1)
            dve.tensor_copy(W_T[:, :], ps[0:D, 0, 0:D])
            dve.tensor_copy(W1_T[:, :], ps[0:D, 1, 0:2 * HD])
            dve.tensor_copy(W2_T[:, :], ps[:, 0, 256:256 + D])
            dve.tensor_copy(c_row[:, :], ps[0:1, 0, 384:512])
            dve.tensor_copy(Wih_T[:, :], ps[0:D, 2, 0:3 * D])
            dve.tensor_copy(Whh_T[:, :], ps[0:D, 3, 0:3 * D])


def edge_columns(nc, src, dst, w, ident, src_cols, edge_cols):
    with ExitStack() as ctx:
        raw = ctx.enter_context(nc.sbuf_tensor("edge_raw", [BT, 2, 3, P], I32))
        part = ctx.enter_context(nc.sbuf_tensor("edge_part", [BT, 2, 2, P], I32))
        rows = ctx.enter_context(nc.sbuf_tensor("edge_rows", [BT, 2, NCOL, P], F32))
        ps = ctx.enter_context(nc.psum_tensor("ps_cols", [P, 2, 512], F32))
        raw_in = [ctx.enter_context(nc.semaphore(f"raw_in{s}")) for s in range(2)]
        parted = ctx.enter_context(nc.semaphore("parts_made"))
        rows_made = ctx.enter_context(nc.semaphore("rows_made"))
        turned = ctx.enter_context(nc.semaphore("cols_turned"))
        copied = ctx.enter_context(nc.semaphore("cols_copied"))
        block = ctx.enter_context(nc.Block())
        views = [v.rearrange("(t p) -> t p", p=P) for v in (src, dst, w)]

        @block.sync
        def _(sp):
            def load(i, s, use):
                wait(sp, rows_made, i - 1)
                for a, v in enumerate(views):
                    d = raw[:, s, a, :] if a < 2 else raw[:, s, a, :].bitcast(F32)
                    sp.dma_start(d, v[bass.ds(i * BT, BT), :]).then_inc(raw_in[s], 16)
            over_pairs(sp, NB, load)

        @block.vector
        def _(dve):
            def make(i, s, use):
                dve.wait_ge(raw_in[s], use * 48 + 48)
                wait(dve, turned, i - 1)
                dve.tensor_scalar(part[:, s, 0, :], raw[:, s, 0, :], 7, None, ALU.logical_shift_right).then_inc(parted, 1)
                dve.tensor_scalar(part[:, s, 1, :], raw[:, s, 0, :], P - 1, None, ALU.bitwise_and).then_inc(parted, 1)
                dve.tensor_copy(rows[:, s, 2, :], raw[:, s, 2, :].bitcast(F32))
                dve.tensor_copy(rows[:, s, 3, :], raw[:, s, 1, :])
                dve.wait_ge(parted, i * 2 + 2)
                dve.tensor_copy(rows[:, s, 0:2, :], part[:, s, :, :]).then_inc(rows_made, 1)
            over_pairs(dve, NB, make)

        @block.tensor
        def _(pe):
            def turn(i, s, use):
                pe.wait_ge(rows_made, i + 1)
                wait(pe, copied, i - 1)
                for a in range(NCOL):
                    last = pe.transpose(ps[:, s, a * BT:(a + 1) * BT], rows[:, s, a, :], ident[0:BT, 0:BT])
                last.then_inc(turned, 1)
            over_pairs(pe, NB, turn)

        @block.scalar
        def _(act):
            def copy(i, s, use):
                act.wait_ge(turned, i + 1)
                act.activation(src_cols[:, :, bass.ds(i * BT, BT)], split3(ps[:, s, 0:2 * BT], 2), ACT.Copy)
                act.activation(edge_cols[:, :, bass.ds(i * BT, BT)], split3(ps[:, s, 2 * BT:4 * BT], 2), ACT.Copy).then_inc(copied, 1)
            over_pairs(act, NB, copy)


def steps_table(nc, dst, before, table, sums, step_tab, q_tab):
    R = NG // G
    with ExitStack() as ctx:
        def sb(name, shape, dt):
            return ctx.enter_context(nc.sbuf_tensor(name, shape, dt))

        ids = sums[:, :, :].rearrange("p a b -> p (a b)")[0:R, 0:G * GE].bitcast(I32)
        ends = sb("ends", [R, 2, G], I32)
        wins = sb("wins", [R, 2, G], I32)
        win_f = sb("win_f", [R, 2, G], F32)
        width = sb("width", [R, G + 1], F32)
        first = sb("first", [R, G + 1], F32)
        last_f = sb("last_f", [R, G], F32)
        tab_i = sb("tab_i", [R, 4, G], I32)
        packed = sb("packed", [R, G], I32)
        ps = ctx.enter_context(nc.psum_tensor("ps_steps", [P, 512], F32))
        ids_in = ctx.enter_context(nc.semaphore("ids_in"))
        chain = ctx.enter_context(nc.semaphore("steps_chain"))
        widths = ctx.enter_context(nc.semaphore("widths_made"))
        summed = ctx.enter_context(nc.semaphore("widths_summed"))
        made = ctx.enter_context(nc.semaphore("steps_made"))
        kept = ctx.enter_context(nc.semaphore("steps_kept"))
        back = ctx.enter_context(nc.semaphore("steps_back"))
        block = ctx.enter_context(nc.Block())

        @block.sync
        def _(sp):
            sp.dma_start(ids, dst.rearrange("(p e) -> p e", p=R)).then_inc(ids_in, 16)
            sp.wait_ge(made, 1)
            sp.dma_start(table.rearrange("(p e) -> p e", p=R), packed[:, :]).then_inc(kept, 16)
            sp.wait_ge(kept, 16)
            sp.dma_start(step_tab[:, 1:NG + 1], table.unsqueeze(0)).then_inc(back, 16)
            sp.wait_ge(back, 16)

        @block.tensor
        def _(pe):
            pe.wait_ge(widths, 1)
            pe.matmul(ps[0:R, 0:1], before[0:R, 0:R], width[:, G:G + 1], start=True, stop=True).then_inc(summed, 1)

        @block.vector
        def _(dve):
            n = 0

            def then(instruction):
                nonlocal n
                n += 1
                instruction.then_inc(chain, 1)
                dve.wait_ge(chain, n)

            dve.memset(step_tab[:, 0:1], 0)
            dve.memset(q_tab[:, 0:1], 0)
            dve.wait_ge(ids_in, 16)
            dve.tensor_reduce(ends[:, 0, :], split3(ids, G), AX_X, ALU.min)
            then(dve.tensor_reduce(ends[:, 1, :], split3(ids, G), AX_X, ALU.max))
            then(dve.tensor_scalar(wins[:, :, :], ends[:, :, :], 7, None, ALU.logical_shift_right))
            then(dve.tensor_copy(win_f[:, :, :], wins[:, :, :]))
            then(dve.scalar_tensor_tensor(width[:, 0:G], win_f[:, 1, :], 1.0, win_f[:, 0, :], ALU.add, ALU.subtract))
            dve.tensor_reduce(width[:, G:G + 1], width[:, 0:G], AX_X, ALU.add).then_inc(widths, 1)
            dve.wait_ge(summed, 1)
            then(dve.tensor_copy(first[:, 0:1], ps[0:R, 0:1]))
            for j in range(G):
                then(dve.tensor_tensor(first[:, j + 1:j + 2], first[:, j:j + 1], width[:, j:j + 1], ALU.add))
            then(dve.tensor_scalar(last_f[:, :], width[:, 0:G], -1.0, None, ALU.add))
            dve.tensor_copy(tab_i[:, 0, :], first[:, 0:G])
            then(dve.tensor_copy(tab_i[:, 1, :], last_f[:, :]))
            dve.tensor_scalar(tab_i[:, 2, :], wins[:, 0, :], 16, None, ALU.logical_shift_left)
            then(dve.tensor_scalar(tab_i[:, 3, :], tab_i[:, 1, :], 23, None, ALU.logical_shift_left))
            then(dve.tensor_tensor(tab_i[:, 0, :], tab_i[:, 0, :], tab_i[:, 2, :], ALU.bitwise_or))
            dve.tensor_tensor(packed[:, :], tab_i[:, 0, :], tab_i[:, 3, :], ALU.bitwise_or).then_inc(made, 1)


def counts(nc, lane_row, ones, ones_bf, before, src_hi, src_lo, weight, moved, places, sums, dinv, start_row, q_tab):
    ZG = 4
    with ExitStack() as ctx:
        def sb(name, shape, dt):
            return ctx.enter_context(nc.sbuf_tensor(name, shape, dt))

        def sem(name):
            return ctx.enter_context(nc.semaphore(name))

        lo_hot = sb("lo_hot", [P, 2, G, P], F32)
        hi_hot = sb("hi_hot", [P, 2, G, 2, NW], F32)
        ps = ctx.enter_context(nc.psum_tensor("ps_counts", [P, 2, NW], F32))
        ps_sum = ctx.enter_context(nc.psum_tensor("ps_sum", [P, 512], F32))
        zeros = sums[:, :, :].rearrange("p a b -> p (a b)")[:, 0:ZG * G * ROW]
        deg, live, safe, root = (sb(n, [P, NW], F32) for n in ("deg", "live", "safe", "root"))
        per_lane = sb("per_lane", [P, NW], F32)
        total = sb("total", [NW, 1], F32)
        groups = sb("groups", [NW, 1], F32)
        steps_i = sb("steps_i", [NW, NG + 1], I32)
        full = sb("full", [NW, NG + 1], F32)
        padded = sb("padded", [NW, 1], F32)
        padded_b = sb("padded_b", [NW, P], F32)
        q_i = sb("q_i", [P, QP], I32)
        q_f = sb("q_f", [P, QP], F32)
        q_le = sb("q_le", [P, QP, NW], F32)
        q_win = sb("q_win", [P, QP], F32)
        q_out = sb("q_out", [P, QP], I32)
        zeroed, zero_done = sem("zeros_made"), sem("zero_done")
        hot_made, weighted, used = sem("hot_made"), sem("hot_weighted"), sem("hot_used")
        chain, lane_counts, win_counts = sem("count_chain"), sem("lane_counts"), sem("window_counts")
        pads_made, starts_made = sem("pads_made"), sem("starts_made")
        guarded, rooted = sem("degree_guarded"), sem("degree_rooted")
        q_ready, q_made, q_kept, q_back = sem("q_ready"), sem("q_made"), sem("q_kept"), sem("q_back")
        block = ctx.enter_context(nc.Block())

        @block.sync
        def _(sp):
            sp.wait_ge(zeroed, 1)
            with sp.Fori(0, NQ // ZG) as i:
                sp.dma_start(moved[bass.ds(i * (ZG * GE), ZG * GE), :].rearrange("(p r) c -> p (r c)", p=P),
                             zeros).then_inc(zero_done, 16)
            for i in range(NQ // ZG * ZG, NQ):
                sp.dma_start(moved[i * GE:(i + 1) * GE, :].rearrange("(p r) c -> p (r c)", p=P),
                             zeros[:, 0:G * ROW]).then_inc(zero_done, 16)
            sp.wait_ge(q_made, 1)
            sp.dma_start(places.rearrange("(p e) -> p e", p=P), q_out[:, :]).then_inc(q_kept, 16)
            sp.wait_ge(q_kept, 16)
            sp.dma_start(q_tab[:, 1:], places.unsqueeze(0)).then_inc(q_back, 16)
            sp.wait_ge(q_back, 16)
            sp.wait_ge(zero_done, 16 * (NQ // ZG + NQ % ZG))

        @block.gpsimd
        def _(pool):
            pool.memset(zeros, 0.0).then_inc(zeroed, 1)
            pool.iota(q_i[:, :], [[GE, QP]], base=0, channel_multiplier=GE * QP).then_inc(q_ready, 1)
            pool.iota(steps_i[:, :], [[GE, NG + 1]], base=GE, channel_multiplier=0).then_inc(q_ready, 1)

            def body(g, s, use):
                pool.wait_ge(hot_made, g + 1)
                pool.tensor_tensor(hi_hot[:, s, :, 0, :], hi_hot[:, s, :, 1, :],
                                   cols(weight, g * G, G).unsqueeze(2).to_broadcast([P, G, NW]), ALU.mult).then_inc(weighted, 1)
            over_pairs(pool, NG, body)

        @block.vector
        def _(dve):
            def body(g, s, use):
                wait(dve, used, g - 1)
                dve.tensor_tensor(hi_hot[:, s, :, 1, :], lane_row[:, 0:NW].unsqueeze(1).to_broadcast([P, G, NW]),
                                  cols(src_hi, g * G, G).unsqueeze(2).to_broadcast([P, G, NW]), ALU.is_equal).then_inc(hot_made, 1)
                dve.tensor_tensor(lo_hot[:, s, :, :], lane_row[:, :].unsqueeze(1).to_broadcast([P, G, P]),
                                  cols(src_lo, g * G, G).unsqueeze(2).to_broadcast([P, G, P]), ALU.is_equal).then_inc(chain, 1)
            over_pairs(dve, NG, body)
            n = NG

            def then(instruction):
                nonlocal n
                n += 1
                instruction.then_inc(chain, 1)
                dve.wait_ge(chain, n)

            dve.wait_ge(used, NG)
            dve.tensor_copy(per_lane[:, :], ps[:, 1, :]).then_inc(lane_counts, 1)
            then(dve.tensor_scalar(deg[:, :], ps[:, 0, :], 1.0, None, ALU.add))
            then(dve.tensor_scalar(live[:, :], deg[:, :], 0.0, None, ALU.is_gt))
            then(dve.tensor_tensor(safe[:, :], deg[:, :], live[:, :], ALU.mult))
            then(dve.scalar_tensor_tensor(root[:, :], live[:, :], -1.0, safe[:, :], ALU.mult, ALU.add))
            then(dve.tensor_scalar(safe[:, :], root[:, :], 1.0, None, ALU.add))
            dve.engine_nop().then_inc(guarded, 1)
            dve.wait_ge(rooted, 1)
            then(dve.reciprocal(safe[:, :], root[:, :]))
            then(dve.tensor_tensor(dinv[:, :], safe[:, :], live[:, :], ALU.mult))
            dve.wait_ge(win_counts, 1)
            dve.wait_ge(q_ready, 2)
            then(dve.tensor_scalar(total[:, :], ps_sum[0:NW, 0:1], float(GE - 1), None, ALU.add))
            then(dve.tensor_scalar(full[:, :], steps_i[:, :], total[:, 0:1], None, ALU.is_le))
            then(dve.tensor_reduce(groups[:, :], full[:, :], AX_X, ALU.add))
            then(dve.tensor_scalar(padded[:, :], groups[:, :], float(GE), None, ALU.mult))
            dve.tensor_copy(padded_b[:, :], padded[:, 0:1].to_broadcast([NW, P])).then_inc(pads_made, 1)
            dve.wait_ge(starts_made, 1)
            dve.tensor_copy(q_f[:, :], q_i[:, :])
            then(dve.tensor_copy(start_row[:, :], ps_sum[:, 128:128 + NW]))
            then(dve.tensor_tensor(q_le[:, :, :], start_row[:, :].unsqueeze(1).to_broadcast([P, QP, NW]),
                                   q_f[:, :].unsqueeze(2).to_broadcast([P, QP, NW]), ALU.is_le))
            then(dve.tensor_reduce(q_win[:, :], q_le[:, :, :], AX_X, ALU.add))
            dve.tensor_scalar(q_out[:, :], q_win[:, :], -1.0, None, ALU.add).then_inc(q_made, 1)

        @block.scalar
        def _(act):
            act.wait_ge(guarded, 1)
            act.activation(root[:, :], safe[:, :], ACT.Sqrt).then_inc(rooted, 1)

        @block.tensor
        def _(pe):
            def body(g, s, use):
                pe.wait_ge(weighted, g + 1)
                pe.wait_ge(chain, g + 1)
                for j in range(G):
                    last = pe.matmul(ps[:, :, :].rearrange("p a b -> p (a b)"), lo_hot[:, s, j, :],
                                     hi_hot[:, s, j, :, :].rearrange("p a b -> p (a b)"),
                                     start=isinstance(g, int) and g == 0 and j == 0,
                                     stop=isinstance(g, int) and g == NG - 1 and j == G - 1, skip_group_check=True)
                last.then_inc(used, 1)
            over_pairs(pe, NG, body)
            pe.wait_ge(lane_counts, 1)
            pe.matmul(ps_sum[0:NW, 0:1], per_lane[:, :], ones[:, 0:1], start=True, stop=True).then_inc(win_counts, 1)
            pe.wait_ge(pads_made, 1)
            pe.matmul(ps_sum[:, 128:128 + NW], padded_b[:, :], before[0:NW, 0:NW], start=True, stop=True).then_inc(starts_made, 1)


def split_bf16(dve, then, value, rest, parts, last_sem):
    then(dve.tensor_copy(parts[0], value))
    then(dve.tensor_tensor(rest, value, parts[0], ALU.subtract))
    then(dve.tensor_copy(parts[1], rest))
    dve.tensor_tensor(parts[2], rest, parts[1], ALU.subtract).then_inc(last_sem, 1)


def scaled_nodes(nc, x, xs, dinv, tables, acc):
    with ExitStack() as ctx:
        y = acc.rearrange("p (a b) -> p a b", b=D)
        rest = tables[:, NW * 3 * D:NW * 5 * D].bitcast(F32).rearrange("p (a b) -> p a b", b=D)
        parts = tables[:, 0:NW * 3 * D].rearrange("p (a k b) -> p a k b", k=3, b=D)
        cleared = ctx.enter_context(nc.semaphore("x_cleared"))
        x_in = ctx.enter_context(nc.semaphore("x_in"))
        chain = ctx.enter_context(nc.semaphore("y_chain"))
        done = ctx.enter_context(nc.semaphore("y_done"))
        block = ctx.enter_context(nc.Block())

        @block.sync
        def _(sp):
            sp.wait_ge(cleared, 1)
            sp.dma_start(xs[:, 0:NW - 1, :], x[0:(NW - 1) * P, :].rearrange("(a p) c -> p a c", p=P)).then_inc(x_in, 16)
            sp.dma_start(xs[0:LAST, NW - 1, :], x[(NW - 1) * P:N, :]).then_inc(x_in, 16)

        @block.vector
        def _(dve):
            n = 0

            def then(instruction):
                nonlocal n
                n += 1
                instruction.then_inc(chain, 1)
                dve.wait_ge(chain, n)

            dve.memset(xs[:, NW - 1, :], 0.0).then_inc(cleared, 1)
            dve.wait_ge(x_in, 32)
            then(dve.tensor_tensor(y, xs[:, :, :], dinv[:, :].unsqueeze(2).to_broadcast([P, NW, D]), ALU.mult))
            split_bf16(dve, then, y, rest, [parts[:, :, k, :] for k in range(3)], done)


def move_rows(nc, dst, lane_row, node_id, before_bf, upto_bf, ones_bf, ones, zero_bf, src_hi, src_lo, weight,
              step_tab, start_row, tables, moved):
    with ExitStack() as ctx:
        def sb(name, shape, dt):
            return ctx.enter_context(nc.sbuf_tensor(name, shape, dt))

        def sem(name):
            return ctx.enter_context(nc.semaphore(name))

        dst_rows = sb("dst_rows", [P, S, GE], I32)
        dst_hot = sb("dst_hot", [P, 2 * GE], BF16)
        hi_hot = sb("place_hot", [P, 2, G, NW], BF16)
        junk = sb("junk", [P, 2, G, NW], F32)
        place_f = sb("place_f", [P, 2, G], F32)
        place = sb("place", [P, S, G], I32)
        rows = sb("rows", [P, S, G, ROW], F32)
        ps_rows = ctx.enter_context(nc.psum_tensor("ps_rows", [P, 2, 512], F32))
        ps_mark = ctx.enter_context(nc.psum_tensor("ps_moved_mark", [P, 512], F32))
        ps_place = ctx.enter_context(nc.psum_tensor("ps_place", [P, G, NW], F32))
        rows_in = [sem(f"dst_rows_in{s}") for s in range(S)]
        scattered = [sem(f"scattered{s}") for s in range(S)]
        hot_made, steps_done = sem("dst_hot_made"), sem("gather_steps_done")
        gathered = sem("gathered")
        hi_made, placed, read = sem("place_hot_made"), sem("placed"), sem("places_read")
        cast, rows_ready = sem("places_cast"), sem("rows_ready")
        parts = tables[:, 0:NW * 3 * D]
        passed = sem("move_rows_passed")
        block = ctx.enter_context(nc.Block())

        @block.sync
        def _(sp):
            def body(g, s, use, _):
                wait(sp, placed, g - (S - 1))
                sp.dma_start(dst_rows[:, s, :], dst[bass.ds(g * GE, GE)].unsqueeze(0).to_broadcast([P, GE])).then_inc(rows_in[s], 16)
            over_groups(sp, NG, body)

        @block.vector
        def _(dve):
            dve_regs = [dve.alloc_register(f"move_dve{i}") for i in range(S + 1)]

            def read_places(g, s, use):
                dve.wait_ge(placed, g + 1)
                h = s % 2
                for j in range(G):
                    last = dve.tensor_tensor_reduce(junk[:, h, j, :], ps_place[:, j, :], hi_hot[:, h, j, :], 1.0, 0.0,
                                                    ALU.mult, ALU.add, place_f[:, h, j:j + 1])
                last.then_inc(read, 1)
                dve.wait_ge(read, g + 1)
                wait(dve, scattered[s], use * (16 * G))
                dve.tensor_copy(place[:, s, :], place_f[:, h, :]).then_inc(cast, 1)

            def body(g, s, use, steps):
                wait_alone(dve, rows_in[s], use * 16 + 16, passed)
                k0, k1, least = steps[s + 1]
                with dve.Fori(k0, k1) as k:
                    dve.wait_ge(steps_done, k + 1)
                    dve.tensor_scalar(cols(dst_hot, (k % 2) * GE, GE), dst_rows[:, s, :],
                                      cols(node_id, window(k - k0 + least), 1), None, ALU.is_equal).then_inc(hot_made, 1)
                if not is_first(g):
                    read_places(*last_of(g, s, use))
                dve.tensor_tensor(hi_hot[:, s % 2, :, :], lane_row[:, 0:NW].unsqueeze(1).to_broadcast([P, G, NW]),
                                  cols(src_hi, g * G, G).unsqueeze(2).to_broadcast([P, G, NW]), ALU.is_equal).then_inc(hi_made, 1)
            over_groups(dve, NG, body, lambda g0, n: load_steps(dve, step_tab, dve_regs, g0, n))
            read_places(NG - 1, (NG - 1) % S, (NG - 1) // S)

        @block.tensor
        def _(pe):
            pe_regs = [pe.alloc_register(f"move_pe{i}") for i in range(S + 1)]
            pe.sem_inc(steps_done, 2)
            pe.matmul(ps_place[:, :, :], ones[0:1, :], start_row[0:1, :].unsqueeze(1).to_broadcast([1, G, NW]),
                      start=True, stop=False, skip_group_check=True)

            def body(g, s, use, steps):
                wait(pe, rows_ready, g - 1)
                h = s % 2
                pe.matmul(ps_rows[:, h, 0:G * D], zero_bf[:, 0:P], zero_bf[:, 0:G * D], start=True, stop=False, skip_group_check=True)
                k0, k1, least = steps[s + 1]
                with pe.Fori(k0, k1) as k:
                    pe.wait_ge(hot_made, k + 1)
                    at = window(k - k0 + least) * (3 * D)
                    for j in range(G):
                        for i in range(3):
                            last = pe.matmul(ps_rows[:, h, j * D:(j + 1) * D], cols(dst_hot, (k % 2) * GE + j * P, P),
                                             cols(parts, at + i * D, D), start=False, stop=False, skip_group_check=True)
                    last.then_inc(steps_done, 1)
                pe.matmul(ps_mark[:, 0:1], ones_bf[:, :], ones_bf[:, 0:1], start=True, stop=True).then_inc(gathered, 1)

                def advance(j0, j1, stationary, hot):
                    return pe.matmul(ps_place[:, j0:j1, :], stationary[:, :], hot, start=False, stop=False, skip_group_check=True)

                if not is_first(g):
                    pe.wait_ge(read, g)
                    advance(0, G, upto_bf, hi_hot[:, 1 - h, :, :])
                    for j in range(1, G):
                        advance(0, j, ones_bf, hi_hot[:, 1 - h, j:j + 1, :].to_broadcast([P, j, NW]))
                pe.wait_ge(hi_made, g + 1)
                for j in range(G - 1):
                    advance(j + 1, G, ones_bf, hi_hot[:, h, j:j + 1, :].to_broadcast([P, G - 1 - j, NW]))
                advance(0, G, before_bf, hi_hot[:, h, :, :]).then_inc(placed, 1)
            over_groups(pe, NG, body, lambda g0, n: load_steps(pe, step_tab, pe_regs, g0, n))

        @block.scalar
        def _(act):
            def body(g, s, use, _):
                act.wait_ge(gathered, g + 1)
                wait(act, scattered[s], use * (16 * G))
                for j in range(G):
                    act.activation(rows[:, s, j, 0:D], ps_rows[:, s % 2, j * D:(j + 1) * D], ACT.Copy, scale=cols(weight, g * G + j, 1))
                act.activation(rows[:, s, :, D], cols(src_lo, g * G, G), ACT.Copy).then_inc(rows_ready, 1)
            over_groups(act, NG, body)

        @block.gpsimd
        def _(pool):
            def body(g, s, use, _):
                pool.wait_ge(cast, g + 1)
                wait_alone(pool, rows_ready, g + 1, passed)
                for j in range(G):
                    pool.indirect_dma_start(out=moved[:, :], out_offset=bass.IndirectOffsetOnAxis(ap=place[:, s, j:j + 1], axis=0),
                                            in_=rows[:, s, j, :], in_offset=None).then_inc(scattered[s], 16)
            over_groups(pool, NG, body)
            for s in range(S):
                pool.wait_ge(scattered[s], 16 * G * ((NG - 1 - s) // S + 1))


def load_steps(eng, step_tab, regs, g0, count):
    eng.load(regs[0:count + 1], step_tab[0:1, bass.ds(g0, count + 1)])
    got = []
    for r in regs[0:count + 1]:
        v = eng.snap(r).with_bounds(min_val=0, max_val=(1 << 30) - 1)
        k0 = eng.snap(v & 0xFFFF)
        least = eng.snap((v >> 16) & 127)
        got.append((k0, eng.snap(k0 + (v >> 23) + 1), least))
    return got


def window(value):
    return value.with_bounds(min_val=0, max_val=NW - 1)


def sum_moved(nc, lane_row, q_tab, moved, acc):
    PT = 2
    with ExitStack() as ctx:
        def sb(name, shape, dt):
            return ctx.enter_context(nc.sbuf_tensor(name, shape, dt))

        def sem(name):
            return ctx.enter_context(nc.semaphore(name))

        rows = sb("moved_rows", [P, S, G, ROW], F32)
        hot = sb("lane_hot", [P, S, G, P], F32)
        ps = ctx.enter_context(nc.psum_tensor("ps_moved", [P, S, 512], F32))
        rows_in = [sem(f"moved_in{s}") for s in range(S)]
        hot_made, pool_made = sem("lane_hot_made"), sem("pool_hot_made")
        summed, added, cleared = sem("rows_summed"), sem("sums_added"), sem("sums_cleared")
        passed = sem("sum_moved_passed")
        block = ctx.enter_context(nc.Block())

        @block.sync
        def _(sp):
            def body(q, s, use, _):
                wait(sp, summed, q - (S - 1))
                sp.dma_start(rows[:, s, :, :].rearrange("p a b -> p (a b)"),
                             moved[bass.ds(q * GE, GE), :].rearrange("(p r) c -> p (r c)", p=P)).then_inc(rows_in[s], 16)
            over_groups(sp, NQ, body)

        @block.gpsimd
        def _(pool):
            def body(q, s, use, _):
                wait(pool, summed, q - (S - 1))
                wait_alone(pool, rows_in[s], use * 16 + 16, passed)
                for j in range(PT):
                    last = pool.tensor_scalar(hot[:, s, j, :], lane_row[:, :], rows[:, s, j, D:D + 1], None, ALU.is_equal)
                last.then_inc(pool_made, 1)
            over_groups(pool, NQ, body)

        @block.vector
        def _(dve):
            regs = [dve.alloc_register(f"sum_dve{i}") for i in range(S + 1)]

            def load(q0, count):
                dve.load(regs[0:count + 1], q_tab[0:1, bass.ds(q0, count + 1)])
                return [dve.snap(x).with_bounds(min_val=0, max_val=NW - 1) for x in regs[0:count + 1]]

            def add(q, s, win):
                dve.wait_ge(summed, q + 1)
                wait(dve, added, q)
                here = cols(acc, win * D, D)
                dve.tensor_tensor(here, here, ps[:, s, 0:D], ALU.add).then_inc(added, 1)

            dve.memset(acc, 0.0).then_inc(cleared, 1)
            dve.wait_ge(cleared, 1)

            def body(q, s, use, wins):
                dve.wait_ge(rows_in[s], use * 16 + 16)
                wait(dve, summed, q - (S - 1))
                dve.tensor_tensor(hot[:, s, PT:, :], lane_row[:, :].unsqueeze(1).to_broadcast([P, G - PT, P]),
                                  rows[:, s, PT:, D:D + 1].to_broadcast([P, G - PT, P]), ALU.is_equal).then_inc(hot_made, 1)
                if not is_first(q):
                    add(q - 1, (s - 1) % S, wins[s])
            over_groups(dve, NQ, body, load)
            add(NQ - 1, (NQ - 1) % S, load(NQ - 1, 1)[1])

        @block.tensor
        def _(pe):
            def body(q, s, use, _):
                pe.wait_ge(hot_made, q + 1)
                pe.wait_ge(pool_made, q + 1)
                wait(pe, added, q - (S - 1))
                for j in range(G):
                    last = pe.matmul(ps[:, s, 0:D], hot[:, s, j, :], rows[:, s, j, 0:D], start=(j == 0), stop=(j == G - 1))
                last.then_inc(summed, 1)
            over_groups(pe, NQ, body)


def nodes(nc, ident, eps, xs, dinv, acc, W_T, b_b, W1_T, b1_b, tables, a_dram, x1_dram):
    with ExitStack() as ctx:
        def sb(name, shape, dt=F32):
            return ctx.enter_context(nc.sbuf_tensor(name, shape, dt))

        def sem(name):
            return ctx.enter_context(nc.semaphore(name))

        agg = sb("agg", [P, UB, D])
        aggT = sb("aggT", [D, UB * P])
        z = sb("z", [P, UB, D])
        stats = sb("stats", [P, UB, 6])
        mv = sb("mv", [P, UB, 2])
        std = sb("std", [P, UB])
        rstd = sb("rstd", [P, UB])
        x_new = sb("x_new", [P, UB, D])
        xT = sb("xT", [D, UB * P])
        a_out = sb("a_out", [P, UB, HD])
        b_f = sb("b_f", [P, UB, HD])
        b_rest = sb("b_rest", [P, UB, HD])
        ps_T = ctx.enter_context(nc.psum_tensor("ps_T", [P, 1024], F32))
        ps_z = ctx.enter_context(nc.psum_tensor("ps_z", [P, UB, D], F32))
        ps_ab = ctx.enter_context(nc.psum_tensor("ps_ab", [P, 8, 2 * HD], F32))
        chain, made, turned, copied = sem("node_chain"), sem("agg_made"), sem("agg_turned"), sem("agg_copied")
        projected, varied, rooted, normed = sem("projected"), sem("variance_made"), sem("variance_rooted"), sem("normed")
        x_turned, x_copied, halves, b_read, b_split = sem("x_turned"), sem("x_copied"), sem("halves_made"), sem("b_read"), sem("b_split")
        a_copied, stored = sem("a_copied"), sem("a_stored")
        passed = sem("nodes_passed")
        block = ctx.enter_context(nc.Block())

        @block.vector
        def _(dve):
            def batch(m, steps):
                n = 0

                def then(instruction):
                    nonlocal n
                    n += 1
                    instruction.then_inc(chain, 1)
                    wait_alone(dve, chain, m * steps + n, passed)

                x_b = xs[:, bass.ds(m * UB, UB), :]
                d_b = cols(dinv, m * UB, UB).unsqueeze(2).to_broadcast([P, UB, D])
                a_b = split3(cols(acc, m * (UB * D), UB * D), UB)
                then(dve.tensor_tensor(z[:, :, :], x_b, d_b, ALU.mult))
                then(dve.tensor_tensor(z[:, :, :], z[:, :, :], a_b, ALU.add))
                dve.tensor_tensor(agg[:, :, :], z[:, :, :], d_b, ALU.mult).then_inc(made, 1)
                dve.wait_ge(projected, m + 1)
                then(dve.tensor_tensor(z[:, :, :], ps_z[:, :, :], b_b[:, :].unsqueeze(1).to_broadcast([P, UB, D]), ALU.add))
                then(dve.tensor_tensor(z[:, :, :], z[:, :, :], x_b, ALU.add))
                for j in range(UB):
                    last = dve.bn_stats(stats[:, j, :], z[:, j, :])
                then(last)
                for j in range(UB):
                    last = dve.bn_aggr(mv[:, j, :], stats[:, j, :])
                last.then_inc(varied, 1)
                dve.wait_ge(rooted, m + 1)
                then(dve.reciprocal(rstd[:, :], std[:, :]))
                then(dve.tensor_tensor(z[:, :, :], z[:, :, :], mv[:, :, 0:1].to_broadcast([P, UB, D]), ALU.subtract))
                dve.tensor_tensor(x_new[:, :, :], z[:, :, :], rstd[:, :].unsqueeze(2).to_broadcast([P, UB, D]), ALU.mult).then_inc(normed, 1)
                dve.wait_ge(halves, m + 1)
                dve.tensor_tensor(b_f[:, :, :], ps_ab[:, 0:UB, HD:], b1_b[:, :].unsqueeze(1).to_broadcast([P, UB, HD]), ALU.add).then_inc(b_read, 1)
                dve.wait_ge(b_read, m + 1)
                b_parts = cols(tables, m * (UB * 3 * HD), UB * 3 * HD).rearrange("p (a k b) -> p a k b", k=3, b=HD)
                split_bf16(dve, then, b_f[:, :, :], b_rest[:, :, :], [b_parts[:, :, i, :] for i in range(3)], b_split)
                dve.wait_ge(b_split, m + 1)
                dve.wait_ge(stored, m * 32 + 32)
                assert n == steps, n

            with dve.Fori(0, NU) as m:
                batch(m, 10)

        @block.scalar
        def _(act):
            with act.Fori(0, NU) as m:
                act.wait_ge(turned, m + 1)
                act.activation(aggT[:, :], ps_T[0:D, 0:UB * P], ACT.Copy).then_inc(copied, 1)
                act.wait_ge(varied, m + 1)
                act.activation(std[:, :], mv[:, :, 1], ACT.Sqrt, bias=eps[:, 0:1]).then_inc(rooted, 1)
                act.wait_ge(x_turned, m + 1)
                act.activation(xT[:, :], ps_T[0:D, 0:UB * P], ACT.Copy).then_inc(x_copied, 1)
                act.wait_ge(b_read, m + 1)
                act.activation(a_out[:, :, :], ps_ab[:, 0:UB, 0:HD], ACT.Copy).then_inc(a_copied, 1)
                act.wait_ge(normed, m + 1)
                act.dma_start(x1_dram[bass.ds(m * (UB * P), UB * P), :].rearrange("(a p) c -> p a c", p=P),
                              x_new[:, :, :]).then_inc(stored, 16)
                act.wait_ge(a_copied, m + 1)
                act.dma_start(a_dram[bass.ds(m * (UB * P), UB * P), :].rearrange("(a p) c -> p a c", p=P),
                              a_out[:, :, :]).then_inc(stored, 16)
                act.wait_ge(stored, m * 32 + 32)

        @block.tensor
        def _(pe):
            with pe.Fori(0, NU) as m:
                wait_alone(pe, made, m + 1, passed)
                for j in range(UB):
                    last = pe.transpose(ps_T[0:D, j * P:(j + 1) * P], agg[:, j, :], ident[:, :])
                last.then_inc(turned, 1)
                pe.wait_ge(copied, m + 1)
                for j in range(UB):
                    last = pe.matmul(ps_z[:, j, :], aggT[:, j * P:(j + 1) * P], W_T[:, :], start=True, stop=True)
                last.then_inc(projected, 1)
                wait_alone(pe, normed, m + 1, passed)
                for j in range(UB):
                    last = pe.transpose(ps_T[0:D, j * P:(j + 1) * P], x_new[:, j, :], ident[:, :])
                last.then_inc(x_turned, 1)
                pe.wait_ge(x_copied, m + 1)
                for j in range(UB):
                    last = pe.matmul(ps_ab[:, j, :], xT[:, j * P:(j + 1) * P], W1_T[:, :], start=True, stop=True)
                last.then_inc(halves, 1)


def messages(nc, dst, attr, lane_row, node_id, window_base, ones_bf, src_hi, src_lo, src_f, dst_f, c_row, step_tab, tables, sums, a_dram):
    with ExitStack() as ctx:
        def sb(name, shape, dt):
            return ctx.enter_context(nc.sbuf_tensor(name, shape, dt))

        def sem(name):
            return ctx.enter_context(nc.semaphore(name))

        dst_rows = sb("m_dst_rows", [P, 2, GE], I32)
        attr_row = sb("attr_row", [1, 2, GE], F32)
        dst_hot = sb("m_dst_hot", [P, 2 * GE], BF16)
        node_hot = sb("node_hot", [P, G, P], F32)
        src_i = sb("src_i", [P, S, G], I32)
        a_rows = sb("a_rows", [P, S, G, HD], F32)
        hidden = sb("hidden", [P, 2, G, HD + 1], F32)
        ps_pre = ctx.enter_context(nc.psum_tensor("ps_pre", [P, 2, 1024], F32))
        ps_sum = ctx.enter_context(nc.psum_tensor("ps_msum", [P, 512], F32))
        ps_mark = ctx.enter_context(nc.psum_tensor("ps_mark", [P, 512], F32))
        rows_in = [sem(f"edge_rows_in{s}") for s in range(S)]
        a_in = [sem(f"a_rows_in{s}") for s in range(S)]
        cleared, indexed, index_f = sem("m_cleared"), sem("indexed"), sem("index_f")
        hot_made, steps_done, gathered = sem("m_dst_hot_made"), sem("m_steps_done"), sem("m_gathered")
        added, relued = sem("pre_added"), sem("relued")
        node_hot_made, summed, kept = sem("node_hot_made"), sem("window_summed"), sem("window_kept")
        passed = sem("messages_passed")
        block = ctx.enter_context(nc.Block())

        @block.sync
        def _(sp):
            def body(g, s, use, _):
                wait(sp, gathered, g - 1)
                h = s % 2
                sp.dma_start(dst_rows[:, h, :], dst[bass.ds(g * GE, GE)].unsqueeze(0).to_broadcast([P, GE])).then_inc(rows_in[s], 16)
                sp.dma_start(attr_row[:, h, :], attr[bass.ds(g * GE, GE), :].rearrange("e c -> c e")).then_inc(rows_in[s], 16)
            over_groups(sp, NG, body)

        @block.gpsimd
        def _(pool):
            def body(g, s, use, _):
                wait(pool, added, g - (S - 1))
                wait_alone(pool, indexed, g + 1, passed)
                for j in range(G):
                    pool.indirect_dma_start(out=a_rows[:, s, j, :], out_offset=None, in_=a_dram[:, :],
                                            in_offset=bass.IndirectOffsetOnAxis(ap=src_i[:, s, j:j + 1], axis=0)).then_inc(a_in[s], 16)
            over_groups(pool, NG, body)

        @block.vector
        def _(dve):
            regs = [dve.alloc_register(f"msg_dve{i}") for i in range(S + 1)]

            def sum_windows(g, h, steps):
                k0, k1, least = steps
                with dve.Fori(k0, k1) as k:
                    at = window(k - k0 + least)
                    for j in range(G):
                        last = dve.tensor_scalar(node_hot[:, j, :], lane_row[:, :], cols(window_base, at, 1), cols(dst_f, g * G + j, 1),
                                                 ALU.add, ALU.is_equal)
                    last.then_inc(node_hot_made, 1)
                    dve.wait_ge(summed, k + 1)
                    dve.wait_ge(kept, k + 1)
                    here = sums[:, bass.ds(at, 1), :].rearrange("p a b -> p (a b)")
                    dve.tensor_tensor(here, here, ps_sum[:, 0:HD + 1], ALU.add).then_inc(kept, 1)

            def message_windows(g, s, use, steps):
                dve.wait_ge(a_in[s], use * (16 * G) + 16 * G)
                dve.wait_ge(gathered, g + 1)
                dve.tensor_tensor(hidden[:, s % 2, :, 0:HD], split3(ps_pre[:, s % 2, 0:G * HD], G), a_rows[:, s, :, :],
                                  ALU.add).then_inc(added, 1)
                sum_windows(g, s % 2, steps)

            dve.scalar_tensor_tensor(src_f, src_hi, float(P), src_lo, ALU.mult, ALU.add).then_inc(index_f, 1)
            dve.memset(sums[:, :, :], 0.0).then_inc(kept, 1)
            dve.memset(hidden[:, :, :, HD], 1.0).then_inc(cleared, 1)

            def body(g, s, use, steps):
                wait_alone(dve, rows_in[s], use * 32 + 32, passed)
                k0, k1, least = steps[s + 1]
                with dve.Fori(k0, k1) as k:
                    dve.wait_ge(steps_done, k + 1)
                    dve.tensor_scalar(cols(dst_hot, (k % 2) * GE, GE), dst_rows[:, s % 2, :],
                                      cols(node_id, window(k - k0 + least), 1), None, ALU.is_equal).then_inc(hot_made, 1)
                if not is_first(g):
                    message_windows(*last_of(g, s, use), steps[s])
            over_groups(dve, NG, body, lambda g0, n: load_steps(dve, step_tab, regs, g0, n))
            message_windows(NG - 1, (NG - 1) % S, (NG - 1) // S, load_steps(dve, step_tab, regs, NG - 1, 1)[1])

        @block.scalar
        def _(act):
            def index(g, s, use):
                wait(act, a_in[s], use * (16 * G))
                act.activation(src_i[:, s, :], cols(src_f, g * G, G), ACT.Copy).then_inc(indexed, 1)

            act.wait_ge(index_f, 1)
            index(0, 0, 0)

            def body(g, s, use, _):
                if not isinstance(g, int) or g + 1 < NG:
                    index(g + 1, (s + 1) % S, use if s + 1 < S else use + 1)
                act.wait_ge(added, g + 1)
                act.activation(hidden[:, s % 2, :, 0:HD], hidden[:, s % 2, :, 0:HD], ACT.Relu).then_inc(relued, 1)
            over_groups(act, NG, body)

        @block.tensor
        def _(pe):
            regs = [pe.alloc_register(f"msg_pe{i}") for i in range(S + 1)]

            def sum_windows(g, h, steps):
                k0, k1, _ = steps
                wait_alone(pe, relued, g + 1, passed)
                with pe.Fori(k0, k1) as k:
                    pe.wait_ge(node_hot_made, k + 1)
                    for j in range(G):
                        last = pe.matmul(ps_sum[:, 0:HD + 1], node_hot[:, j, :], hidden[:, h, j, :], start=(j == 0), stop=(j == G - 1))
                    last.then_inc(summed, 1)

            pe.sem_inc(steps_done, 2)
            pe.wait_ge(cleared, 1)

            def body(g, s, use, steps):
                h = s % 2
                wait(pe, added, g - 1)
                pe.wait_ge(rows_in[s], use * 32 + 32)
                for j in range(G):
                    pe.matmul(ps_pre[:, h, j * HD:(j + 1) * HD], attr_row[:, h, j * P:(j + 1) * P], c_row[:, :],
                              start=j in (0, 4), stop=False, skip_group_check=True)
                k0, k1, least = steps[s + 1]
                with pe.Fori(k0, k1) as k:
                    pe.wait_ge(hot_made, k + 1)
                    at = window(k - k0 + least) * (3 * HD)
                    for j in range(G):
                        for i in range(3):
                            last = pe.matmul(ps_pre[:, h, j * HD:(j + 1) * HD], cols(dst_hot, (k % 2) * GE + j * P, P),
                                             cols(tables, at + i * HD, HD), start=False, stop=False, skip_group_check=True)
                    last.then_inc(steps_done, 1)
                pe.matmul(ps_mark[:, 0:1], ones_bf[:, :], ones_bf[:, 0:1], start=True, stop=True).then_inc(gathered, 1)
                if not is_first(g):
                    sum_windows(g - 1, 1 - h, steps[s])
            over_groups(pe, NG, body, lambda g0, n: load_steps(pe, step_tab, regs, g0, n))
            sum_windows(NG - 1, (NG - 1) % 2, load_steps(pe, step_tab, regs, NG - 1, 1)[1])


def update(nc, ident, eps, x1_dram, sums, W2_T, b2_b, Wih_T, bih_b, Whh_T, bhh_b, out):
    UG = 2
    NS = NW // UG
    with ExitStack() as ctx:
        def sb(name, shape, dt=F32):
            return ctx.enter_context(nc.sbuf_tensor(name, shape, dt))

        def sem(name):
            return ctx.enter_context(nc.semaphore(name))

        hx = sb("hx", [P, UG, HD + 1])
        xws = sb("xw", [P, 2, UG, D])
        hT = sb("hT", [P, UG * P])
        xT = sb("u_xT", [D, UG * P])
        agT = sb("agT", [D, UG * P])
        ag = sb("ag", [P, UG, D])
        cb2 = sb("cb2", [P, UG, D])
        gi, gh = sb("gi", [P, UG, 3 * D]), sb("gh", [P, UG, 3 * D])
        pre_rz, rz = sb("pre_rz", [P, UG, 2 * D]), sb("rz", [P, UG, 2 * D])
        t1, t2, nn = sb("t1", [P, UG, D]), sb("t2", [P, UG, D]), sb("nn", [P, UG, D])
        t3, t4, z1, z2 = (sb(n, [P, UG, D]) for n in ("t3", "t4", "z1", "z2"))
        stats, mv = sb("u_stats", [P, UG, 6]), sb("u_mv", [P, UG, 2])
        rstd, var, power = sb("u_rstd", [P, UG]), sb("u_var", [P, UG]), sb("power", [P, UG])
        res = sb("res", [P, 2, UG, D])
        ps_hT = ctx.enter_context(nc.psum_tensor("ps_hT", [P, 512], F32))
        ps_xT = ctx.enter_context(nc.psum_tensor("ps_xT", [P, 512], F32))
        ps_ag = ctx.enter_context(nc.psum_tensor("ps_ag", [P, UG, D], F32))
        ps_agT = ctx.enter_context(nc.psum_tensor("ps_agT", [P, 512], F32))
        ps_gi = ctx.enter_context(nc.psum_tensor("ps_gi", [P, UG, 256], F32))
        ps_gh = ctx.enter_context(nc.psum_tensor("ps_gh", [P, UG, 256], F32))
        chain, staged, turned, copied = sem("u_chain"), sem("u_staged"), sem("u_turned"), sem("u_copied")
        second, ag_made, ag_turned, ag_copied = sem("second_layer"), sem("ag_made"), sem("ag_turned"), sem("ag_copied")
        gates, rz_ready, rz_done = sem("gates_made"), sem("rz_ready"), sem("rz_done")
        n_ready, n_done, varied, rooted = sem("n_ready"), sem("n_done"), sem("u_varied"), sem("u_rooted")
        eps_added = sem("eps_added")
        x_in = [sem("u_x_in0"), sem("u_x_in1")]
        ready, stored = sem("result_ready"), [sem("stored0"), sem("stored1")]
        passed = sem("update_passed")
        block = ctx.enter_context(nc.Block())

        def per_step(eng, body):
            over_pairs(eng, NS, body)

        @block.vector
        def _(dve):
            def body(m, s, use):
                n, steps = 0, 10

                def then(instruction):
                    nonlocal n
                    n += 1
                    instruction.then_inc(chain, 1)
                    wait_alone(dve, chain, m * steps + n, passed)

                dve.tensor_copy(hx[:, :, :], sums[:, bass.ds(m * UG, UG), :]).then_inc(staged, 1)
                dve.wait_ge(x_in[s], use * 16 + 16)
                dve.wait_ge(staged, m + 1)
                then(dve.tensor_tensor(cb2[:, :, :], hx[:, :, HD:HD + 1].to_broadcast([P, UG, D]),
                                       b2_b[:, :].unsqueeze(1).to_broadcast([P, UG, D]), ALU.mult))
                dve.wait_ge(second, m + 1)
                dve.tensor_tensor(ag[:, :, :], ps_ag[:, :, :], cb2[:, :, :], ALU.add).then_inc(ag_made, 1)
                dve.wait_ge(gates, m + 1)
                dve.tensor_tensor(gi[:, :, :], ps_gi[:, :, 0:3 * D], bih_b[:, :].unsqueeze(1).to_broadcast([P, UG, 3 * D]), ALU.add)
                then(dve.tensor_tensor(gh[:, :, :], ps_gh[:, :, 0:3 * D], bhh_b[:, :].unsqueeze(1).to_broadcast([P, UG, 3 * D]), ALU.add))
                dve.tensor_tensor(pre_rz[:, :, :], gi[:, :, 0:2 * D], gh[:, :, 0:2 * D], ALU.add).then_inc(rz_ready, 1)
                dve.wait_ge(rz_done, m + 1)
                then(dve.tensor_tensor(t1[:, :, :], rz[:, :, 0:D], gh[:, :, 2 * D:], ALU.mult))
                dve.tensor_tensor(t2[:, :, :], gi[:, :, 2 * D:], t1[:, :, :], ALU.add).then_inc(n_ready, 1)
                then(dve.tensor_scalar(t3[:, :, :], rz[:, :, D:], -1.0, 1.0, ALU.mult, ALU.add))
                then(dve.tensor_tensor(t4[:, :, :], rz[:, :, D:], xws[:, s, :, :], ALU.mult))
                dve.wait_ge(n_done, m + 1)
                then(dve.tensor_tensor(t3[:, :, :], t3[:, :, :], nn[:, :, :], ALU.mult))
                then(dve.tensor_tensor(z1[:, :, :], t3[:, :, :], t4[:, :, :], ALU.add))
                then(dve.tensor_tensor(z2[:, :, :], z1[:, :, :], xws[:, s, :, :], ALU.add))
                for j in range(UG):
                    last = dve.bn_stats(stats[:, j, :], z2[:, j, :])
                then(last)
                for j in range(UG):
                    last = dve.bn_aggr(mv[:, j, :], stats[:, j, :])
                last.then_inc(varied, 1)
                dve.wait_ge(rooted, m + 1)
                then(dve.tensor_tensor(z1[:, :, :], z2[:, :, :], mv[:, :, 0:1].to_broadcast([P, UG, D]), ALU.subtract))
                wait(dve, stored[s], use * (16 * UG))
                dve.tensor_tensor(res[:, s, :, :], z1[:, :, :], rstd[:, :].unsqueeze(2).to_broadcast([P, UG, D]), ALU.mult).then_inc(ready, 1)
                assert n == steps, n
            per_step(dve, body)

        @block.gpsimd
        def _(pool):
            pool.memset(power[:, :], -0.5)

            def body(m, s, use):
                pool.wait_ge(varied, m + 1)
                pool.tensor_tensor(var[:, :], mv[:, :, 1], eps[:, 0:1].to_broadcast([P, UG]), ALU.add).then_inc(eps_added, 1)
                pool.wait_ge(eps_added, m + 1)
                pool.tensor_tensor(rstd[:, :], var[:, :], power[:, :], ALU.pow).then_inc(rooted, 1)
            per_step(pool, body)

        @block.scalar
        def _(act):
            def body(m, s, use):
                act.wait_ge(turned, m + 1)
                act.activation(hT[:, :], ps_hT[:, 0:UG * P], ACT.Copy)
                act.activation(xT[:, :], ps_xT[0:D, 0:UG * P], ACT.Copy).then_inc(copied, 1)
                act.wait_ge(ag_turned, m + 1)
                act.activation(agT[:, :], ps_agT[0:D, 0:UG * P], ACT.Copy).then_inc(ag_copied, 1)
                act.wait_ge(rz_ready, m + 1)
                act.activation(rz[:, :, :], pre_rz[:, :, :], ACT.Sigmoid).then_inc(rz_done, 1)
                act.wait_ge(n_ready, m + 1)
                act.activation(nn[:, :, :], t2[:, :, :], ACT.Tanh).then_inc(n_done, 1)
            per_step(act, body)

        @block.tensor
        def _(pe):
            def body(m, s, use):
                pe.wait_ge(staged, m + 1)
                pe.wait_ge(x_in[s], use * 16 + 16)
                for j in range(UG):
                    pe.transpose(ps_hT[:, j * P:(j + 1) * P], hx[:, j, 0:HD], ident[:, :])
                    last = pe.transpose(ps_xT[0:D, j * P:(j + 1) * P], xws[:, s, j, :], ident[:, :])
                last.then_inc(turned, 1)
                pe.wait_ge(copied, m + 1)
                for j in range(UG):
                    last = pe.matmul(ps_ag[:, j, :], hT[:, j * P:(j + 1) * P], W2_T[:, :], start=True, stop=True)
                last.then_inc(second, 1)
                for j in range(UG):
                    pe.matmul(ps_gh[:, j, 0:3 * D], xT[:, j * P:(j + 1) * P], Whh_T[:, :], start=True, stop=True)
                wait_alone(pe, ag_made, m + 1, passed)
                for j in range(UG):
                    last = pe.transpose(ps_agT[0:D, j * P:(j + 1) * P], ag[:, j, :], ident[:, :])
                last.then_inc(ag_turned, 1)
                pe.wait_ge(ag_copied, m + 1)
                for j in range(UG):
                    last = pe.matmul(ps_gi[:, j, 0:3 * D], agT[:, j * P:(j + 1) * P], Wih_T[:, :], start=True, stop=True)
                last.then_inc(gates, 1)
            per_step(pe, body)

        @block.sync
        def _(sp):
            def load(m, s):
                sp.dma_start(xws[:, s, :, :], x1_dram[bass.ds(m * (UG * P), UG * P), :].rearrange("(a p) c -> p a c", p=P)).then_inc(x_in[s], 16)

            load(0, 0)

            def body(m, s, use):
                if not isinstance(m, int) or m + 1 < NS:
                    load(m + 1, 1 - s)
                sp.wait_ge(ready, m + 1)
                for j in range(UG):
                    rows = LAST if isinstance(m, int) and m * UG + j == NW - 1 else P
                    sp.dma_start(out[bass.ds(m * (UG * P) + j * P, rows), :], res[0:rows, s, j, :]).then_inc(stored[s], 16)
            per_step(sp, body)
            sp.wait_ge(stored[0], 16 * UG * ((NS + 1) // 2))
            sp.wait_ge(stored[1], 16 * UG * (NS // 2))


INS = ["x", "src", "dst", "edge_weight", "edge_weight1", "L0_gnn_W", "L0_gnn_b", "L1_gnn_W1", "L1_gnn_b1", "L1_gnn_W2",
       "L1_gnn_b2", "L1_gnn_W_ih", "L1_gnn_b_ih", "L1_gnn_W_hh", "L1_gnn_b_hh"]


def kernel(**inputs):
    import numpy as np
    import concourse.bacc as bacc
    from concourse.bass_utils import run_bass_kernel_spmd

    nc = bacc.Bacc("TRN2", target_bir_lowering=False, num_devices=1)
    arrays, args = {}, []
    for name in INS:
        a = np.ascontiguousarray(inputs[name])
        arrays[f"in_{name}"] = a
        args.append(nc.dram_tensor(f"in_{name}", a.shape, mybir.dt.from_np(a.dtype), kind="ExternalInput").ap())
    x1_dram = nc.dram_tensor("x_after_layer0", (NW * P, D), F32, kind="Internal").ap()
    result = nc.dram_tensor("result", (N, D), F32, kind="ExternalOutput").ap()
    q_windows = nc.dram_tensor("q_windows", (P * QP,), I32, kind="Internal").ap()
    steps = nc.dram_tensor("steps", (NG,), I32, kind="Internal").ap()
    moved = nc.dram_tensor("moved", (NQ * GE, ROW), F32, kind="Internal").ap()
    a_dram = nc.dram_tensor("a_half", (NW * P, HD), F32, kind="Internal").ap()
    program(nc, *args, result, q_windows, steps, moved, a_dram, x1_dram)
    r = run_bass_kernel_spmd(nc, [arrays], core_ids=[0])
    return r.results[0]["result"]
```

```python
from contextlib import ExitStack

import concourse.bass as bass
from concourse import mybir

F32, BF16, I32 = mybir.dt.float32, mybir.dt.bfloat16, mybir.dt.int32
ALU, ACT = mybir.AluOpType, mybir.ActivationFunctionType
AX_X = mybir.AxisListType.X

P = 128
N, E, D, HD = 12500, 400000, 64, 128
NW = (N + P - 1) // P
LAST = N - (NW - 1) * P
TILES = E // P
G = 5
GE = G * P
NG = TILES // G
NB = 25
BT = TILES // NB
ROW = D + 1
NQ = (E + NW * (GE - 1)) // GE + 1
QP = 6
EPS = 1e-05
UB = 7
NU = NW // UB
S = 4
LAG = 3
NCOL = 4
assert NG * (NW - 1) < 1 << 16 and NW <= 1 << 7
assert TILES == NG * G == NB * BT and E == TILES * P and NG % G == 0 and NG // G <= P and NW % UB == 0 and NQ <= P * QP


def wait(eng, sem, value):
    if not isinstance(value, int) or value > 0:
        eng.wait_ge(sem, value)


def wait_alone(eng, sem, value, passed):
    eng.wait_ge(sem, value)
    eng.sem_inc(passed, 1)


def over_pairs(eng, n, body):
    body(0, 0, 0)
    body(1, 1, 0)
    with eng.Fori(1, n // 2) as i:
        body(i * 2, 0, i)
        body(i * 2 + 1, 1, i)
    if n % 2:
        body(n - 1, 0, n // 2)


def over_steps(eng, body):
    over_pairs(eng, NU - 1, body)
    body(NU - 1, (NU - 1) % 2, (NU - 1) // 2)


def is_within(m, ahead):
    return not isinstance(m, int) or m + ahead < NU


def over_groups(eng, n, body, load=None, slots=S):
    def turn(i, count):
        loaded = load(i * slots, count) if load else None
        for s in range(count):
            body(i * slots + s, s, i, loaded)
    turn(0, slots)
    with eng.Fori(1, n // slots) as i:
        turn(i, slots)
    if n % slots:
        turn(n // slots, n % slots)


def last_of(g, s, use):
    return g - 1, (s - 1) % S, use if s else use - 1


def is_first(g):
    return isinstance(g, int) and g == 0


def cols(t, start, size):
    return t[:, bass.ds(start, size)]


def high_halves(ap):
    return ap.bitcast(BF16).rearrange("p (a b) -> p a b", b=2)[:, :, 1]


def fold(ap, n):
    return ap.rearrange("p (a b) -> p a b", a=n)


def program(nc, x, src, dst, w, attr, W, b, W1, b1, W2, b2, W_ih, b_ih, W_hh, b_hh, out,
            places, table, moved, a_dram, x1_dram, x1T_dram, attr9, c_dram, edges_dram):
    with ExitStack() as ctx:
        def sb(name, shape, dt):
            return ctx.enter_context(nc.sbuf_tensor(name, shape, dt))

        lane_row = sb("lane_row", [P, P], BF16)
        node_id = sb("node_id", [P, NW], F32)
        window_base = sb("window_base", [P, NW], F32)
        ident = sb("ident", [P, P], F32)
        before = sb("before", [P, P], F32)
        before_bf = sb("before_bf", [P, P], BF16)
        upto_bf = sb("upto_bf", [P, P], BF16)
        ones_bf = sb("ones_bf", [P, P], BF16)
        ones = sb("ones", [P, P], F32)
        eps = sb("eps", [P, 1], F32)
        zero_bf = sb("zero_bf", [P, 512], BF16)
        src_flat = sb("src_cols", [P, 2 * TILES], BF16)
        src_cols = fold(src_flat[:, :], 2)
        edge_cols = sb("edge_cols", [P, 2, TILES], F32)
        src_hi, src_lo = src_cols[:, 0, :], src_cols[:, 1, :]
        weight, dst_f = edge_cols[:, 0, :], edge_cols[:, 1, :]
        step_tab = sb("step_tab", [1, NG + 2], I32)
        q_tab = sb("q_tab", [1, P * QP + LAG], I32)
        dinv = sb("dinv", [P, NW], F32)
        start_row = sb("start_row", [P, NW], F32)
        tables = sb("tables", [P, NW * 3 * HD], BF16)
        sums = sb("sums", [P, NW, HD + 1], F32)
        W_T = sb("W_T", [D, D], F32)
        W1_T = sb("W1_T", [D, 2 * HD], F32)
        c_row = sb("c_row", [1, HD], F32)
        c_parts = sb("c_parts", [9, HD], BF16)
        W2_T = sb("W2_T", [HD, D], F32)
        Wih_x = sb("Wih_x", [D + 1, 4 * D], F32)
        Whh_x = sb("Whh_x", [D + 1, 4 * D], F32)
        b_b = sb("b_b", [P, D], F32)
        b1_b = sb("b1_b", [P, HD], F32)
        b2_row = sb("b2_row", [1, D], F32)

        flat = sums[:, :, :].rearrange("p a b -> p (a b)")
        acc = flat[:, 0:NW * D]
        xs = flat[:, NW * D:2 * NW * D].rearrange("p (a b) -> p a b", b=D)

        constants(nc, lane_row, node_id, window_base, ident, before, before_bf, upto_bf, ones_bf, ones, eps, zero_bf)
        weights(nc, ident, W, W1, W2, W_ih, W_hh, b, b1, b2, b_ih, b_hh, W_T, W1_T, c_row, W2_T, Wih_x, Whh_x,
                b_b, b1_b, b2_row)
        edge_columns(nc, src, dst, w, ident, src_cols, edge_cols)
        attr_in_parts = ctx.enter_context(nc.semaphore("attr_parts_stored"))
        attribute_parts(nc, attr, c_row, c_parts, tables, attr9, c_dram, attr_in_parts)
        steps_table(nc, dst, before, table, sums, step_tab, q_tab)
        counts(nc, lane_row, ident, ones_bf, before, tables, src_hi, src_lo, weight, moved, places, sums, dinv, start_row, q_tab, attr_in_parts)
        scaled_nodes(nc, x, xs, dinv, tables, acc)
        move_rows(nc, dst, lane_row, node_id, before_bf, upto_bf, ones_bf, ones, zero_bf, src_hi, src_lo, weight,
                  step_tab, start_row, tables, moved)
        sum_moved(nc, lane_row, ones, q_tab, tables, moved, acc)
        nodes(nc, ident, eps, weight, xs, dinv, acc, W_T, b_b, W1_T, b1_b, tables, a_dram, x1_dram, x1T_dram)
        messages(nc, dst, attr9, lane_row, node_id, window_base, ones_bf, src_flat, src_hi, src_lo, weight, dst_f, c_parts, step_tab, tables, sums, a_dram)
        edge_counts(nc, ident, sums, edges_dram)
        update(nc, ident, eps, x1_dram, x1T_dram, sums, tables, src_flat, edges_dram, W2_T, b2_row, Wih_x, Whh_x, out)


def constants(nc, lane_row, node_id, window_base, ident, before, before_bf, upto_bf, ones_bf, ones, eps, zero_bf):
    with ExitStack() as ctx:
        row_i = ctx.enter_context(nc.sbuf_tensor("row_i", [P, P], I32))
        node_i = ctx.enter_context(nc.sbuf_tensor("node_i", [P, NW], I32))
        base_i = ctx.enter_context(nc.sbuf_tensor("base_i", [P, NW], I32))
        made = ctx.enter_context(nc.semaphore("iotas_made"))
        lanes = ctx.enter_context(nc.semaphore("lanes_made"))
        block = ctx.enter_context(nc.Block())

        @block.gpsimd
        def _(pool):
            pool.iota(row_i[:, :], [[1, P]], base=0, channel_multiplier=0)
            pool.iota(node_i[:, :], [[P, NW]], base=0, channel_multiplier=1)
            pool.iota(base_i[:, :], [[P, NW]], base=0, channel_multiplier=0).then_inc(made, 1)

        @block.vector
        def _(dve):
            dve.memset(ones[:, :], 1.0)
            dve.memset(ones_bf[:, :], 1.0)
            dve.memset(eps[:, :], EPS)
            dve.memset(zero_bf[:, :], 0.0)
            dve.wait_ge(made, 1)
            dve.tensor_copy(lane_row[:, :], row_i[:, :]).then_inc(lanes, 1)
            dve.tensor_copy(window_base[:, :], base_i[:, :]).then_inc(lanes, 1)
            dve.tensor_copy(node_id[:, :], node_i[:, :]).then_inc(lanes, 1)
            dve.wait_ge(lanes, 3)
            lane = node_id[:, 0:1]
            dve.tensor_scalar(ident[:, :], lane_row[:, :], lane, None, ALU.is_equal)
            dve.tensor_scalar(before[:, :], lane_row[:, :], lane, None, ALU.is_gt)
            dve.tensor_scalar(before_bf[:, :], lane_row[:, :], lane, None, ALU.is_gt)
            dve.tensor_scalar(upto_bf[:, :], lane_row[:, :], lane, None, ALU.is_le)


def weights(nc, ident, W, W1, W2, W_ih, W_hh, b, b1, b2, b_ih, b_hh, W_T, W1_T, c_row, W2_T, Wih_x, Whh_x,
            b_b, b1_b, b2_row):
    with ExitStack() as ctx:
        def sb(name, shape):
            return ctx.enter_context(nc.sbuf_tensor(name, shape, F32))

        W_s, W1_s, W2_s = sb("W_s", [D, D]), sb("W1_s", [HD, 2 * D + 1]), sb("W2_s", [D, HD])
        ih_s, hh_s = sb("ih_s", [D, 3, D]), sb("hh_s", [D, 3, D])
        ps = ctx.enter_context(nc.psum_tensor("ps_weights", [P, 4, 512], F32))
        loaded = ctx.enter_context(nc.semaphore("weights_loaded"))
        turned = ctx.enter_context(nc.semaphore("weights_turned"))
        cleared = ctx.enter_context(nc.semaphore("gru_cleared"))
        biases_in = ctx.enter_context(nc.semaphore("gru_biases_in"))
        block = ctx.enter_context(nc.Block())
        loads = [(W_s[:, :], W), (W1_s[:, :], W1), (W2_s[:, :], W2),
                 (ih_s[:, :, :], W_ih.rearrange("(a r) c -> r a c", a=3)),
                 (hh_s[:, :, :], W_hh.rearrange("(a r) c -> r a c", a=3))]
        loads += [(t[:, :], v.unsqueeze(0).to_broadcast([P, v.shape[0]])) for t, v in ((b_b, b), (b1_b, b1))]
        loads += [(b2_row[:, :], b2.unsqueeze(0))]
        bias_rows = [(Wih_x[D:D + 1, 0:2 * D], b_ih[0:2 * D]), (Wih_x[D:D + 1, 3 * D:4 * D], b_ih[2 * D:3 * D]),
                     (Whh_x[D:D + 1, 0:3 * D], b_hh)]

        @block.sync
        def _(sp):
            for dest, source in loads:
                sp.dma_start(dest, source).then_inc(loaded, 16)
            sp.wait_ge(cleared, 1)
            for dest, source in bias_rows:
                sp.dma_start(dest, source.unsqueeze(0)).then_inc(biases_in, 16)
            sp.wait_ge(biases_in, 16 * len(bias_rows))

        @block.tensor
        def _(pe):
            pe.wait_ge(loaded, 16 * len(loads))
            pe.transpose(ps[0:D, 0, 0:D], W_s[:, :], ident[0:D, 0:D])
            pe.transpose(ps[0:D, 1, 0:HD], W1_s[:, 0:D], ident[:, :])
            pe.transpose(ps[0:D, 1, HD:2 * HD], W1_s[:, D:2 * D], ident[:, :])
            pe.transpose(ps[:, 0, 256:256 + D], W2_s[:, :], ident[0:D, 0:D])
            pe.matmul(ps[0:1, 0, 384:512], W1_s[:, 2 * D:2 * D + 1], ident[:, :], start=True, stop=True)
            for i in range(3):
                pe.transpose(ps[0:D, 2, i * D:(i + 1) * D], ih_s[:, i, :], ident[0:D, 0:D])
                last = pe.transpose(ps[0:D, 3, i * D:(i + 1) * D], hh_s[:, i, :], ident[0:D, 0:D])
            last.then_inc(turned, 1)

        @block.vector
        def _(dve):
            dve.memset(Wih_x[:, :], 0.0)
            dve.memset(Whh_x[:, :], 0.0).then_inc(cleared, 1)
            dve.wait_ge(cleared, 1)
            dve.wait_ge(turned, 1)
            dve.tensor_copy(W_T[:, :], ps[0:D, 0, 0:D])
            dve.tensor_copy(W1_T[:, :], ps[0:D, 1, 0:2 * HD])
            dve.tensor_copy(W2_T[:, :], ps[:, 0, 256:256 + D])
            dve.tensor_copy(c_row[:, :], ps[0:1, 0, 384:512])
            dve.tensor_copy(Wih_x[0:D, 0:2 * D], ps[0:D, 2, 0:2 * D])
            dve.tensor_copy(Wih_x[0:D, 3 * D:4 * D], ps[0:D, 2, 2 * D:3 * D])
            dve.tensor_copy(Whh_x[0:D, 0:3 * D], ps[0:D, 3, 0:3 * D])


def edge_columns(nc, src, dst, w, ident, src_cols, edge_cols):
    with ExitStack() as ctx:
        raw = ctx.enter_context(nc.sbuf_tensor("edge_raw", [BT, 2, 3, P], I32))
        part = ctx.enter_context(nc.sbuf_tensor("edge_part", [BT, 2, 2, P], I32))
        rows = ctx.enter_context(nc.sbuf_tensor("edge_rows", [BT, 2, NCOL, P], F32))
        ps = ctx.enter_context(nc.psum_tensor("ps_cols", [P, 2, 512], F32))
        raw_in = [ctx.enter_context(nc.semaphore(f"raw_in{s}")) for s in range(2)]
        parted = ctx.enter_context(nc.semaphore("parts_made"))
        rows_made = ctx.enter_context(nc.semaphore("rows_made"))
        turned = ctx.enter_context(nc.semaphore("cols_turned"))
        copied = ctx.enter_context(nc.semaphore("cols_copied"))
        block = ctx.enter_context(nc.Block())
        views = [v.rearrange("(t p) -> t p", p=P) for v in (src, dst, w)]

        @block.sync
        def _(sp):
            def load(i, s, use):
                wait(sp, rows_made, i - 1)
                for a, v in enumerate(views):
                    d = raw[:, s, a, :] if a < 2 else raw[:, s, a, :].bitcast(F32)
                    sp.dma_start(d, v[bass.ds(i * BT, BT), :]).then_inc(raw_in[s], 16)
            over_pairs(sp, NB, load)

        @block.vector
        def _(dve):
            def make(i, s, use):
                dve.wait_ge(raw_in[s], use * 48 + 48)
                wait(dve, turned, i - 1)
                dve.tensor_scalar(part[:, s, 0, :], raw[:, s, 0, :], 7, None, ALU.logical_shift_right).then_inc(parted, 1)
                dve.tensor_scalar(part[:, s, 1, :], raw[:, s, 0, :], P - 1, None, ALU.bitwise_and).then_inc(parted, 1)
                dve.tensor_copy(rows[:, s, 2, :], raw[:, s, 2, :].bitcast(F32))
                dve.tensor_copy(rows[:, s, 3, :], raw[:, s, 1, :])
                dve.wait_ge(parted, i * 2 + 2)
                dve.tensor_copy(rows[:, s, 0:2, :], part[:, s, :, :]).then_inc(rows_made, 1)
            over_pairs(dve, NB, make)

        @block.tensor
        def _(pe):
            def turn(i, s, use):
                pe.wait_ge(rows_made, i + 1)
                wait(pe, copied, i - 1)
                for a in range(NCOL):
                    last = pe.transpose(ps[:, s, a * BT:(a + 1) * BT], rows[:, s, a, :], ident[0:BT, 0:BT])
                last.then_inc(turned, 1)
            over_pairs(pe, NB, turn)

        @block.scalar
        def _(act):
            def copy(i, s, use):
                act.wait_ge(turned, i + 1)
                act.activation(src_cols[:, :, bass.ds(i * BT, BT)], fold(ps[:, s, 0:2 * BT], 2), ACT.Copy)
                act.activation(edge_cols[:, :, bass.ds(i * BT, BT)], fold(ps[:, s, 2 * BT:4 * BT], 2), ACT.Copy).then_inc(copied, 1)
            over_pairs(act, NB, copy)


def steps_table(nc, dst, before, table, sums, step_tab, q_tab):
    R = NG // G
    with ExitStack() as ctx:
        def sb(name, shape, dt):
            return ctx.enter_context(nc.sbuf_tensor(name, shape, dt))

        ids = sums[:, :, :].rearrange("p a b -> p (a b)")[0:R, 0:G * GE].bitcast(I32)
        ends = sb("ends", [R, 2, G], I32)
        wins = sb("wins", [R, 2, G], I32)
        win_f = sb("win_f", [R, 2, G], F32)
        width = sb("width", [R, G + 1], F32)
        first = sb("first", [R, G + 1], F32)
        tab_i = sb("tab_i", [R, 4, G], I32)
        packed = sb("packed", [R, G], I32)
        ps = ctx.enter_context(nc.psum_tensor("ps_steps", [P, 512], F32))
        ids_in = ctx.enter_context(nc.semaphore("ids_in"))
        chain = ctx.enter_context(nc.semaphore("steps_chain"))
        widths = ctx.enter_context(nc.semaphore("widths_made"))
        summed = ctx.enter_context(nc.semaphore("widths_summed"))
        made = ctx.enter_context(nc.semaphore("steps_made"))
        kept = ctx.enter_context(nc.semaphore("steps_kept"))
        back = ctx.enter_context(nc.semaphore("steps_back"))
        block = ctx.enter_context(nc.Block())

        @block.sync
        def _(sp):
            sp.dma_start(ids, dst.rearrange("(p e) -> p e", p=R)).then_inc(ids_in, 16)
            sp.wait_ge(made, 1)
            sp.dma_start(table.rearrange("(p e) -> p e", p=R), packed[:, :]).then_inc(kept, 16)
            sp.wait_ge(kept, 16)
            sp.dma_start(step_tab[:, 2:NG + 2], table.unsqueeze(0)).then_inc(back, 16)
            sp.wait_ge(back, 16)

        @block.tensor
        def _(pe):
            pe.wait_ge(widths, 1)
            pe.matmul(ps[0:R, 0:1], before[0:R, 0:R], width[:, G:G + 1], start=True, stop=True).then_inc(summed, 1)

        @block.vector
        def _(dve):
            n = 0

            def then(instruction):
                nonlocal n
                n += 1
                instruction.then_inc(chain, 1)
                dve.wait_ge(chain, n)

            dve.memset(step_tab[:, 0:2], 0)
            dve.memset(q_tab[:, 0:LAG], 0)
            dve.wait_ge(ids_in, 16)
            dve.tensor_reduce(ends[:, 0, :], fold(ids, G), AX_X, ALU.min)
            then(dve.tensor_reduce(ends[:, 1, :], fold(ids, G), AX_X, ALU.max))
            then(dve.tensor_scalar(wins[:, :, :], ends[:, :, :], 7, None, ALU.logical_shift_right))
            then(dve.tensor_copy(win_f[:, :, :], wins[:, :, :]))
            then(dve.tensor_tensor(width[:, 0:G], win_f[:, 1, :], win_f[:, 0, :], ALU.subtract))
            dve.tensor_reduce(width[:, G:G + 1], width[:, 0:G], AX_X, ALU.add).then_inc(widths, 1)
            dve.wait_ge(summed, 1)
            then(dve.tensor_copy(first[:, 0:1], ps[0:R, 0:1]))
            for j in range(G):
                then(dve.tensor_tensor(first[:, j + 1:j + 2], first[:, j:j + 1], width[:, j:j + 1], ALU.add))
            dve.tensor_copy(tab_i[:, 0, :], first[:, 0:G])
            then(dve.tensor_copy(tab_i[:, 1, :], width[:, 0:G]))
            dve.tensor_scalar(tab_i[:, 2, :], wins[:, 0, :], 16, None, ALU.logical_shift_left)
            then(dve.tensor_scalar(tab_i[:, 3, :], tab_i[:, 1, :], 23, None, ALU.logical_shift_left))
            then(dve.tensor_tensor(tab_i[:, 0, :], tab_i[:, 0, :], tab_i[:, 2, :], ALU.bitwise_or))
            dve.tensor_tensor(packed[:, :], tab_i[:, 0, :], tab_i[:, 3, :], ALU.bitwise_or).then_inc(made, 1)


def attribute_parts(nc, attr, c_row, c_parts, tables, attr9, c_dram, stored):
    with ExitStack() as ctx:
        wide = tables[:, 0:2 * 2 * TILES].bitcast(F32).rearrange("p (a b) -> p a b", a=2)
        parts = tables[:, 4 * TILES:7 * TILES].rearrange("p (a b) -> p a b", a=3)
        c_rest = ctx.enter_context(nc.sbuf_tensor("c_rest", [1, HD], F32))
        c_cut = ctx.enter_context(nc.sbuf_tensor("c_cut", [1, 3, HD], BF16))
        attr_in, c_kept, c_back = (ctx.enter_context(nc.semaphore(n)) for n in ("attr_in", "c_kept", "c_back"))
        chain, c_done, attr_done = (ctx.enter_context(nc.semaphore(n)) for n in ("parts_chain", "c_split", "attr_split"))
        block = ctx.enter_context(nc.Block())

        @block.sync
        def _(sp):
            sp.dma_start(wide[:, 0, :], attr.rearrange("(p t) c -> p (t c)", p=P)).then_inc(attr_in, 16)
            sp.wait_ge(c_done, 1)
            sp.dma_start(c_dram.unsqueeze(0), c_cut[:, :, :]).then_inc(c_kept, 16)
            sp.wait_ge(c_kept, 16)
            for i in range(3):
                sp.dma_start(c_parts[3 * i:3 * i + 3, :], c_dram[i:i + 1, :].to_broadcast([3, HD])).then_inc(c_back, 16)
            sp.wait_ge(attr_done, 1)
            for i in range(9):
                sp.dma_start(attr9[i, :].rearrange("(p t) -> p t", p=P), parts[:, i % 3, :]).then_inc(stored, 16)
            sp.wait_ge(c_back, 48)

        @block.vector
        def _(dve):
            n = 0

            def then(instruction):
                nonlocal n
                n += 1
                instruction.then_inc(chain, 1)
                dve.wait_ge(chain, n)

            split_bf16(dve, then, c_row[:, :], c_rest[:, :], [c_cut[:, i, :] for i in range(3)], c_done)
            dve.wait_ge(attr_in, 16)
            split_bf16(dve, then, wide[:, 0, :], wide[:, 1, :], [parts[:, i, :] for i in range(3)], attr_done)


def counts(nc, lane_row, ident, ones_bf, before, tables, src_hi, src_lo, weight, moved, places, sums, dinv, start_row, q_tab, attr_in_parts):
    ZG = 4
    with ExitStack() as ctx:
        def sb(name, shape, dt):
            return ctx.enter_context(nc.sbuf_tensor(name, shape, dt))

        def sem(name):
            return ctx.enter_context(nc.semaphore(name))

        lo_hot = sb("lo_hot", [P, S, G, P], F32)
        hi_hot = sb("hi_hot", [P, S, G, NW], BF16)
        hi_weight = tables[:, 8 * TILES:8 * TILES + 2 * S * G * P].bitcast(F32).rearrange("p (a b c) -> p a b c", a=S, b=G)
        ps = ctx.enter_context(nc.psum_tensor("ps_degrees", [P, 512], F32))
        ps_edges = ctx.enter_context(nc.psum_tensor("ps_edges", [P, G, NW], F32))
        edges_b = sb("edges_b", [P, NW], F32)
        own = sb("own", [NW, NW], F32)
        ps_sum = ctx.enter_context(nc.psum_tensor("ps_sum", [P, 512], F32))
        zeros = sums[:, :, :].rearrange("p a b -> p (a b)")[:, 0:ZG * G * ROW]
        deg, live, safe, root = (sb(n, [P, NW], F32) for n in ("deg", "live", "safe", "root"))
        total = sb("total", [NW, 1], F32)
        groups = sb("groups", [NW, 1], F32)
        steps_i = sb("steps_i", [NW, NG + 1], I32)
        full = sb("full", [NW, NG + 1], F32)
        padded = sb("padded", [NW, 1], F32)
        padded_b = sb("padded_b", [NW, P], F32)
        q_i = sb("q_i", [P, QP], I32)
        q_f = sb("q_f", [P, QP], F32)
        q_le = sb("q_le", [P, QP, NW], F32)
        q_win = sb("q_win", [P, QP], F32)
        q_out = sb("q_out", [P, QP], I32)
        zeroed, zero_done = sem("zeros_made"), sem("zero_done")
        hot_made, weighted, used = sem("hot_made"), sem("hot_weighted"), sem("hot_used")
        chain = sem("count_chain")
        pads_made, starts_made = sem("pads_made"), sem("starts_made")
        guarded, rooted = sem("degree_guarded"), sem("degree_rooted")
        q_ready, q_made, q_kept, q_back = sem("q_ready"), sem("q_made"), sem("q_kept"), sem("q_back")
        block = ctx.enter_context(nc.Block())

        @block.sync
        def _(sp):
            sp.wait_ge(zeroed, 1)
            with sp.Fori(0, NQ // ZG) as i:
                sp.dma_start(moved[bass.ds(i * (ZG * GE), ZG * GE), :].rearrange("(p r) c -> p (r c)", p=P),
                             zeros).then_inc(zero_done, 16)
            for i in range(NQ // ZG * ZG, NQ):
                sp.dma_start(moved[i * GE:(i + 1) * GE, :].rearrange("(p r) c -> p (r c)", p=P),
                             zeros[:, 0:G * ROW]).then_inc(zero_done, 16)
            sp.wait_ge(q_made, 1)
            sp.dma_start(places.rearrange("(p e) -> p e", p=P), q_out[:, :]).then_inc(q_kept, 16)
            sp.wait_ge(q_kept, 16)
            sp.dma_start(q_tab[:, LAG:], places.unsqueeze(0)).then_inc(q_back, 16)
            sp.wait_ge(q_back, 16)
            sp.wait_ge(zero_done, 16 * (NQ // ZG + NQ % ZG))
            sp.wait_ge(attr_in_parts, 16 * 9)

        @block.gpsimd
        def _(pool):
            pool.memset(zeros, 0.0).then_inc(zeroed, 1)
            pool.iota(q_i[:, :], [[GE, QP]], base=0, channel_multiplier=GE * QP).then_inc(q_ready, 1)
            pool.iota(steps_i[:, :], [[GE, NG + 1]], base=GE, channel_multiplier=0).then_inc(q_ready, 1)

            pool.memset(hi_weight[:, :, :, NW:], 0.0)

            def body(g, s, use, _):
                pool.wait_ge(hot_made, g + 1)
                wait(pool, used, g - (S - 1))
                pool.tensor_tensor(hi_weight[:, s, :, 0:NW], hi_hot[:, s, :, :],
                                   cols(weight, g * G, G).unsqueeze(2).to_broadcast([P, G, NW]), ALU.mult).then_inc(weighted, 1)
            over_groups(pool, NG, body)

        @block.vector
        def _(dve):
            def body(g, s, use, _):
                wait(dve, used, g - (S - 1))
                dve.tensor_tensor(hi_hot[:, s, :, :], lane_row[:, 0:NW].unsqueeze(1).to_broadcast([P, G, NW]),
                                  cols(src_hi, g * G, G).unsqueeze(2).to_broadcast([P, G, NW]), ALU.is_equal).then_inc(hot_made, 1)
                dve.tensor_tensor(lo_hot[:, s, :, :], lane_row[:, :].unsqueeze(1).to_broadcast([P, G, P]),
                                  cols(src_lo, g * G, G).unsqueeze(2).to_broadcast([P, G, P]), ALU.is_equal).then_inc(chain, 1)
            over_groups(dve, NG, body)
            n = NG

            def then(instruction):
                nonlocal n
                n += 1
                instruction.then_inc(chain, 1)
                dve.wait_ge(chain, n)

            dve.wait_ge(used, NG)
            then(dve.tensor_scalar(deg[:, :], ps[:, 0:NW], 1.0, None, ALU.add))
            then(dve.tensor_scalar(live[:, :], deg[:, :], 0.0, None, ALU.is_gt))
            then(dve.tensor_tensor(safe[:, :], deg[:, :], live[:, :], ALU.mult))
            then(dve.scalar_tensor_tensor(root[:, :], live[:, :], -1.0, safe[:, :], ALU.mult, ALU.add))
            then(dve.tensor_scalar(safe[:, :], root[:, :], 1.0, None, ALU.add))
            dve.engine_nop().then_inc(guarded, 1)
            dve.wait_ge(rooted, 1)
            then(dve.reciprocal(safe[:, :], root[:, :]))
            then(dve.tensor_tensor(dinv[:, :], safe[:, :], live[:, :], ALU.mult))
            dve.wait_ge(q_ready, 2)
            then(dve.tensor_reduce(edges_b[:, :], ps_edges[:, :, :].rearrange("p a b -> p b a"), AX_X, ALU.add))
            then(dve.tensor_tensor(own[:, :], edges_b[0:NW, :], ident[0:NW, 0:NW], ALU.mult))
            then(dve.tensor_reduce(groups[:, :], own[:, :], AX_X, ALU.add))
            then(dve.tensor_scalar(total[:, :], groups[:, :], float(GE - 1), None, ALU.add))
            then(dve.tensor_scalar(full[:, :], steps_i[:, :], total[:, 0:1], None, ALU.is_le))
            then(dve.tensor_reduce(groups[:, :], full[:, :], AX_X, ALU.add))
            then(dve.tensor_scalar(padded[:, :], groups[:, :], float(GE), None, ALU.mult))
            dve.tensor_copy(padded_b[:, :], padded[:, 0:1].to_broadcast([NW, P])).then_inc(pads_made, 1)
            dve.wait_ge(starts_made, 1)
            dve.tensor_copy(q_f[:, :], q_i[:, :])
            then(dve.tensor_copy(start_row[:, :], ps_sum[:, 128:128 + NW]))
            then(dve.tensor_tensor(q_le[:, :, :], start_row[:, :].unsqueeze(1).to_broadcast([P, QP, NW]),
                                   q_f[:, :].unsqueeze(2).to_broadcast([P, QP, NW]), ALU.is_le))
            then(dve.tensor_reduce(q_win[:, :], q_le[:, :, :], AX_X, ALU.add))
            dve.tensor_scalar(q_out[:, :], q_win[:, :], -1.0, None, ALU.add).then_inc(q_made, 1)

        @block.scalar
        def _(act):
            act.wait_ge(guarded, 1)
            act.activation(root[:, :], safe[:, :], ACT.Sqrt).then_inc(rooted, 1)

        @block.tensor
        def _(pe):
            def body(g, s, use, _):
                first, last_one = is_first(g), isinstance(g, int) and g == NG - 1
                pe.wait_ge(weighted, g + 1)
                pe.matmul(ps_edges[:, :, :], ones_bf[:, :], hi_hot[:, s, :, :], start=first, stop=last_one)
                pe.wait_ge(chain, g + 1)
                for j in range(G):
                    last = pe.matmul(ps[:, 0:P], lo_hot[:, s, j, :], hi_weight[:, s, j, :], start=first and j == 0,
                                     stop=last_one and j == G - 1, skip_group_check=True)
                last.then_inc(used, 1)
            over_groups(pe, NG, body)
            pe.wait_ge(pads_made, 1)
            pe.matmul(ps_sum[:, 128:128 + NW], padded_b[:, :], before[0:NW, 0:NW], start=True, stop=True).then_inc(starts_made, 1)


def split_bf16(dve, then, value, rest, parts, last_sem):
    then(dve.tensor_copy(parts[0], value))
    then(dve.tensor_tensor(rest, value, parts[0], ALU.subtract))
    then(dve.tensor_copy(parts[1], rest))
    dve.tensor_tensor(parts[2], rest, parts[1], ALU.subtract).then_inc(last_sem, 1)


def scaled_nodes(nc, x, xs, dinv, tables, acc):
    with ExitStack() as ctx:
        y = acc.rearrange("p (a b) -> p a b", b=D)
        rest = tables[:, NW * 3 * D:NW * 5 * D].bitcast(F32).rearrange("p (a b) -> p a b", b=D)
        parts = tables[:, 0:NW * 3 * D].rearrange("p (a k b) -> p a k b", k=3, b=D)
        cleared = ctx.enter_context(nc.semaphore("x_cleared"))
        x_in = ctx.enter_context(nc.semaphore("x_in"))
        chain = ctx.enter_context(nc.semaphore("y_chain"))
        done = ctx.enter_context(nc.semaphore("y_done"))
        block = ctx.enter_context(nc.Block())

        @block.sync
        def _(sp):
            sp.wait_ge(cleared, 1)
            sp.dma_start(xs[:, 0:NW - 1, :], x[0:(NW - 1) * P, :].rearrange("(a p) c -> p a c", p=P)).then_inc(x_in, 16)
            sp.dma_start(xs[0:LAST, NW - 1, :], x[(NW - 1) * P:N, :]).then_inc(x_in, 16)

        @block.vector
        def _(dve):
            n = 0

            def then(instruction):
                nonlocal n
                n += 1
                instruction.then_inc(chain, 1)
                dve.wait_ge(chain, n)

            dve.memset(xs[:, NW - 1, :], 0.0).then_inc(cleared, 1)
            dve.wait_ge(x_in, 32)
            then(dve.tensor_tensor(y, xs[:, :, :], dinv[:, :].unsqueeze(2).to_broadcast([P, NW, D]), ALU.mult))
            split_bf16(dve, then, y, rest, [parts[:, :, k, :] for k in range(3)], done)


def move_rows(nc, dst, lane_row, node_id, before_bf, upto_bf, ones_bf, ones, zero_bf, src_hi, src_lo, weight,
              step_tab, start_row, tables, moved):
    with ExitStack() as ctx:
        def sb(name, shape, dt):
            return ctx.enter_context(nc.sbuf_tensor(name, shape, dt))

        def sem(name):
            return ctx.enter_context(nc.semaphore(name))

        dst_rows = sb("dst_rows", [P, S, GE], I32)
        dst_hot = sb("dst_hot", [P, 3, GE], BF16)
        hi_hot = sb("place_hot", [P, 2, G, NW], BF16)
        junk = sb("junk", [P, 2, G, NW], F32)
        place_f = sb("place_f", [P, 2, G], F32)
        place = sb("place", [P, S, G], I32)
        rows = sb("rows", [P, S, G, ROW], F32)
        ps_rows = ctx.enter_context(nc.psum_tensor("ps_rows", [P, 2, 512], F32))
        ps_mark = ctx.enter_context(nc.psum_tensor("ps_moved_mark", [P, 512], F32))
        ps_place = ctx.enter_context(nc.psum_tensor("ps_place", [P, G, NW], F32))
        rows_in = [sem(f"dst_rows_in{s}") for s in range(S)]
        scattered = [sem(f"scattered{s}") for s in range(S)]
        hot_made, extra_made, extra_done = sem("dst_hot_made"), sem("extra_hot_made"), sem("extra_gathered")
        gathered = sem("gathered")
        hi_made, placed, read = sem("place_hot_made"), sem("placed"), sem("places_read")
        cast, rows_ready = sem("places_cast"), sem("rows_ready")
        parts = tables[:, 0:NW * 3 * D]
        passed = sem("move_rows_passed")
        block = ctx.enter_context(nc.Block())

        @block.sync
        def _(sp):
            def body(g, s, use, _):
                wait(sp, placed, g - (S - 1))
                sp.dma_start(dst_rows[:, s, :], dst[bass.ds(g * GE, GE)].unsqueeze(0).to_broadcast([P, GE])).then_inc(rows_in[s], 16)
            over_groups(sp, NG, body)

        @block.vector
        def _(dve):
            dve_regs = [dve.alloc_register(f"move_dve{i}") for i in range(S + 2)]

            def read_places(g, s, use):
                dve.wait_ge(placed, g + 1)
                h = s % 2
                for j in range(G):
                    last = dve.tensor_tensor_reduce(junk[:, h, j, :], ps_place[:, j, :], hi_hot[:, h, j, :], 1.0, 0.0,
                                                    ALU.mult, ALU.add, place_f[:, h, j:j + 1])
                last.then_inc(read, 1)
                dve.wait_ge(read, g + 1)
                wait(dve, scattered[s], use * (16 * G))
                dve.tensor_copy(place[:, s, :], place_f[:, h, :]).then_inc(cast, 1)

            def body(g, s, use, windows):
                dve.wait_ge(rows_in[s], use * 16 + 16)
                wait(dve, gathered, g - 1)
                dve.tensor_scalar(dst_hot[:, s % 2, :], dst_rows[:, s, :], cols(node_id, windows[s + 2][2], 1), None,
                                  ALU.is_equal).then_inc(hot_made, 1)

                def extra(x, win):
                    dve.wait_ge(extra_done, x + 1)
                    dve.tensor_scalar(dst_hot[:, 2, :], dst_rows[:, s, :], cols(node_id, win, 1), None,
                                      ALU.is_equal).then_inc(extra_made, 1)
                extra_windows(dve, windows[s + 2], extra)
                if not is_first(g):
                    read_places(*last_of(g, s, use))
                dve.tensor_tensor(hi_hot[:, s % 2, :, :], lane_row[:, 0:NW].unsqueeze(1).to_broadcast([P, G, NW]),
                                  cols(src_hi, g * G, G).unsqueeze(2).to_broadcast([P, G, NW]), ALU.is_equal).then_inc(hi_made, 1)
            over_groups(dve, NG, body, lambda g0, n: load_windows(dve, step_tab, dve_regs, g0, n))
            read_places(NG - 1, (NG - 1) % S, (NG - 1) // S)

        @block.tensor
        def _(pe):
            pe_regs = [pe.alloc_register(f"move_pe{i}") for i in range(S + 2)]
            pe.sem_inc(extra_done, 1)
            pe.matmul(ps_place[:, :, :], ones[0:1, :], start_row[0:1, :].unsqueeze(1).to_broadcast([1, G, NW]),
                      start=True, stop=False, skip_group_check=True)

            def body(g, s, use, windows):
                wait(pe, rows_ready, g - 1)
                h = s % 2
                pe.matmul(ps_rows[:, h, 0:G * D], zero_bf[:, 0:P], zero_bf[:, 0:G * D], start=True, stop=False, skip_group_check=True)

                def gather(slot, win):
                    for j in range(G):
                        for i in range(3):
                            last = pe.matmul(ps_rows[:, h, j * D:(j + 1) * D], dst_hot[:, slot, j * P:(j + 1) * P],
                                             cols(parts, win * (3 * D) + i * D, D), start=False, stop=False, skip_group_check=True)
                    return last

                pe.wait_ge(hot_made, g + 1)
                gather(h, windows[s + 2][2])

                def extra(x, win):
                    pe.wait_ge(extra_made, x + 1)
                    gather(2, win).then_inc(extra_done, 1)
                extra_windows(pe, windows[s + 2], extra)
                pe.matmul(ps_mark[:, 0:1], ones_bf[:, :], ones_bf[:, 0:1], start=True, stop=True).then_inc(gathered, 1)

                def advance(j0, j1, stationary, hot):
                    return pe.matmul(ps_place[:, j0:j1, :], stationary[:, :], hot, start=False, stop=False, skip_group_check=True)

                if not is_first(g):
                    pe.wait_ge(read, g)
                    advance(0, G, upto_bf, hi_hot[:, 1 - h, :, :])
                    for j in range(1, G):
                        advance(0, j, ones_bf, hi_hot[:, 1 - h, j:j + 1, :].to_broadcast([P, j, NW]))
                pe.wait_ge(hi_made, g + 1)
                for j in range(G - 1):
                    advance(j + 1, G, ones_bf, hi_hot[:, h, j:j + 1, :].to_broadcast([P, G - 1 - j, NW]))
                advance(0, G, before_bf, hi_hot[:, h, :, :]).then_inc(placed, 1)
            over_groups(pe, NG, body, lambda g0, n: load_windows(pe, step_tab, pe_regs, g0, n))

        @block.scalar
        def _(act):
            def body(g, s, use, _):
                act.wait_ge(gathered, g + 1)
                wait(act, scattered[s], use * (16 * G))
                for j in range(G):
                    act.activation(rows[:, s, j, 0:D], ps_rows[:, s % 2, j * D:(j + 1) * D], ACT.Copy, scale=cols(weight, g * G + j, 1))
                act.activation(rows[:, s, :, D], cols(src_lo, g * G, G), ACT.Copy).then_inc(rows_ready, 1)
            over_groups(act, NG, body)

        @block.gpsimd
        def _(pool):
            def body(g, s, use, _):
                pool.wait_ge(cast, g + 1)
                wait_alone(pool, rows_ready, g + 1, passed)
                for j in range(G):
                    pool.indirect_dma_start(out=moved[:, :], out_offset=bass.IndirectOffsetOnAxis(ap=place[:, s, j:j + 1], axis=0),
                                            in_=rows[:, s, j, :], in_offset=None).then_inc(scattered[s], 16)
            over_groups(pool, NG, body)
            for s in range(S):
                pool.wait_ge(scattered[s], 16 * G * ((NG - 1 - s) // S + 1))


def load_windows(eng, step_tab, regs, g0, count):
    eng.load(regs[0:count + 2], step_tab[0:1, bass.ds(g0, count + 2)])
    got = []
    for r in regs[0:count + 2]:
        v = eng.snap(r).with_bounds(min_val=0, max_val=(1 << 30) - 1)
        x0 = eng.snap(v & 0xFFFF)
        got.append((x0, eng.snap(x0 + (v >> 23)), window(eng.snap((v >> 16) & 127))))
    return got


def extra_windows(eng, windows, body):
    x0, x1, least = windows
    with eng.If(x0 < x1):
        with eng.Fori(x0, x1) as x:
            body(x, window(x - x0 + least + 1))


def window(value):
    return value.with_bounds(min_val=0, max_val=NW - 1)


def sum_moved(nc, lane_row, ones, q_tab, tables, moved, acc):
    SL = 8
    VT = 3
    with ExitStack() as ctx:
        def sb(name, shape, dt):
            return ctx.enter_context(nc.sbuf_tensor(name, shape, dt))

        def sem(name):
            return ctx.enter_context(nc.semaphore(name))

        rows = fold(tables[:, 0:2 * SL * G * ROW].bitcast(F32), SL)
        left = fold(tables[:, 2 * SL * G * ROW:2 * SL * G * (ROW + D)].bitcast(F32), SL)
        rest = sb("rows_rest", [P, SL, G * D], BF16)
        hot = sb("lane_hot", [P, SL, G, P], BF16)
        away = sb("lanes_away", [P, SL, G - VT, P], BF16)
        ps = ctx.enter_context(nc.psum_tensor("ps_moved", [P, SL, 512], F32))
        rows_in = [sem(f"moved_in{s}") for s in range(SL)]
        left_made, hot_made, away_made, act_hot_made = sem("left_made"), sem("lane_hot_made"), sem("away_made"), sem("act_hot_made")
        summed, added, cleared = sem("rows_summed"), sem("sums_added"), sem("sums_cleared")
        passed = sem("sum_moved_passed")
        block = ctx.enter_context(nc.Block())

        def high_rows(s):
            return fold(high_halves(rows[:, s, :]), G)[:, :, 0:D]

        @block.sync
        def _(sp):
            def body(q, s, use, _):
                wait(sp, summed, q - (SL - 1))
                sp.dma_start(rows[:, s, :], moved[bass.ds(q * GE, GE), :].rearrange("(p r) c -> p (r c)", p=P)).then_inc(rows_in[s], 16)
            over_groups(sp, NQ, body, slots=SL)

        @block.gpsimd
        def _(pool):
            def body(q, s, use, _):
                wait_alone(pool, rows_in[s], use * 16 + 16, passed)
                pool.tensor_tensor(fold(left[:, s, :], G), fold(rows[:, s, :], G)[:, :, 0:D], high_rows(s), ALU.subtract).then_inc(left_made, 1)
            over_groups(pool, NQ, body, slots=SL)

        @block.scalar
        def _(act):
            def near(s):
                act.activation(hot[:, s, VT:, :], away[:, s, :, :], ACT.Relu, bias=ones[:, 0:1], scale=-1.0).then_inc(act_hot_made, 1)

            def body(q, s, use, _):
                act.wait_ge(rows_in[s], use * 16 + 16)
                wait(act, act_hot_made, q - (SL - 1))
                for j in range(VT, G):
                    last = act.activation(away[:, s, j - VT, :], lane_row[:, :], ACT.Abs,
                                          bias=rows[:, s, j * ROW + D:j * ROW + D + 1], scale=-1.0)
                last.then_inc(away_made, 1)
                if not is_first(q):
                    act.wait_ge(away_made, q)
                    near((s - 1) % SL)
            over_groups(act, NQ, body, slots=SL)
            act.wait_ge(away_made, NQ)
            near((NQ - 1) % SL)

        @block.vector
        def _(dve):
            regs = [dve.alloc_register(f"sum_dve{i}") for i in range(SL + LAG)]

            def load(q0, count):
                dve.load(regs[0:count + LAG], q_tab[0:1, bass.ds(q0, count + LAG)])
                return [dve.snap(x).with_bounds(min_val=0, max_val=NW - 1) for x in regs[0:count + LAG]]

            def add(q, s, win):
                dve.wait_ge(summed, q + 1)
                wait(dve, added, q)
                here = cols(acc, win * D, D)
                dve.tensor_tensor(here, here, ps[:, s, 0:D], ALU.add).then_inc(added, 1)

            dve.memset(acc, 0.0).then_inc(cleared, 1)
            dve.wait_ge(cleared, 1)

            def body(q, s, use, wins):
                dve.wait_ge(rows_in[s], use * 16 + 16)
                dve.tensor_tensor(hot[:, s, 0:VT, :], lane_row[:, :].unsqueeze(1).to_broadcast([P, VT, P]),
                                  fold(rows[:, s, :], G)[:, 0:VT, D:D + 1].to_broadcast([P, VT, P]), ALU.is_equal)
                dve.wait_ge(left_made, q + 1)
                dve.tensor_tensor(rest[:, s, :], left[:, s, :], high_halves(left[:, s, :]), ALU.subtract).then_inc(hot_made, 1)
                if not (isinstance(q, int) and q < LAG):
                    add(q - LAG, (s - LAG) % SL, wins[s])
            over_groups(dve, NQ, body, load, slots=SL)
            wins = load(NQ - LAG, LAG)
            for i in range(LAG):
                add(NQ - LAG + i, (NQ - LAG + i) % SL, wins[LAG + i])

        @block.tensor
        def _(pe):
            def body(q, s, use, _):
                pe.wait_ge(hot_made, q + 1)
                pe.wait_ge(act_hot_made, q + 1)
                wait(pe, added, q - (SL - 1))
                for j in range(G):
                    parts = high_rows(s)[:, j, :], high_halves(left[:, s, :])[:, j * D:(j + 1) * D], rest[:, s, j * D:(j + 1) * D]
                    for i, part in enumerate(parts):
                        last = pe.matmul(ps[:, s, 0:D], hot[:, s, j, :], part, start=(i == j == 0), stop=(i == 2 and j == G - 1))
                last.then_inc(summed, 1)
            over_groups(pe, NQ, body, slots=SL)


def nodes(nc, ident, eps, weight, xs, dinv, acc, W_T, b_b, W1_T, b1_b, tables, a_dram, x1_dram, x1T_dram):
    with ExitStack() as ctx:
        def sb(name, shape, dt=F32):
            return ctx.enter_context(nc.sbuf_tensor(name, shape, dt))

        def sem(name):
            return ctx.enter_context(nc.semaphore(name))

        scaled = sb("scaled", [P, UB, D])
        agg = sb("agg", [P, UB, D])
        aggT = sb("aggT", [D, UB * P])
        z = sb("z", [P, UB, D])
        stats = sb("stats", [P, UB, 6])
        mv = sb("mv", [P, UB, 2])
        std = sb("std", [P, UB])
        rstd = sb("rstd", [P, UB])
        x_new = sb("x_new", [P, 2, UB, D])
        xT = sb("xT", [D, 2, UB * P])
        a_out = sb("a_out", [P, 2, UB, HD])
        b_f, b_rest = (weight[:, i * UB * HD:(i + 1) * UB * HD].rearrange("p (a b) -> p a b", a=UB) for i in range(2))
        ps_T = ctx.enter_context(nc.psum_tensor("ps_T", [P, 1024], F32))
        ps_z = ctx.enter_context(nc.psum_tensor("ps_z", [P, UB, D], F32))
        ps_ab = ctx.enter_context(nc.psum_tensor("ps_ab", [P, 8, 2 * HD], F32))
        made, turned, copied = sem("agg_made"), sem("agg_turned"), sem("agg_copied")
        projected, varied, rooted, normed = sem("projected"), sem("variance_made"), sem("variance_rooted"), sem("normed")
        x_turned, x_copied, halves, b_read, b_split = sem("x_turned"), sem("x_copied"), sem("halves_made"), sem("b_read"), sem("b_split")
        a_copied, stored = sem("a_copied"), [sem("node_stored0"), sem("node_stored1")]
        agg_chain, norm_chain, split_chain = sem("agg_chain"), sem("norm_chain"), sem("split_chain")
        passed = sem("nodes_passed")
        block = ctx.enter_context(nc.Block())

        @block.vector
        def _(dve):
            def in_chain(chain, m, steps):
                n = 0

                def then(instruction):
                    nonlocal n
                    n += 1
                    assert n <= steps
                    instruction.then_inc(chain, 1)
                    wait_alone(dve, chain, m * steps + n, passed)
                return then

            def aggregate(m):
                then = in_chain(agg_chain, m, 2)
                d_b = cols(dinv, m * UB, UB).unsqueeze(2).to_broadcast([P, UB, D])
                a_b = fold(cols(acc, m * (UB * D), UB * D), UB)
                wait(dve, turned, m)
                then(dve.tensor_tensor(scaled[:, :, :], xs[:, bass.ds(m * UB, UB), :], d_b, ALU.mult))
                then(dve.tensor_tensor(scaled[:, :, :], scaled[:, :, :], a_b, ALU.add))
                dve.tensor_tensor(agg[:, :, :], scaled[:, :, :], d_b, ALU.mult).then_inc(made, 1)

            aggregate(0)

            def body(m, s, use):
                then = in_chain(norm_chain, m, 5)
                dve.wait_ge(projected, m + 1)
                then(dve.tensor_tensor(z[:, :, :], ps_z[:, :, :], b_b[:, :].unsqueeze(1).to_broadcast([P, UB, D]), ALU.add))
                then(dve.tensor_tensor(z[:, :, :], z[:, :, :], xs[:, bass.ds(m * UB, UB), :], ALU.add))
                for j in range(UB):
                    last = dve.bn_stats(stats[:, j, :], z[:, j, :])
                then(last)
                for j in range(UB):
                    last = dve.bn_aggr(mv[:, j, :], stats[:, j, :])
                last.then_inc(varied, 1)
                dve.wait_ge(varied, m + 1)
                then(dve.tensor_tensor(z[:, :, :], z[:, :, :], mv[:, :, 0:1].to_broadcast([P, UB, D]), ALU.subtract))
                dve.wait_ge(rooted, m + 1)
                then(dve.reciprocal(rstd[:, :], std[:, :]))
                wait(dve, stored[s], use * 48)
                dve.tensor_tensor(x_new[:, s, :, :], z[:, :, :], rstd[:, :].unsqueeze(2).to_broadcast([P, UB, D]), ALU.mult).then_inc(normed, 1)
                if is_within(m, 1):
                    aggregate(m + 1)
                dve.wait_ge(halves, m + 1)
                wait(dve, b_split, m)
                dve.tensor_tensor(b_f[:, :, :], ps_ab[:, 0:UB, HD:], b1_b[:, :].unsqueeze(1).to_broadcast([P, UB, HD]), ALU.add).then_inc(b_read, 1)
                dve.wait_ge(b_read, m + 1)
                b_parts = cols(tables, m * (UB * 3 * HD), UB * 3 * HD).rearrange("p (a k b) -> p a k b", k=3, b=HD)
                split_bf16(dve, in_chain(split_chain, m, 3), b_f[:, :, :], b_rest[:, :, :], [b_parts[:, :, i, :] for i in range(3)], b_split)
            over_steps(dve, body)

        @block.scalar
        def _(act):
            def copy(m):
                act.wait_ge(turned, m + 1)
                wait(act, projected, m)
                act.activation(aggT[:, :], ps_T[0:D, 0:UB * P], ACT.Copy).then_inc(copied, 1)

            copy(0)

            def body(m, s, use):
                act.wait_ge(varied, m + 1)
                act.activation(std[:, :], mv[:, :, 1], ACT.Sqrt, bias=eps[:, 0:1]).then_inc(rooted, 1)
                act.wait_ge(x_turned, m + 1)
                wait(act, stored[s], use * 48)
                act.activation(xT[:, s, :], ps_T[0:D, 0:UB * P], ACT.Copy).then_inc(x_copied, 1)
                act.wait_ge(b_read, m + 1)
                act.activation(a_out[:, s, :, :], ps_ab[:, 0:UB, 0:HD], ACT.Copy).then_inc(a_copied, 1)
                if is_within(m, 1):
                    copy(m + 1)
            over_steps(act, body)

        @block.tensor
        def _(pe):
            def project(m):
                wait(pe, x_copied, m)
                wait_alone(pe, made, m + 1, passed)
                for j in range(UB):
                    last = pe.transpose(ps_T[0:D, j * P:(j + 1) * P], agg[:, j, :], ident[:, :])
                last.then_inc(turned, 1)
                pe.wait_ge(copied, m + 1)
                for j in range(UB):
                    last = pe.matmul(ps_z[:, j, :], aggT[:, j * P:(j + 1) * P], W_T[:, :], start=True, stop=True)
                last.then_inc(projected, 1)

            project(0)

            def body(m, s, use):
                wait_alone(pe, normed, m + 1, passed)
                for j in range(UB):
                    last = pe.transpose(ps_T[0:D, j * P:(j + 1) * P], x_new[:, s, j, :], ident[:, :])
                last.then_inc(x_turned, 1)
                wait(pe, a_copied, m)
                pe.wait_ge(x_copied, m + 1)
                for j in range(UB):
                    last = pe.matmul(ps_ab[:, j, :], xT[:, s, j * P:(j + 1) * P], W1_T[:, :], start=True, stop=True)
                last.then_inc(halves, 1)
                if is_within(m, 1):
                    project(m + 1)
            over_steps(pe, body)

        @block.sync
        def _(sp):
            def body(m, s, use):
                nodes_of = bass.ds(m * (UB * P), UB * P)
                sp.wait_ge(normed, m + 1)
                sp.dma_start(x1_dram[nodes_of, :].rearrange("(a p) c -> p a c", p=P), x_new[:, s, :, :]).then_inc(stored[s], 16)
                wait_alone(sp, x_copied, m + 1, passed)
                sp.dma_start(x1T_dram[:, nodes_of], xT[:, s, :]).then_inc(stored[s], 16)
                wait_alone(sp, a_copied, m + 1, passed)
                sp.dma_start(a_dram[nodes_of, :].rearrange("(a p) c -> p a c", p=P), a_out[:, s, :, :]).then_inc(stored[s], 16)
            over_steps(sp, body)
            sp.wait_ge(stored[0], 48 * ((NU + 1) // 2))
            sp.wait_ge(stored[1], 48 * (NU // 2))


def messages(nc, dst, attr9, lane_row, node_id, window_base, ones_bf, src_flat, src_hi, src_lo, src_f, dst_f, c_parts, step_tab, tables, sums, a_dram):
    with ExitStack() as ctx:
        def sb(name, shape, dt):
            return ctx.enter_context(nc.sbuf_tensor(name, shape, dt))

        def sem(name):
            return ctx.enter_context(nc.semaphore(name))

        dst_rows = sb("m_dst_rows", [P, 2, GE], I32)
        attr_rows = sb("attr_rows", [9, 2, GE], BF16)
        dst_hot = sb("m_dst_hot", [P, 3, GE], BF16)
        node_hot = sb("node_hot", [P, 3, G, P], F32)
        src_i = sb("src_i", [P, S, G], I32)
        a_rows = sb("a_rows", [P, S, G, HD], F32)
        hidden = src_flat[:, 0:4 * G * (HD + 1)].bitcast(F32).rearrange("p (a b c) -> p a b c", a=2, b=G)
        ps_pre = ctx.enter_context(nc.psum_tensor("ps_pre", [P, 2, 1024], F32))
        ps_sum = ctx.enter_context(nc.psum_tensor("ps_msum", [P, 3, 512], F32))
        ps_mark = ctx.enter_context(nc.psum_tensor("ps_mark", [P, 512], F32))
        rows_in = [sem(f"edge_rows_in{s}") for s in range(S)]
        a_in = [sem(f"a_rows_in{s}") for s in range(S)]
        cleared, indexed, index_f = sem("m_cleared"), sem("indexed"), sem("index_f")
        hot_made, gathered = sem("m_dst_hot_made"), sem("m_gathered")
        extra_made, extra_done = sem("m_extra_hot_made"), sem("m_extra_gathered")
        extra_node_made, extra_summed = sem("extra_node_hot_made"), sem("extra_summed")
        added, relued = sem("pre_added"), sem("relued")
        node_hot_made, summed, kept = sem("node_hot_made"), sem("window_summed"), sem("window_kept")
        extra_kept = sem("extra_kept")
        passed = sem("messages_passed")
        block = ctx.enter_context(nc.Block())

        @block.sync
        def _(sp):
            def body(g, s, use, _):
                wait(sp, gathered, g - 1)
                h = s % 2
                sp.dma_start(dst_rows[:, h, :], dst[bass.ds(g * GE, GE)].unsqueeze(0).to_broadcast([P, GE])).then_inc(rows_in[s], 16)
                sp.dma_start(attr_rows[:, h, :], attr9[:, bass.ds(g * GE, GE)]).then_inc(rows_in[s], 16)
            over_groups(sp, NG, body)

        @block.gpsimd
        def _(pool):
            def body(g, s, use, _):
                wait(pool, added, g - (S - 1))
                wait_alone(pool, indexed, g + 1, passed)
                for j in range(G):
                    pool.indirect_dma_start(out=a_rows[:, s, j, :], out_offset=None, in_=a_dram[:, :],
                                            in_offset=bass.IndirectOffsetOnAxis(ap=src_i[:, s, j:j + 1], axis=0)).then_inc(a_in[s], 16)
            over_groups(pool, NG, body)

        @block.vector
        def _(dve):
            regs = [dve.alloc_register(f"msg_dve{i}") for i in range(S + 2)]

            def make_node_hot(g, slot, win, made):
                for j in range(G):
                    last = dve.tensor_scalar(node_hot[:, slot, j, :], lane_row[:, :], cols(window_base, win, 1), cols(dst_f, g * G + j, 1),
                                             ALU.add, ALU.is_equal)
                last.then_inc(made, 1)

            def add_sums(slot, win):
                here = sums[:, bass.ds(win, 1), :].rearrange("p a b -> p (a b)")
                return dve.tensor_tensor(here, here, ps_sum[:, slot, 0:HD + 1], ALU.add)

            def add_pre(g, s, use):
                dve.wait_ge(a_in[s], use * (16 * G) + 16 * G)
                dve.wait_ge(gathered, g + 1)
                wait(dve, summed, g - 1)
                dve.tensor_tensor(hidden[:, s % 2, :, 0:HD], fold(ps_pre[:, s % 2, 0:G * HD], G), a_rows[:, s, :, :],
                                  ALU.add).then_inc(added, 1)

            def sum_extras(g, windows):
                def extra(x, win):
                    make_node_hot(g, 2, win, extra_node_made)
                    dve.wait_ge(extra_summed, x + 1)
                    dve.wait_ge(kept, g + 1)
                    add_sums(2, win).then_inc(extra_kept, 1)
                    dve.wait_ge(extra_kept, x + 1)
                extra_windows(dve, windows, extra)

            def keep_first(f, slot, windows):
                dve.wait_ge(summed, f + 1)
                dve.wait_ge(kept, f + 1)
                add_sums(slot, windows[2]).then_inc(kept, 1)

            dve.scalar_tensor_tensor(src_f, src_hi, float(P), src_lo, ALU.mult, ALU.add).then_inc(index_f, 1)
            dve.memset(sums[:, :, :], 0.0).then_inc(kept, 1)
            dve.wait_ge(index_f, 1)
            dve.memset(hidden[:, :, :, HD], 1.0).then_inc(cleared, 1)

            def body(g, s, use, windows):
                h = s % 2
                if not is_first(g):
                    add_pre(*last_of(g, s, use))
                dve.wait_ge(rows_in[s], use * 32 + 32)
                wait(dve, gathered, g - 1)
                dve.tensor_scalar(dst_hot[:, h, :], dst_rows[:, h, :], cols(node_id, windows[s + 2][2], 1), None,
                                  ALU.is_equal).then_inc(hot_made, 1)

                def extra(x, win):
                    dve.wait_ge(extra_done, x + 1)
                    dve.tensor_scalar(dst_hot[:, 2, :], dst_rows[:, h, :], cols(node_id, win, 1), None,
                                      ALU.is_equal).then_inc(extra_made, 1)
                extra_windows(dve, windows[s + 2], extra)
                if not is_first(g):
                    make_node_hot(g - 1, 1 - h, windows[s + 1][2], node_hot_made)
                    if not (isinstance(g, int) and g < 2):
                        keep_first(g - 2, h, windows[s])
                    sum_extras(g - 1, windows[s + 1])
            over_groups(dve, NG, body, lambda g0, n: load_windows(dve, step_tab, regs, g0, n))
            h, windows = (NG - 1) % 2, load_windows(dve, step_tab, regs, NG - 1, 1)
            add_pre(NG - 1, (NG - 1) % S, (NG - 1) // S)
            make_node_hot(NG - 1, h, windows[2][2], node_hot_made)
            keep_first(NG - 2, 1 - h, windows[1])
            sum_extras(NG - 1, windows[2])
            keep_first(NG - 1, h, windows[2])

        @block.scalar
        def _(act):
            def index(g, s, use):
                wait(act, a_in[s], use * (16 * G))
                act.activation(src_i[:, s, :], cols(src_f, g * G, G), ACT.Copy).then_inc(indexed, 1)

            act.wait_ge(index_f, 1)
            index(0, 0, 0)

            def body(g, s, use, _):
                if not isinstance(g, int) or g + 1 < NG:
                    index(g + 1, (s + 1) % S, use if s + 1 < S else use + 1)
                act.wait_ge(added, g + 1)
                act.activation(hidden[:, s % 2, :, 0:HD], hidden[:, s % 2, :, 0:HD], ACT.Relu).then_inc(relued, 1)
            over_groups(act, NG, body)

        @block.tensor
        def _(pe):
            regs = [pe.alloc_register(f"msg_pe{i}") for i in range(S + 2)]

            def sum_windows(g, h, windows):
                def products(slot):
                    for j in range(G):
                        last = pe.matmul(ps_sum[:, slot, 0:HD + 1], node_hot[:, slot, j, :], hidden[:, h, j, :], start=(j == 0), stop=(j == G - 1))
                    return last

                pe.wait_ge(relued, g + 1)
                pe.wait_ge(node_hot_made, g + 1)
                products(h).then_inc(summed, 1)

                def extra(x, win):
                    pe.wait_ge(extra_node_made, x + 1)
                    products(2).then_inc(extra_summed, 1)
                extra_windows(pe, windows, extra)

            pe.sem_inc(extra_done, 1)
            pe.wait_ge(cleared, 1)

            def body(g, s, use, windows):
                h = s % 2
                wait(pe, added, g - 1)
                pe.wait_ge(rows_in[s], use * 32 + 32)
                for j in range(G):
                    pe.matmul(ps_pre[:, h, j * HD:(j + 1) * HD], attr_rows[:, h, j * P:(j + 1) * P], c_parts[:, :],
                              start=j in (0, 4), stop=False, skip_group_check=True)

                def gather(slot, win):
                    for j in range(G):
                        for i in range(3):
                            last = pe.matmul(ps_pre[:, h, j * HD:(j + 1) * HD], dst_hot[:, slot, j * P:(j + 1) * P],
                                             cols(tables, win * (3 * HD) + i * HD, HD), start=False, stop=False, skip_group_check=True)
                    return last

                pe.wait_ge(hot_made, g + 1)
                gather(h, windows[s + 2][2])

                def extra(x, win):
                    pe.wait_ge(extra_made, x + 1)
                    gather(2, win).then_inc(extra_done, 1)
                extra_windows(pe, windows[s + 2], extra)
                pe.matmul(ps_mark[:, 0:1], ones_bf[:, :], ones_bf[:, 0:1], start=True, stop=True).then_inc(gathered, 1)
                if not is_first(g):
                    sum_windows(g - 1, 1 - h, windows[s + 1])
            over_groups(pe, NG, body, lambda g0, n: load_windows(pe, step_tab, regs, g0, n))
            sum_windows(NG - 1, (NG - 1) % 2, load_windows(pe, step_tab, regs, NG - 1, 1)[2])


def edge_counts(nc, ident, sums, edges_dram):
    with ExitStack() as ctx:
        by_lane = ctx.enter_context(nc.sbuf_tensor("edges_by_lane", [P, NW], F32))
        by_window = ctx.enter_context(nc.sbuf_tensor("edges_by_window", [NW, P], F32))
        ps = ctx.enter_context(nc.psum_tensor("ps_by_window", [P, 512], F32))
        staged, turned, copied, kept = (ctx.enter_context(nc.semaphore(n)) for n in ("e_staged", "e_turned", "e_copied", "e_kept"))
        block = ctx.enter_context(nc.Block())

        @block.vector
        def _(dve):
            dve.tensor_copy(by_lane[:, :], sums[:, :, HD]).then_inc(staged, 1)
            dve.wait_ge(turned, 1)
            dve.tensor_copy(by_window[:, :], ps[0:NW, 0:P]).then_inc(copied, 1)

        @block.tensor
        def _(pe):
            pe.wait_ge(staged, 1)
            pe.transpose(ps[0:NW, 0:P], by_lane[:, :], ident[:, :]).then_inc(turned, 1)

        @block.sync
        def _(sp):
            sp.wait_ge(copied, 1)
            sp.dma_start(edges_dram.rearrange("(a p) -> a p", p=P), by_window[:, :]).then_inc(kept, 16)
            sp.wait_ge(kept, 16)


def update(nc, ident, eps, x1_dram, x1T_dram, sums, tables, src_flat, edges_dram, W2_T, b2_row, Wih_x, Whh_x, out):
    HALF = UB * P // 2
    with ExitStack() as ctx:
        def sb(name, shape, dt=F32):
            return ctx.enter_context(nc.sbuf_tensor(name, shape, dt))

        def sem(name):
            return ctx.enter_context(nc.semaphore(name))

        spare, taken = tables[:, :].bitcast(F32), 0

        def two_slots(width):
            nonlocal taken
            taken += 2 * UB * width
            return spare[:, taken - 2 * UB * width:taken].rearrange("p (a b c) -> p a b c", a=2, b=UB)

        hx, rz, x_rows, nn, xn, res = (two_slots(width) for width in (HD, 2 * D, D, D, D, D))
        hT = sb("hT", [P, UB * P])
        xT = sb("u_xT", [D + 1, 2, UB * P])
        edges_row = sb("edges_row", [1, 2, UB * P])
        agT = sb("agT", [D + 1, UB * P])
        t1, t2, d1, d2, z, centred = (src_flat[:, 2 * i * UB * D:2 * (i + 1) * UB * D].bitcast(F32).rearrange("p (a b) -> p a b", a=UB)
                                      for i in range(6))
        stats, mv = sb("u_stats", [P, UB, 6]), sb("u_mv", [P, UB, 2])
        rstd, var, power = sb("u_rstd", [P, UB]), sb("u_var", [P, UB]), sb("power", [P, UB])
        ps_hT = ctx.enter_context(nc.psum_tensor("ps_hT", [P, 1024], F32))
        ps_ag = ctx.enter_context(nc.psum_tensor("ps_ag", [P, 2, 512], F32))
        ps_gates = ctx.enter_context(nc.psum_tensor("ps_gates", [P, 8, 4 * D], F32))
        chain, staged, turned, copied = sem("u_chain"), sem("u_staged"), sem("u_turned"), sem("u_copied")
        second, ag_copied, gates = sem("second_layer"), sem("ag_copied"), sem("gates_made")
        rz_done, n_ready, n_done, xn_made = sem("rz_done"), sem("n_ready"), sem("n_done"), sem("xn_made")
        blended, varied, eps_added, rooted = sem("blended"), sem("u_varied"), sem("eps_added"), sem("u_rooted")
        ones_set, x_in = sem("ones_set"), [sem("u_x_in0"), sem("u_x_in1")]
        edges_in = [sem("edges_in0"), sem("edges_in1")]
        ready, stored = sem("result_ready"), [sem("stored0"), sem("stored1")]
        passed = sem("update_passed")
        block = ctx.enter_context(nc.Block())

        @block.gpsimd
        def _(pool):
            def stage(m, s):
                wait(pool, turned, m - 1)
                pool.tensor_copy(hx[:, s, :, :], sums[:, bass.ds(m * UB, UB), 0:HD]).then_inc(staged, 1)

            stage(0, 0)
            stage(1, 1)
            pool.memset(power[:, :], -0.5)

            def body(m, s, use):
                pool.wait_ge(n_done, m + 1)
                pool.tensor_tensor(xn[:, s, :, :], x_rows[:, s, :, :], nn[:, s, :, :], ALU.add).then_inc(xn_made, 1)
                if is_within(m, 2):
                    stage(m + 2, s)
                pool.wait_ge(varied, m + 1)
                pool.tensor_tensor(var[:, :], mv[:, :, 1], eps[:, 0:1].to_broadcast([P, UB]), ALU.add).then_inc(eps_added, 1)
                pool.wait_ge(eps_added, m + 1)
                pool.tensor_tensor(rstd[:, :], var[:, :], power[:, :], ALU.pow).then_inc(rooted, 1)
            over_steps(pool, body)

        @block.tensor
        def _(pe):
            def turn(m, s):
                wait(pe, copied, m)
                wait_alone(pe, staged, m + 1, passed)
                for j in range(UB):
                    last = pe.transpose(ps_hT[:, j * P:(j + 1) * P], hx[:, s, j, :], ident[:, :])
                last.then_inc(turned, 1)

            def second_layer(m, s, use):
                pe.wait_ge(edges_in[s], use * 16 + 16)
                pe.wait_ge(copied, m + 1)
                wait(pe, ag_copied, m)
                for i in range(2):
                    pe.matmul(ps_ag[0:D, i, 0:HALF], W2_T[:, :], hT[:, i * HALF:(i + 1) * HALF], start=True, stop=False)
                    last = pe.matmul(ps_ag[0:D, i, 0:HALF], b2_row[:, :], edges_row[:, s, i * HALF:(i + 1) * HALF],
                                     start=False, stop=True)
                last.then_inc(second, 1)

            turn(0, 0)
            second_layer(0, 0, 0)

            def body(m, s, use):
                if is_within(m, 1):
                    turn(m + 1, 1 - s)
                pe.wait_ge(x_in[s], use * 32 + 32)
                wait(pe, n_ready, m)
                for j in range(UB):
                    pe.matmul(ps_gates[:, j, :], xT[:, s, j * P:(j + 1) * P], Whh_x[:, :], start=j % 2 == 0, stop=False, skip_group_check=True)
                pe.wait_ge(ag_copied, m + 1)
                for j in range(UB):
                    last = pe.matmul(ps_gates[:, j, :], agT[:, j * P:(j + 1) * P], Wih_x[:, :], start=False, stop=True, skip_group_check=True)
                last.then_inc(gates, 1)
                if is_within(m, 1):
                    second_layer(m + 1, 1 - s, use + s)
            pe.wait_ge(ones_set, 1)
            over_steps(pe, body)

        @block.scalar
        def _(act):
            def copy(m):
                act.wait_ge(turned, m + 1)
                wait(act, second, m)
                act.activation(hT[:, :], ps_hT[:, 0:UB * P], ACT.Copy).then_inc(copied, 1)

            copy(0)

            def body(m, s, use):
                if is_within(m, 1):
                    copy(m + 1)
                act.wait_ge(gates, m + 1)
                wait(act, blended, m - 1)
                act.activation(rz[:, s, :, :], ps_gates[:, 0:UB, 0:2 * D], ACT.Sigmoid).then_inc(rz_done, 1)
                act.wait_ge(n_ready, m + 1)
                act.activation(nn[:, s, :, :], t2[:, :, :], ACT.Tanh).then_inc(n_done, 1)
            over_steps(act, body)

        @block.vector
        def _(dve):
            dve.memset(xT[D:D + 1, :, :], 1.0)
            dve.memset(agT[D:D + 1, :], 1.0).then_inc(ones_set, 1)

            def copy(m):
                dve.wait_ge(second, m + 1)
                wait(dve, gates, m)
                dve.tensor_copy(fold(agT[0:D, :], 2), ps_ag[0:D, :, 0:HALF]).then_inc(ag_copied, 1)

            copy(0)

            def body(m, s, use):
                n, steps = 0, 5

                def then(instruction):
                    nonlocal n
                    n += 1
                    instruction.then_inc(chain, 1)
                    wait_alone(dve, chain, m * steps + n, passed)

                dve.wait_ge(rz_done, m + 1)
                then(dve.tensor_tensor(t1[:, :, :], rz[:, s, :, 0:D], ps_gates[:, 0:UB, 2 * D:3 * D], ALU.mult))
                wait(dve, n_done, m)
                dve.tensor_tensor(t2[:, :, :], t1[:, :, :], ps_gates[:, 0:UB, 3 * D:4 * D], ALU.add).then_inc(n_ready, 1)
                if is_within(m, 1):
                    copy(m + 1)
                dve.wait_ge(x_in[s], use * 32 + 32)
                dve.wait_ge(n_done, m + 1)
                then(dve.tensor_tensor(d1[:, :, :], x_rows[:, s, :, :], nn[:, s, :, :], ALU.subtract))
                then(dve.tensor_tensor(d2[:, :, :], rz[:, s, :, D:], d1[:, :, :], ALU.mult))
                dve.wait_ge(xn_made, m + 1)
                dve.tensor_tensor(z[:, :, :], xn[:, s, :, :], d2[:, :, :], ALU.add).then_inc(blended, 1)
                dve.wait_ge(blended, m + 1)
                for j in range(UB):
                    last = dve.bn_stats(stats[:, j, :], z[:, j, :])
                then(last)
                for j in range(UB):
                    last = dve.bn_aggr(mv[:, j, :], stats[:, j, :])
                last.then_inc(varied, 1)
                dve.wait_ge(varied, m + 1)
                then(dve.tensor_tensor(centred[:, :, :], z[:, :, :], mv[:, :, 0:1].to_broadcast([P, UB, D]), ALU.subtract))
                dve.wait_ge(rooted, m + 1)
                wait(dve, stored[s], use * 32)
                dve.tensor_tensor(res[:, s, :, :], centred[:, :, :], rstd[:, :].unsqueeze(2).to_broadcast([P, UB, D]), ALU.mult).then_inc(ready, 1)
                assert n == steps, n
            over_steps(dve, body)

        @block.sync
        def _(sp):
            def load(m, s):
                wait(sp, varied, m - 1)
                first = m * (UB * P)
                sp.dma_start(edges_row[:, s, :], edges_dram[bass.ds(first, UB * P)].unsqueeze(0)).then_inc(edges_in[s], 16)
                sp.dma_start(x_rows[:, s, :, :], x1_dram[bass.ds(first, UB * P), :].rearrange("(a p) c -> p a c", p=P)).then_inc(x_in[s], 16)
                sp.dma_start(xT[0:D, s, :], x1T_dram[:, bass.ds(first, UB * P)]).then_inc(x_in[s], 16)

            load(0, 0)

            def body(m, s, use):
                if is_within(m, 1):
                    load(m + 1, 1 - s)
                sp.wait_ge(ready, m + 1)
                full, rows = UB - 1, P if is_within(m, 1) else LAST
                first = m * (UB * P)
                sp.dma_start(out[bass.ds(first, full * P), :].rearrange("(a p) c -> p a c", p=P), res[:, s, 0:full, :]).then_inc(stored[s], 16)
                sp.dma_start(out[bass.ds(first + full * P, rows), :], res[0:rows, s, full, :]).then_inc(stored[s], 16)
            over_steps(sp, body)
            sp.wait_ge(stored[0], 32 * ((NU + 1) // 2))
            sp.wait_ge(stored[1], 32 * (NU // 2))


INS = ["x", "src", "dst", "edge_weight", "edge_weight1", "L0_gnn_W", "L0_gnn_b", "L1_gnn_W1", "L1_gnn_b1", "L1_gnn_W2",
       "L1_gnn_b2", "L1_gnn_W_ih", "L1_gnn_b_ih", "L1_gnn_W_hh", "L1_gnn_b_hh"]


def kernel(**inputs):
    import numpy as np
    import concourse.bacc as bacc
    from concourse.bass_utils import run_bass_kernel_spmd

    nc = bacc.Bacc("TRN2", target_bir_lowering=False, num_devices=1)
    arrays, args = {}, []
    for name in INS:
        a = np.ascontiguousarray(inputs[name])
        arrays[f"in_{name}"] = a
        args.append(nc.dram_tensor(f"in_{name}", a.shape, mybir.dt.from_np(a.dtype), kind="ExternalInput").ap())
    attr9 = nc.dram_tensor("attr_parts", (9, E), BF16, kind="Internal").ap()
    c_dram = nc.dram_tensor("c_parts_dram", (3, HD), BF16, kind="Internal").ap()
    x1_dram = nc.dram_tensor("x_after_layer0", (NW * P, D), F32, kind="Internal").ap()
    result = nc.dram_tensor("result", (N, D), F32, kind="ExternalOutput").ap()
    q_windows = nc.dram_tensor("q_windows", (P * QP,), I32, kind="Internal").ap()
    steps = nc.dram_tensor("steps", (NG,), I32, kind="Internal").ap()
    moved = nc.dram_tensor("moved", (NQ * GE, ROW), F32, kind="Internal").ap()
    a_dram = nc.dram_tensor("a_half", (NW * P, HD), F32, kind="Internal").ap()
    x1T_dram = nc.dram_tensor("x_after_layer0_T", (D, NW * P), F32, kind="Internal").ap()
    edges_dram = nc.dram_tensor("edges_into_nodes", (NW * P,), F32, kind="Internal").ap()
    program(nc, *args, result, q_windows, steps, moved, a_dram, x1_dram, x1T_dram, attr9, c_dram, edges_dram)
    r = run_bass_kernel_spmd(nc, [arrays], core_ids=[0])
    return r.results[0]["result"]
```
